# Optimizing a Trainium2 kernel written in Bass

```python
import numpy as np
import jax
import jax.numpy as jnp

def _softmax(x, axis=-1):
    return jax.nn.softmax(x, axis=axis)

def _gelu(x):
    return jax.nn.gelu(x, approximate=True)

def _silu(x):
    return jax.nn.silu(x)

def _sigmoid(x):
    return jax.nn.sigmoid(x)

def _layernorm(x, axis=-1, eps=1e-05):
    m = jnp.mean(x, axis=axis, keepdims=True)
    v = jnp.var(x, axis=axis, keepdims=True)
    return (x - m) / jnp.sqrt(v + eps)

def _scatter_add(tgt, idx, src, axis=0):
    return tgt.at[idx].add(src)

def _segment_sum(src, seg, n):
    return jax.ops.segment_sum(src, seg, n)
kernel_name = 'mk_sandwich_d2_jaxref_r8_9a14f2'

def setup_inputs(seed: int=0):
    np.random.seed(seed)
    _w = jnp.asarray

    def _L0_attn_setup():
        import jax, jax.numpy as jnp
        import numpy as np
        EMB = 128
        HEADS = 16
        BLOCK = 128
        key = jax.random.key(seed)
        k1, k2, k3 = jax.random.split(key, 3)
        B, T, C = (4, 512, EMB)
        x = jax.random.normal(k1, (B, T, C), dtype=jnp.float32)
        W_qkv = jax.random.normal(k2, (C, 3 * C), dtype=jnp.float32) * 0.02
        W_proj = jax.random.normal(k3, (C, C), dtype=jnp.float32) * 0.02
        b_proj = jnp.zeros((C,), dtype=jnp.float32)
        return {'x': x, 'W_qkv': W_qkv, 'W_proj': W_proj, 'b_proj': b_proj}
    _L0_attn_in = _L0_attn_setup()

    def _L0_ffn_setup():
        import jax, jax.numpy as jnp
        import numpy as np
        TOP_K = 2
        NUM_EXPERTS = 8
        key = jax.random.key(seed)
        ks = jax.random.split(key, 8)
        h, d, ds, E = (128, 64, 128, NUM_EXPERTS)
        s = 1.0 / np.sqrt(h)
        return {'x': jax.random.normal(ks[0], (2, 256, h), jnp.float32), 'router': jax.random.normal(ks[1], (h, E), jnp.float32) * s, 'experts_gate': jax.random.normal(ks[2], (E, h, d), jnp.float32) * s, 'experts_up': jax.random.normal(ks[3], (E, h, d), jnp.float32) * s, 'experts_down': jax.random.normal(ks[4], (E, d, h), jnp.float32) * (1.0 / np.sqrt(d)), 'shared_gate': jax.random.normal(ks[5], (h, ds), jnp.float32) * s, 'shared_up': jax.random.normal(ks[6], (h, ds), jnp.float32) * s, 'shared_down': jax.random.normal(ks[7], (ds, h), jnp.float32) * (1.0 / np.sqrt(ds))}
    _L0_ffn_in = _L0_ffn_setup()

    def _L1_attn_setup():
        import jax, jax.numpy as jnp
        import numpy as np
        import math
        B, T, C, FFN = (8, 256, 128, 512)
        LAYER_ID, N_LAYER = (1, 12)

        def layer_norm(x, g, b, eps=1e-05):
            m = jnp.mean(x, axis=-1, keepdims=True)
            v = jnp.mean(jnp.square(x - m), axis=-1, keepdims=True)
            return (x - m) * jax.lax.rsqrt(v + eps) * g + b

        def token_shift(x):
            return jnp.concatenate([jnp.zeros_like(x[:, :1]), x[:, :-1]], axis=1)

        def wkv(w, u, k, v):
            w = -jnp.exp(w)
            kT = jnp.swapaxes(k, 0, 1)
            vT = jnp.swapaxes(v, 0, 1)

            def step(carry, kv_t):
                aa, bb, pp = carry
                kt, vt = kv_t
                ww = u + kt
                p = jnp.maximum(pp, ww)
                e1 = jnp.exp(pp - p)
                e2 = jnp.exp(ww - p)
                y = (e1 * aa + e2 * vt) / (e1 * bb + e2)
                ww2 = pp + w
                p2 = jnp.maximum(ww2, kt)
                e1b = jnp.exp(ww2 - p2)
                e2b = jnp.exp(kt - p2)
                return ((e1b * aa + e2b * vt, e1b * bb + e2b, p2), y)
            z = jnp.zeros((k.shape[0], k.shape[2]), k.dtype)
            init = (z, z, jnp.full_like(z, -1e+38))
            _, yT = jax.lax.scan(step, init, (kT, vT))
            return jnp.swapaxes(yT, 0, 1)
        key = jax.random.key(seed)
        ks = jax.random.split(key, 8)
        x = jax.random.normal(ks[0], (B, T, C), jnp.float32)
        r0 = LAYER_ID / (N_LAYER - 1)
        r1 = 1.0 - LAYER_ID / N_LAYER
        ddd = (jnp.arange(C, dtype=jnp.float32) / C).reshape(1, 1, C)
        att_mix_k = jnp.power(ddd, r1)
        att_mix_v = jnp.power(ddd, r1) + 0.3 * r0
        att_mix_r = jnp.power(ddd, 0.5 * r1)
        h = jnp.arange(C, dtype=jnp.float32)
        time_decay = -5.0 + 8.0 * jnp.power(h / (C - 1), 0.7 + 1.3 * r0)
        zigzag = ((jnp.arange(C) + 1) % 3 - 1).astype(jnp.float32) * 0.5
        time_first = jnp.full((C,), math.log(0.3), jnp.float32) + zigzag
        ffn_mix_k = jnp.power(ddd, r1)
        ffn_mix_r = jnp.power(ddd, r1)
        s = 0.02
        return {'x': x, 'ln1_g': jnp.ones((C,), jnp.float32), 'ln1_b': jnp.zeros((C,), jnp.float32), 'ln2_g': jnp.ones((C,), jnp.float32), 'ln2_b': jnp.zeros((C,), jnp.float32), 'att_mix_k': att_mix_k, 'att_mix_v': att_mix_v, 'att_mix_r': att_mix_r, 'time_decay': time_decay, 'time_first': time_first, 'Wk': s * jax.random.normal(ks[1], (C, C), jnp.float32), 'Wv': s * jax.random.normal(ks[2], (C, C), jnp.float32), 'Wr': s * jax.random.normal(ks[3], (C, C), jnp.float32), 'Wo': s * jax.random.normal(ks[4], (C, C), jnp.float32), 'ffn_mix_k': ffn_mix_k, 'ffn_mix_r': ffn_mix_r, 'Wk_ffn': s * jax.random.normal(ks[5], (FFN, C), jnp.float32), 'Wr_ffn': s * jax.random.normal(ks[6], (C, C), jnp.float32), 'Wv_ffn': s * jax.random.normal(ks[7], (C, FFN), jnp.float32)}
    _L1_attn_in = _L1_attn_setup()

    def _L1_ffn_setup():
        import jax, jax.numpy as jnp
        import numpy as np
        B, L, D = (2, 256, 128)
        E = 15
        H = D * 1
        K = 3
        T = 1.0
        key = jax.random.key(seed)
        ks = jax.random.split(key, 12)
        s = 0.02
        return {'x': jax.random.normal(ks[0], (B, L, D), dtype=jnp.float32), 'router_W': jax.random.normal(ks[1], (D, E), dtype=jnp.float32) * s, 'router_b': jnp.zeros((E,), dtype=jnp.float32), 'sW1': jax.random.normal(ks[2], (D, H), dtype=jnp.float32) * s, 'sb1': jnp.zeros((H,), dtype=jnp.float32), 'sW2': jax.random.normal(ks[3], (H, D), dtype=jnp.float32) * s, 'sb2': jnp.zeros((D,), dtype=jnp.float32), 'eW1': jax.random.normal(ks[4], (E, D, H), dtype=jnp.float32) * s, 'eb1': jnp.zeros((E, H), dtype=jnp.float32), 'eW2': jax.random.normal(ks[5], (E, H, D), dtype=jnp.float32) * s, 'eb2': jnp.zeros((E, D), dtype=jnp.float32)}
    _L1_ffn_in = _L1_ffn_setup()
    _d = {'L0_attn_x': _L0_attn_in['x'], 'L0_attn_W_qkv': _L0_attn_in['W_qkv'], 'L0_attn_W_proj': _L0_attn_in['W_proj'], 'L0_attn_b_proj': _L0_attn_in['b_proj'], 'L0_ffn_router': _L0_ffn_in['router'], 'L0_ffn_experts_gate': _L0_ffn_in['experts_gate'], 'L0_ffn_experts_up': _L0_ffn_in['experts_up'], 'L0_ffn_experts_down': _L0_ffn_in['experts_down'], 'L0_ffn_shared_gate': _L0_ffn_in['shared_gate'], 'L0_ffn_shared_up': _L0_ffn_in['shared_up'], 'L0_ffn_shared_down': _L0_ffn_in['shared_down'], 'L1_attn_ln1_g': _L1_attn_in['ln1_g'], 'L1_attn_ln1_b': _L1_attn_in['ln1_b'], 'L1_attn_ln2_g': _L1_attn_in['ln2_g'], 'L1_attn_ln2_b': _L1_attn_in['ln2_b'], 'L1_attn_att_mix_k': _L1_attn_in['att_mix_k'], 'L1_attn_att_mix_v': _L1_attn_in['att_mix_v'], 'L1_attn_att_mix_r': _L1_attn_in['att_mix_r'], 'L1_attn_time_decay': _L1_attn_in['time_decay'], 'L1_attn_time_first': _L1_attn_in['time_first'], 'L1_attn_Wk': _L1_attn_in['Wk'], 'L1_attn_Wv': _L1_attn_in['Wv'], 'L1_attn_Wr': _L1_attn_in['Wr'], 'L1_attn_Wo': _L1_attn_in['Wo'], 'L1_attn_ffn_mix_k': _L1_attn_in['ffn_mix_k'], 'L1_attn_ffn_mix_r': _L1_attn_in['ffn_mix_r'], 'L1_attn_Wk_ffn': _L1_attn_in['Wk_ffn'], 'L1_attn_Wr_ffn': _L1_attn_in['Wr_ffn'], 'L1_attn_Wv_ffn': _L1_attn_in['Wv_ffn'], 'L1_ffn_router_W': _L1_ffn_in['router_W'], 'L1_ffn_router_b': _L1_ffn_in['router_b'], 'L1_ffn_sW1': _L1_ffn_in['sW1'], 'L1_ffn_sb1': _L1_ffn_in['sb1'], 'L1_ffn_sW2': _L1_ffn_in['sW2'], 'L1_ffn_sb2': _L1_ffn_in['sb2'], 'L1_ffn_eW1': _L1_ffn_in['eW1'], 'L1_ffn_eb1': _L1_ffn_in['eb1'], 'L1_ffn_eW2': _L1_ffn_in['eW2'], 'L1_ffn_eb2': _L1_ffn_in['eb2']}
    _x0 = _d['L0_attn_x']
    _d['L0_attn_x'] = jax.random.normal(jax.random.fold_in(jax.random.key(seed), 1), (8, 512, 128), dtype=_x0.dtype)
    del _x0
    return _d

def reference(L0_attn_x, L0_attn_W_qkv, L0_attn_W_proj, L0_attn_b_proj, L0_ffn_router, L0_ffn_experts_gate, L0_ffn_experts_up, L0_ffn_experts_down, L0_ffn_shared_gate, L0_ffn_shared_up, L0_ffn_shared_down, L1_attn_ln1_g, L1_attn_ln1_b, L1_attn_ln2_g, L1_attn_ln2_b, L1_attn_att_mix_k, L1_attn_att_mix_v, L1_attn_att_mix_r, L1_attn_time_decay, L1_attn_time_first, L1_attn_Wk, L1_attn_Wv, L1_attn_Wr, L1_attn_Wo, L1_attn_ffn_mix_k, L1_attn_ffn_mix_r, L1_attn_Wk_ffn, L1_attn_Wr_ffn, L1_attn_Wv_ffn, L1_ffn_router_W, L1_ffn_router_b, L1_ffn_sW1, L1_ffn_sb1, L1_ffn_sW2, L1_ffn_sb2, L1_ffn_eW1, L1_ffn_eb1, L1_ffn_eW2, L1_ffn_eb2):

    def _L0_attn_ref(x, W_qkv, W_proj, b_proj):
        import jax, jax.numpy as jnp
        import numpy as np
        EMB = 128
        HEADS = 16
        BLOCK = 128
        B, T, C = x.shape
        H, D, BS = (HEADS, C // HEADS, BLOCK)
        nb = T // BS
        qkv = x @ W_qkv
        q, k, v = jnp.split(qkv, 3, axis=-1)
        q = q.reshape(B, nb, BS, H, D)
        k = k.reshape(B, nb, BS, H, D)
        v = v.reshape(B, nb, BS, H, D)
        scores = jnp.einsum('bnqhd,bnkhd->bnhqk', q, k) / jnp.sqrt(jnp.float32(D))
        tril = jnp.tril(jnp.ones((BS, BS), dtype=bool))
        scores = jnp.where(tril, scores, -jnp.inf)
        scores = scores - jnp.max(scores, axis=-1, keepdims=True)
        e = jnp.exp(scores)
        p = e / (jnp.sum(e, axis=-1, keepdims=True) + 1e-06)
        out = jnp.einsum('bnhqk,bnkhd->bnqhd', p, v).reshape(B, T, C)
        return out @ W_proj + b_proj

    def _L0_ffn_ref(x, router, experts_gate, experts_up, experts_down, shared_gate, shared_up, shared_down):
        import jax, jax.numpy as jnp
        import numpy as np
        TOP_K = 2
        NUM_EXPERTS = 8
        b, s, h = x.shape
        E = router.shape[1]
        shared_act = jax.nn.silu(jnp.einsum('bsh,hd->bsd', x, shared_gate))
        shared_up_out = jnp.einsum('bsh,hd->bsd', x, shared_up)
        shared_out = jnp.einsum('bsd,dh->bsh', shared_act * shared_up_out, shared_down)
        router_probs = jax.nn.softmax(jnp.einsum('bsh,he->bse', x, router), axis=-1)
        topk_probs, topk_idx = jax.lax.top_k(router_probs, TOP_K)
        coef = jnp.sum(jax.nn.one_hot(topk_idx, E, dtype=x.dtype) * topk_probs[..., None], axis=2)
        coef = coef.reshape(b * s, E)
        x_flat = x.reshape(b * s, h)
        gate = jnp.einsum('th,ehd->etd', x_flat, experts_gate)
        up = jnp.einsum('th,ehd->etd', x_flat, experts_up)
        expert_out = jnp.einsum('etd,edh->eth', jax.nn.silu(gate) * up, experts_down)
        routed = jnp.einsum('eth,te->th', expert_out, coef)
        return routed.reshape(b, s, h) + shared_out

    def _L1_attn_ref(x, ln1_g, ln1_b, ln2_g, ln2_b, att_mix_k, att_mix_v, att_mix_r, time_decay, time_first, Wk, Wv, Wr, Wo, ffn_mix_k, ffn_mix_r, Wk_ffn, Wr_ffn, Wv_ffn):
        import jax, jax.numpy as jnp
        import numpy as np
        import math
        B, T, C, FFN = (8, 256, 128, 512)
        LAYER_ID, N_LAYER = (1, 12)

        def layer_norm(x, g, b, eps=1e-05):
            m = jnp.mean(x, axis=-1, keepdims=True)
            v = jnp.mean(jnp.square(x - m), axis=-1, keepdims=True)
            return (x - m) * jax.lax.rsqrt(v + eps) * g + b

        def token_shift(x):
            return jnp.concatenate([jnp.zeros_like(x[:, :1]), x[:, :-1]], axis=1)

        def wkv(w, u, k, v):
            w = -jnp.exp(w)
            kT = jnp.swapaxes(k, 0, 1)
            vT = jnp.swapaxes(v, 0, 1)

            def step(carry, kv_t):
                aa, bb, pp = carry
                kt, vt = kv_t
                ww = u + kt
                p = jnp.maximum(pp, ww)
                e1 = jnp.exp(pp - p)
                e2 = jnp.exp(ww - p)
                y = (e1 * aa + e2 * vt) / (e1 * bb + e2)
                ww2 = pp + w
                p2 = jnp.maximum(ww2, kt)
                e1b = jnp.exp(ww2 - p2)
                e2b = jnp.exp(kt - p2)
                return ((e1b * aa + e2b * vt, e1b * bb + e2b, p2), y)
            z = jnp.zeros((k.shape[0], k.shape[2]), k.dtype)
            init = (z, z, jnp.full_like(z, -1e+38))
            _, yT = jax.lax.scan(step, init, (kT, vT))
            return jnp.swapaxes(yT, 0, 1)
        xn = layer_norm(x, ln1_g, ln1_b)
        xx = token_shift(xn)
        xk = xn * att_mix_k + xx * (1.0 - att_mix_k)
        xv = xn * att_mix_v + xx * (1.0 - att_mix_v)
        xr = xn * att_mix_r + xx * (1.0 - att_mix_r)
        k = jnp.einsum('btc,dc->btd', xk, Wk)
        v = jnp.einsum('btc,dc->btd', xv, Wv)
        sr = jax.nn.sigmoid(jnp.einsum('btc,dc->btd', xr, Wr))
        rwkv = sr * wkv(time_decay, time_first, k, v)
        x = x + jnp.einsum('btd,cd->btc', rwkv, Wo)
        xn2 = layer_norm(x, ln2_g, ln2_b)
        xx2 = token_shift(xn2)
        xk2 = xn2 * ffn_mix_k + xx2 * (1.0 - ffn_mix_k)
        xr2 = xn2 * ffn_mix_r + xx2 * (1.0 - ffn_mix_r)
        kf = jnp.square(jax.nn.relu(jnp.einsum('btc,fc->btf', xk2, Wk_ffn)))
        kv = jnp.einsum('btf,cf->btc', kf, Wv_ffn)
        x = x + jax.nn.sigmoid(jnp.einsum('btc,dc->btd', xr2, Wr_ffn)) * kv
        return x

    def _L1_ffn_ref(x, router_W, router_b, sW1, sb1, sW2, sb2, eW1, eb1, eW2, eb2):
        import jax, jax.numpy as jnp
        import numpy as np
        B, L, D = (2, 256, 128)
        E = 15
        H = D * 1
        K = 3
        T = 1.0
        b, l, d = x.shape
        n = b * l
        xt = x.reshape(n, d)
        shared = jax.nn.relu(xt @ sW1 + sb1) @ sW2 + sb2
        logits = xt @ router_W + router_b
        probs = jax.nn.softmax(logits / T, axis=-1)
        top_p, top_i = jax.lax.top_k(probs, K)
        cw = jnp.zeros((n, E), dtype=probs.dtype)
        cw = cw.at[jnp.arange(n)[:, None], top_i].set(top_p)
        h = jax.nn.relu(jnp.einsum('nd,edh->neh', xt, eW1) + eb1)
        ye = jnp.einsum('neh,ehd->ned', h, eW2) + eb2
        routed = jnp.einsum('ned,ne->nd', ye, cw)
        return (shared + routed).reshape(b, l, d)
    x = L0_attn_x
    x = x + _layernorm(_L0_attn_ref(_layernorm(x, axis=-1), L0_attn_W_qkv, L0_attn_W_proj, L0_attn_b_proj), axis=-1)
    x = x + _layernorm(_L0_ffn_ref(_layernorm(x, axis=-1), L0_ffn_router, L0_ffn_experts_gate, L0_ffn_experts_up, L0_ffn_experts_down, L0_ffn_shared_gate, L0_ffn_shared_up, L0_ffn_shared_down), axis=-1)
    x = x + _layernorm(_L1_attn_ref(_layernorm(x, axis=-1), L1_attn_ln1_g, L1_attn_ln1_b, L1_attn_ln2_g, L1_attn_ln2_b, L1_attn_att_mix_k, L1_attn_att_mix_v, L1_attn_att_mix_r, L1_attn_time_decay, L1_attn_time_first, L1_attn_Wk, L1_attn_Wv, L1_attn_Wr, L1_attn_Wo, L1_attn_ffn_mix_k, L1_attn_ffn_mix_r, L1_attn_Wk_ffn, L1_attn_Wr_ffn, L1_attn_Wv_ffn), axis=-1)
    x = x + _layernorm(_L1_ffn_ref(_layernorm(x, axis=-1), L1_ffn_router_W, L1_ffn_router_b, L1_ffn_sW1, L1_ffn_sb1, L1_ffn_sW2, L1_ffn_sb2, L1_ffn_eW1, L1_ffn_eb1, L1_ffn_eW2, L1_ffn_eb2), axis=-1)
    return x

_drawn_inputs = setup_inputs


def setup_inputs(seed=0):
    import zlib

    import numpy as np

    out = dict(_drawn_inputs(seed))
    spreads = {'L0_attn_b_proj': (0.0, 0.1),
     'L1_attn_ln1_g': (1.0, 0.6),
     'L1_attn_ln1_b': (0.0, 0.8),
     'L1_attn_ln2_g': (1.0, 0.6),
     'L1_attn_ln2_b': (0.0, 0.8),
     'L1_ffn_router_b': (0.0, 0.1),
     'L1_ffn_sb1': (0.0, 0.1),
     'L1_ffn_sb2': (0.0, 0.1),
     'L1_ffn_eb1': (0.0, 0.8),
     'L1_ffn_eb2': (0.0, 0.1)}
    factors = {'L1_attn_att_mix_k': 8.0,
     'L1_attn_att_mix_v': 8.0,
     'L1_attn_att_mix_r': 8.0,
     'L1_attn_time_decay': 8.0,
     'L1_attn_time_first': 8.0,
     'L1_attn_Wk': 8.0,
     'L1_attn_Wv': 6.703,
     'L1_attn_Wr': 8.0,
     'L1_attn_Wo': 7.738,
     'L1_attn_ffn_mix_k': 8.0,
     'L1_attn_ffn_mix_r': 8.0,
     'L1_attn_Wk_ffn': 8.0,
     'L1_attn_Wr_ffn': 8.0,
     'L1_attn_Wv_ffn': 8.0,
     'L1_ffn_eW1': 3.648,
     'L1_ffn_eW2': 2.862}
    for name, (base, spread) in spreads.items():
        noise = np.random.default_rng([zlib.crc32(name.encode()), seed]).standard_normal(out[name].shape)
        drawn = base * np.exp(spread * noise) if base else spread * noise
        out[name] = jnp.asarray(drawn.astype(out[name].dtype))
    for name, factor in factors.items():
        out[name] = (out[name] * factor).astype(out[name].dtype)
    return out
```

```python
import numpy as np
import concourse.bass as bass
from concourse import mybir
from contextlib import ExitStack

FP32 = mybir.dt.float32
BF16 = mybir.dt.bfloat16
ALU = mybir.AluOpType
ACT = mybir.ActivationFunctionType
AX = mybir.AxisListType

P = 128
SEQS = 8
TILES = 4
TOK = TILES * P
C = 128
EPS = 1e-5
X_LOADS = 32
MASKED = -1e30


class Norm:

    def __init__(self, sb, sem, name, minus_half, x_loaded, eps=EPS):
        self.stats = sb(f"{name}_stats", [P, TILES, 6], FP32)
        self.moments = sb(f"{name}_moments", [P, TILES, 2], FP32)
        self.var_eps = sb(f"{name}_var_eps", [P, TILES], FP32)
        self.rstd = sb(f"{name}_rstd", [P, TILES], FP32)
        self.minus_half = minus_half
        self.eps = eps
        self.x_loaded = x_loaded
        self.stats_done = sem(f"{name}_stats_done")
        self.moments_done = sem(f"{name}_moments_done")
        self.var_done = sem(f"{name}_var_done")
        self.rstd_done = sem(f"{name}_rstd_done")

    def take_moments(self, dve, b, tile):
        for t in range(TILES):
            dve.bn_stats(self.stats[:, t, :], tile(t)).then_inc(self.stats_done, 1)
        count = dve.to_reg(b * TILES + TILES)
        dve.wait_ge(self.x_loaded, X_LOADS)
        dve.wait_ge(self.stats_done, count)
        for t in range(TILES):
            dve.bn_aggr(self.moments[:, t, :], self.stats[:, t, :]).then_inc(self.moments_done, 1)
        dve.wait_ge(self.moments_done, b * TILES + TILES)
        dve.tensor_scalar(self.var_eps[:, :], self.moments[:, :, 1], self.eps, None, ALU.add)\
           .then_inc(self.var_done, 1)

    def take_power(self, pool, b):
        pool.wait_ge(self.var_done, b + 1)
        pool.tensor_tensor(self.rstd[:, :], self.var_eps[:, :], self.minus_half[:, :], ALU.pow)\
            .then_inc(self.rstd_done, 1)

    def apply(self, dve, b, out, tile, done):
        dve.wait_ge(self.rstd_done, b + 1)
        for t in range(TILES):
            dve.tensor_scalar(out(t), tile(t), self.moments[:, t, 0:1], self.rstd[:, t:t + 1],
                              ALU.subtract, ALU.mult).then_inc(done, 1)


def attention_layer(nc, x, ident, ident_bf, minus_half, w_qkv, w_proj, b_proj, x_loaded, weights_loaded, weights_count):
    HEADS, D = 16, 8
    GROUP = TOK // P
    GROUPS = HEADS // GROUP
    UNITS = TILES * GROUPS
    SET = HEADS // 2
    TERMS_Q = ((0, 1, 4), (2, 3), (5,))
    TERMS_K = ((0, 2, 5), (1, 3), (4,))
    MAX_ROW = 64
    SCALE = float(D) ** -0.5
    LAG = 2
    PROBS = 3

    with ExitStack() as ctx:
        def sb(name, shape, dt):
            return ctx.enter_context(nc.sbuf_tensor("at_" + name, shape, dt))

        def sem(name):
            return ctx.enter_context(nc.semaphore("at_" + name))

        banks = [ctx.enter_context(nc.psum_tensor(f"at_bank{i}", [P, TOK], FP32)) for i in range(8)]
        score_bank, key_bank, out_bank, misc_bank = banks[0:2], banks[2:4], banks[4:6], banks[6:8]

        xn = sb("xn", [P, TILES, C], FP32)
        xnT = sb("xnT", [C, TOK], FP32)
        q_parts = [sb(f"q{i + 1}", [C, TOK], BF16) for i in range(3)]
        k_parts = [sb(f"k{i + 1}", [C, TOK], BF16) for i in range(3)]
        q_rest = sb("q_rest", [C, TOK], FP32)
        k_rest = sb("k_rest", [C, TOK], FP32)
        q_rows = [sb(f"q_rows{i}", [P, HEADS, TOK], BF16) for i in range(2)]
        k_rows = [sb(f"k_rows{i}", [P, HEADS, TOK], BF16) for i in range(2)]
        zero_rows = sb("zero_rows", [3, TOK], BF16)
        v_wide = [sb(f"v_wide{i}", [P, TILES, HEADS * P], FP32) for i in range(2)]
        probs = sb("probs", [P, PROBS, TOK], FP32)
        sums = sb("sums", [P, P], FP32)
        sums_inv = sb("sums_inv", [P, P], FP32)
        outT = sb("outT", [C, TOK], FP32)
        neg_max = sb("neg_max", [P, TILES, HEADS], FP32)
        max_rest = sb("max_rest", [P, TILES, HEADS], FP32)
        max_parts = sb("max_parts", [P, TILES, 3, HEADS], BF16)
        max_partsT = sb("max_partsT", [3 * HEADS, TOK], BF16)
        mask = sb("mask", [P, P], BF16)
        y = sb("y", [P, TILES, C], FP32)
        norm_in = Norm(sb, sem, "norm_in", minus_half, x_loaded)
        norm_out = Norm(sb, sem, "norm_out", minus_half, x_loaded)

        filled = sem("filled")
        mask_zeroed = sem("mask_zeroed")
        k_zeroed = sem("k_zeroed")
        v_zeroed = sem("v_zeroed")
        xn_done = sem("xn_done")
        xT_moved = sem("xT_moved")
        xnT_done = sem("xnT_done")
        qk_projected = sem("qk_projected")
        v_projected = sem("v_projected")
        part1_done = sem("part1_done")
        rest_done = sem("rest_done")
        part2_done = sem("part2_done")
        part3_done = sem("part3_done")
        rows_loaded = sem("rows_loaded")
        v_done = sem("v_done")
        scored = sem("scored")
        max_done = sem("max_done")
        max_split = sem("max_split")
        max_moved = sem("max_moved")
        maxT_done = sem("maxT_done")
        max_loaded = sem("max_loaded")
        key_scored = sem("key_scored")
        exp_done = sem("exp_done")
        probs_done = sem("probs_done")
        weighed = sem("weighed")
        sums_done = sem("sums_done")
        inverted = sem("inverted")
        outT_done = sem("outT_done")
        proj_done = sem("proj_done")
        y_done = sem("y_done")
        yn_done = sem("yn_done")
        x_added = sem("x_added")
        FILLS = 1 + 1 + 2 + 2 + 4

        def tile_of(ap, t):
            return ap[:, t * P:(t + 1) * P]

        def own_columns(wide, s, start):
            w = wide[:, :, s * SET * P + start:(s + 1) * SET * P]
            return bass.AP(w.tensor, w.offset, [w.ap[0], w.ap[1], [P + D, SET], [1, D]])

        with nc.Block() as block:

            @block.sync
            def _(sp):
                def spread(b, p):
                    def send(parts, rows, i, terms):
                        for r in terms:
                            sp.dma_start(rows[p][r * D:(r + 1) * D, :, :],
                                         parts[i][:, :])\
                              .then_inc(rows_loaded, 16)
                    sp.wait_ge(part1_done, 2 * b + 1)
                    send(q_parts, q_rows, 0, TERMS_Q[0])
                    sp.dma_start(q_rows[p][MAX_ROW:MAX_ROW + 3, :, :],
                                 zero_rows[:, :].rearrange("r (a t) -> r a t", a=1).to_broadcast([3, HEADS, TOK]))\
                      .then_inc(rows_loaded, 16)
                    sp.wait_ge(part1_done, 2 * b + 2)
                    send(k_parts, k_rows, 0, TERMS_K[0])
                    sp.wait_ge(part2_done, 2 * b + 1)
                    send(q_parts, q_rows, 1, TERMS_Q[1])
                    sp.wait_ge(part2_done, 2 * b + 2)
                    send(k_parts, k_rows, 1, TERMS_K[1])
                    sp.wait_ge(part3_done, 2 * b + 1)
                    send(q_parts, q_rows, 2, TERMS_Q[2])
                    sp.wait_ge(part3_done, 2 * b + 2)
                    send(k_parts, k_rows, 2, TERMS_K[2])

                def send_max(b, p):
                    sp.wait_ge(maxT_done, b + 1)
                    for i in range(3):
                        sp.dma_start(q_rows[p][MAX_ROW + i:MAX_ROW + i + 1, :, :],
                                     max_partsT[i * HEADS:(i + 1) * HEADS, :])\
                          .then_inc(max_loaded, 16)

                def body(b, p, last=False):
                    if not last:
                        spread(b + 1, 1 - p)
                    send_max(b, p)

                sp.wait_ge(filled, FILLS)
                spread(0, 0)
                body(0, 0)
                with sp.Fori(0, (SEQS - 2) // 2) as pair:
                    b = 2 * pair + 1
                    body(b, 1)
                    body(b + 1, 0)
                body(SEQS - 1, 1, last=True)

            @block.gpsimd
            def _(pool):
                pool.memset(zero_rows[:, :], 0.0).then_inc(filled, 1)
                pool.memset(mask[:, :], 0.0).then_inc(mask_zeroed, 1)
                pool.wait_ge(mask_zeroed, 1)
                pool.affine_select(out=mask[:, :], in_=mask[:, :], compare_op=ALU.is_ge, fill=MASKED,
                                   base=0, pattern=[[-1, P]], channel_multiplier=1).then_inc(filled, 1)

                def third_parts(b):
                    for n, (parts, rest) in enumerate(((q_parts, q_rest), (k_parts, k_rest))):
                        pool.wait_ge(part2_done, 2 * b + n + 1)
                        pool.tensor_tensor(parts[2][:, :], rest[:, :], parts[1][:, :], ALU.subtract)\
                            .then_inc(part3_done, 1)

                def mask_probs(b, u):
                    count = pool.to_reg(b * UNITS + u + 1)
                    pool.wait_ge(mask_zeroed, 1)
                    pool.wait_ge(exp_done, count)
                    slot = probs[:, u % PROBS, :]
                    pool.affine_select(out=slot, in_=slot, compare_op=ALU.is_ge, fill=0.0, base=0,
                                       pattern=[[0, GROUP], [1, P]], channel_multiplier=-1)\
                        .then_inc(probs_done, 1)

                def add_y(b):
                    pool.wait_ge(yn_done, 4 * b + 4)
                    xs = x[:, bass.ds(4 * b, TILES), :]
                    pool.tensor_tensor(xs, xs, y[:, :, :], ALU.add).then_inc(x_added, 1)

                def body(b, first=False, last=False):
                    if not last:
                        norm_in.take_power(pool, b + 1)
                    if not first:
                        norm_out.take_power(pool, b - 1)
                    if not last:
                        third_parts(b + 1)
                    if not first:
                        add_y(b - 1)
                    for u in range(UNITS):
                        mask_probs(b, u)

                for rows in q_rows:
                    pool.memset(rows[:, :, :].bitcast(FP32), 0.0).then_inc(filled, 1)
                norm_in.take_power(pool, 0)
                third_parts(0)
                body(0, first=True)
                with pool.Fori(1, SEQS - 1) as b:
                    body(b)
                body(SEQS - 1, last=True)
                norm_out.take_power(pool, SEQS - 1)
                add_y(SEQS - 1)

            @block.scalar
            def _(act):
                def move_xT(b):
                    act.wait_ge(xT_moved, b + 1)
                    act.activation(xnT[:, :], misc_bank[0][:, :], ACT.Copy).then_inc(xnT_done, 1)

                def parts(b):
                    for n, q in enumerate((q_parts, k_parts)):
                        act.wait_ge(qk_projected, 2 * b + n + 1)
                        act.activation(q[0][:, :], score_bank[n][:, :], ACT.Copy).then_inc(part1_done, 1)
                    for n, (q, rest) in enumerate(((q_parts, q_rest), (k_parts, k_rest))):
                        act.wait_ge(rest_done, 2 * b + n + 1)
                        act.activation(q[1][:, :], rest[:, :], ACT.Copy).then_inc(part2_done, 1)

                def spread_v(b, p):
                    act.wait_ge(v_projected, b + 1)
                    for s in range(2):
                        v = misc_bank[0][:, :].rearrange("p (t s c) -> p t s c", t=TILES, s=2)[:, :, s, :]
                        act.activation(own_columns(v_wide[p], s, 0), v.rearrange("p t (h d) -> p t h d", d=D), ACT.Copy)\
                           .then_inc(v_done, 1)

                def move_max(b):
                    act.wait_ge(max_moved, b + 1)
                    act.activation(max_partsT[:, :], key_bank[0][:, :].bitcast(BF16)[0:3 * HEADS, 0:TOK], ACT.Copy)\
                       .then_inc(maxT_done, 1)

                def exps(b, u, first):
                    act.wait_ge(key_scored, b * UNITS + u + 1)
                    if not first or u >= PROBS:
                        act.wait_ge(weighed, b * UNITS + u + 1 - PROBS)
                    act.activation(probs[:, u % PROBS, :], key_bank[u % 2][:, :], ACT.Exp, scale=SCALE)\
                       .then_inc(exp_done, 1)

                def body(b, p, first=False, last=False):
                    if not last:
                        move_xT(b + 1)
                        parts(b + 1)
                    move_max(b)
                    if not last:
                        spread_v(b + 1, 1 - p)
                    for u in range(UNITS):
                        exps(b, u, first)

                for i in range(2):
                    act.memzero(v_wide[i][:, :, :]).then_inc(v_zeroed, 1)
                move_xT(0)
                parts(0)
                act.wait_ge(filled, FILLS)
                spread_v(0, 0)
                body(0, 0, first=True)
                with act.Fori(0, (SEQS - 2) // 2) as pair:
                    b = 2 * pair + 1
                    body(b, 1)
                    body(b + 1, 0)
                body(SEQS - 1, 1, last=True)

            @block.tensor
            def _(pe):
                def move_x(b, first=False):
                    if not first:
                        pe.wait_ge(v_done, 2 * b)
                    for t in range(TILES):
                        pe.wait_ge(xn_done, 4 * b + t + 1)
                        mm = pe.transpose(tile_of(misc_bank[0], t), xn[:, t, :], ident[:, :])
                    mm.then_inc(xT_moved, 1)

                def project_qk(b):
                    pe.wait_ge(xnT_done, b + 1)
                    for n in range(2):
                        pe.matmul(score_bank[n][:, :], w_qkv[:, n * C:(n + 1) * C], xnT[:, :],
                                  start=True, stop=True).then_inc(qk_projected, 1)

                def project_v(b):
                    for t in range(TILES):
                        mm = pe.matmul(tile_of(misc_bank[0], t), tile_of(xnT, t), w_qkv[:, 2 * C:3 * C],
                                       start=True, stop=True)
                    mm.then_inc(v_projected, 1)

                def scores(b, p, u, first):
                    t, g = u // GROUPS, u % GROUPS
                    bank = score_bank[u % 2]
                    if u < 2:
                        pe.wait_ge(rest_done, 2 * b + u + 1)
                    else:
                        pe.wait_ge(max_done, b * UNITS + u - 1)
                    pe.matmul(bank[:, :], ident_bf[:, :],
                              mask[:, :].rearrange("p (a k) -> p a k", a=1).to_broadcast([P, GROUP, P]),
                              start=True, stop=False, skip_group_check=True)
                    for j in range(GROUP):
                        h = g * GROUP + j
                        mm = pe.matmul(tile_of(bank, j), q_rows[p][:, h, t * P:(t + 1) * P],
                                       k_rows[p][:, h, t * P:(t + 1) * P], start=False, stop=True,
                                       skip_group_check=True)
                    mm.then_inc(scored, 1)

                def move_max(b):
                    count = pe.to_reg(4 * b + 4)
                    pe.wait_ge(weights_loaded, weights_count)
                    pe.wait_ge(max_split, count)
                    for t in range(TILES):
                        mm = pe.transpose(key_bank[0][:, :].bitcast(BF16)[0:3 * HEADS, t * P:(t + 1) * P],
                                          max_parts[:, t, :, :].rearrange("p i h -> p (i h)"), ident_bf[:, :])
                    mm.then_inc(max_moved, 1)

                def key_scores(b, p, u):
                    t, g = u // GROUPS, u % GROUPS
                    if u == 0:
                        pe.wait_ge(max_loaded, 48 * b + 48)
                        pe.wait_ge(maxT_done, b + 1)
                    if u >= 2:
                        pe.wait_ge(exp_done, b * UNITS + u - 1)
                    for j in range(GROUP):
                        h = g * GROUP + j
                        mm = pe.matmul(tile_of(key_bank[u % 2], j), k_rows[p][:, h, t * P:(t + 1) * P],
                                       q_rows[p][:, h, t * P:(t + 1) * P], start=True, stop=True)
                    mm.then_inc(key_scored, 1)

                def weigh(b, p, u, first):
                    t, g = u // GROUPS, u % GROUPS
                    pe.wait_ge(probs_done, b * UNITS + u + 1)
                    if u == 0:
                        pe.wait_ge(v_done, 2 * b + 2)
                    if g == 0 and (t >= 2 or not first):
                        pe.wait_ge(outT_done, b * 2 * TILES + 2 * (t - 1))
                    for j in range(GROUP):
                        h = g * GROUP + j
                        s = h // SET
                        mm = pe.matmul(tile_of(out_bank[t % 2], s), v_wide[p][:, t, h * P:(h + 1) * P],
                                       probs[:, u % PROBS, j * P:(j + 1) * P],
                                       start=(h % SET == 0), stop=(h % SET == SET - 1))
                    mm.then_inc(weighed, 1)

                def project_out(b):
                    pe.wait_ge(outT_done, 2 * TILES * b + 2 * TILES)
                    for t in range(TILES):
                        mm = pe.matmul(tile_of(misc_bank[1], t), tile_of(outT, t), w_proj[:, :],
                                       start=True, stop=True)
                    mm.then_inc(proj_done, 1)

                def body(b, p, first=False, last=False):
                    if first:
                        pe.wait_ge(filled, FILLS)
                    pe.wait_ge(rows_loaded, 208 * b + 208)
                    for u in range(UNITS):
                        scores(b, p, u, first)
                    if not first:
                        project_out(b - 1)
                    if not last:
                        move_x(b + 1)
                        pe.wait_ge(max_done, UNITS * b + UNITS)
                        project_qk(b + 1)
                    move_max(b)
                    if not last:
                        project_v(b + 1)
                    for u in range(UNITS + LAG):
                        if u < UNITS:
                            key_scores(b, p, u)
                        if u >= LAG:
                            weigh(b, p, u - LAG, first)

                pe.wait_ge(weights_loaded, weights_count)
                move_x(0, first=True)
                project_qk(0)
                project_v(0)
                body(0, 0, first=True)
                with pe.Fori(0, (SEQS - 2) // 2) as pair:
                    b = 2 * pair + 1
                    body(b, 1)
                    body(b + 1, 0)
                body(SEQS - 1, 1, last=True)
                project_out(SEQS - 1)

            @block.vector
            def _(dve):
                def fill():
                    for rows in k_rows:
                        dve.memset(rows[:, :, :].bitcast(FP32), 0.0).then_inc(k_zeroed, 1)
                    for i in range(2):
                        dve.wait_ge(k_zeroed, i + 1)
                        dve.memset(k_rows[i][MAX_ROW:MAX_ROW + 32, :, :], 1.0).then_inc(filled, 1)
                    dve.wait_ge(v_zeroed, 2)
                    for s in range(2):
                        for i in range(2):
                            for t in range(TILES):
                                mm = dve.memset(own_columns(v_wide[i], s, P // 2)[:, t, :, :], 1.0)
                                if t == TILES - 1:
                                    mm.then_inc(filled, 1)

                def normalize(b):
                    x_tile = lambda t: x[:, bass.ds(4 * b + t, 1), :].rearrange("p a c -> p (a c)")
                    norm_in.take_moments(dve, b, x_tile)
                    norm_in.apply(dve, b, lambda t: xn[:, t, :], x_tile, xn_done)

                def rests(b):
                    for n, (q, rest) in enumerate(((q_parts, q_rest), (k_parts, k_rest))):
                        dve.wait_ge(part1_done, 2 * b + n + 1)
                        dve.tensor_tensor(rest[:, :], score_bank[n][:, :], q[0][:, :], ALU.subtract)\
                           .then_inc(rest_done, 1)

                def maxima(b):
                    for u in range(UNITS):
                        t, g = u // GROUPS, u % GROUPS
                        dve.wait_ge(scored, b * UNITS + u + 1)
                        dve.tensor_reduce(neg_max[:, t, g * GROUP:(g + 1) * GROUP],
                                          score_bank[u % 2][:, :].rearrange("p (j k) -> p j k", k=P),
                                          AX.X, ALU.max, negate=True).then_inc(max_done, 1)

                def split_max(b):
                    dve.wait_ge(max_done, b * UNITS + UNITS)
                    dve.tensor_copy(max_parts[:, :, 0, :], neg_max[:, :, :]).then_inc(max_split, 1)
                    dve.wait_ge(max_split, 4 * b + 1)
                    dve.tensor_tensor(max_rest[:, :, :], neg_max[:, :, :], max_parts[:, :, 0, :],
                                      ALU.subtract).then_inc(max_split, 1)
                    dve.wait_ge(max_split, 4 * b + 2)
                    dve.tensor_copy(max_parts[:, :, 1, :], max_rest[:, :, :]).then_inc(max_split, 1)
                    dve.wait_ge(max_split, 4 * b + 3)
                    dve.tensor_tensor(max_parts[:, :, 2, :], max_rest[:, :, :], max_parts[:, :, 1, :],
                                      ALU.subtract).then_inc(max_split, 1)

                def add_bias(b, first):
                    dve.wait_ge(proj_done, b + 1)
                    if not first:
                        dve.wait_ge(x_added, b)
                    dve.tensor_tensor(y[:, :, :], misc_bank[1][:, :].rearrange("p (t c) -> p t c", t=TILES),
                                      b_proj[:, :].rearrange("p (a c) -> p a c", a=1).to_broadcast([P, TILES, C]),
                                      ALU.add).then_inc(y_done, 1)

                def y_moments(b):
                    dve.wait_ge(y_done, b + 1)
                    norm_out.take_moments(dve, b, lambda t: y[:, t, :])

                def y_apply(b):
                    norm_out.apply(dve, b, lambda t: y[:, t, :], lambda t: y[:, t, :], yn_done)

                def scale_out(b, t):
                    n = b * TILES + t
                    o = out_bank[t % 2]
                    dve.wait_ge(weighed, UNITS * b + GROUPS * (t + 1))
                    for s in range(2):
                        dve.tensor_scalar(sums[s * 64:(s + 1) * 64, :], o[64:128, s * P:(s + 1) * P],
                                          1e-6, None, ALU.add).then_inc(sums_done, 1)
                    dve.wait_ge(sums_done, 2 * n + 2)
                    dve.reciprocal(sums_inv[:, :], sums[:, :]).then_inc(inverted, 1)
                    dve.wait_ge(inverted, n + 1)
                    for s in range(2):
                        dve.tensor_tensor(outT[s * 64:(s + 1) * 64, t * P:(t + 1) * P],
                                          o[0:64, s * P:(s + 1) * P], sums_inv[s * 64:(s + 1) * 64, :],
                                          ALU.mult).then_inc(outT_done, 1)

                def body(b, first=False, last=False, second=False):
                    if not last:
                        dve.wait_ge(xT_moved, b + 1)
                        normalize(b + 1)
                    if not first:
                        scale_out(b - 1, TILES - 1)
                    maxima(b)
                    split_max(b)
                    if not first:
                        add_bias(b - 1, second)
                        y_moments(b - 1)
                    if not last:
                        rests(b + 1)
                    if not first:
                        y_apply(b - 1)
                    if not first:
                        dve.wait_ge(proj_done, b)
                    for t in range(TILES - 1):
                        scale_out(b, t)

                dve.wait_ge(x_loaded, 32)
                normalize(0)
                fill()
                rests(0)
                body(0, first=True)
                with dve.Fori(1, SEQS - 1) as b:
                    body(b)
                body(SEQS - 1, last=True)
                scale_out(SEQS - 1, TILES - 1)
                add_bias(SEQS - 1, False)
                y_moments(SEQS - 1)
                y_apply(SEQS - 1)


class Router:

    def __init__(self, nc, ctx, name, x, x_loaded, ident, ident_bf, minus_half, experts, top_k, w_router, b_router, bank):
        def sb(n, shape, dt=FP32):
            return ctx.enter_context(nc.sbuf_tensor(f"{name}_{n}", shape, dt))

        def sem(n):
            return ctx.enter_context(nc.semaphore(f"{name}_{n}"))

        self.x, self.x_loaded, self.ident, self.ident_bf, self.bank = x, x_loaded, ident, ident_bf, bank
        self.E, self.K, self.w_router, self.b_router = experts, top_k, w_router, b_router
        self.PAD = 8 - top_k
        self.norm = Norm(sb, sem, "norm", minus_half, x_loaded)
        self.xn = sb("xn", [P, TILES, C])
        self.xnT = [sb(f"xnT{i}", [C, TOK]) for i in range(2)]
        self.logits = sb("logits", [P, TILES, experts])
        self.largest = sb("largest", [P, TILES])
        self.shifted = sb("shifted", [P, TILES, experts])
        self.exps = sb("exps", [P, TILES, experts])
        self.total = sb("total", [P, TILES])
        self.total_inv = sb("total_inv", [P, TILES])
        self.probs = sb("probs", [P, TILES, experts + self.PAD])
        self.top = sb("top", [P, TILES, 8])
        self.taken = sb("taken", [P, TILES, 8])
        self.left = sb("left", [P, TILES, experts + self.PAD])
        self.coef = sb("coef", [P, TILES, experts])
        self.coef_rest = sb("coef_rest", [P, TILES, experts])
        self.coef_parts = sb("coef_parts", [P, TILES, 3, experts], BF16)
        self.coefT = [sb(f"coefT{i}", [P, TOK], BF16) for i in range(2)]
        self.xn_done = sem("xn_done")
        self.xT_moved = sem("xT_moved")
        self.xnT_done = sem("xnT_done")
        self.logits_done = sem("logits_done")
        self.soft = sem("soft")
        self.exp_done = sem("exp_done")
        self.top_done = sem("top_done")
        self.split = sem("split")
        self.coef_moved = sem("coef_moved")
        self.coefT_done = sem("coefT_done")

    SOFT = 6

    def fill(self, dve, done):
        for j in range(self.PAD):
            dve.memset(self.probs[:, :, self.E + j:self.E + j + 1], -1.0 - j)
            last = dve.memset(self.taken[:, :, self.K + j:self.K + j + 1], -1.0 - j)
        last.then_inc(done, 1)
        for coefT in self.coefT:
            last = dve.memset(coefT[:, :].bitcast(FP32), 0.0)
        last.then_inc(done, 1)

    def x_tile(self, b):
        return lambda t: self.x[:, bass.ds(4 * b + t, 1), :].rearrange("p a c -> p (a c)")

    def take_moments(self, dve, b):
        self.norm.take_moments(dve, b, self.x_tile(b))

    def normalize(self, dve, b, first=False):
        if not first:
            dve.wait_ge(self.xT_moved, b)
        self.norm.apply(dve, b, lambda t: self.xn[:, t, :], self.x_tile(b), self.xn_done)

    def shift(self, dve, b):
        E, S = self.E, self.SOFT
        dve.wait_ge(self.logits_done, b + 1)
        logits = self.bank[:, 0:TILES * E].rearrange("p (t e) -> p t e", e=E)
        if self.b_router is not None:
            dve.tensor_tensor(self.logits[:, :, :], logits,
                              self.b_router[:, :].rearrange("p (a e) -> p a e", a=1).to_broadcast([P, TILES, E]),
                              ALU.add).then_inc(self.soft, 1)
        else:
            dve.tensor_copy(self.logits[:, :, :], logits).then_inc(self.soft, 1)
        dve.wait_ge(self.soft, S * b + 1)
        dve.tensor_reduce(self.largest[:, :], self.logits[:, :, :], AX.X, ALU.max).then_inc(self.soft, 1)
        dve.wait_ge(self.soft, S * b + 2)
        dve.tensor_tensor(self.shifted[:, :, :], self.logits[:, :, :],
                          self.largest[:, :].rearrange("p (t a) -> p t a", a=1).to_broadcast([P, TILES, E]),
                          ALU.subtract).then_inc(self.soft, 1)

    def choose(self, dve, b):
        E, K, S = self.E, self.K, self.SOFT
        T = 2 * TILES + 2
        dve.wait_ge(self.exp_done, b + 1)
        dve.tensor_reduce(self.total[:, :], self.exps[:, :, :], AX.X, ALU.add).then_inc(self.soft, 1)
        dve.wait_ge(self.soft, S * b + 4)
        dve.reciprocal(self.total_inv[:, :], self.total[:, :]).then_inc(self.soft, 1)
        dve.wait_ge(self.soft, S * b + 5)
        dve.tensor_tensor(self.probs[:, :, 0:E], self.exps[:, :, :],
                          self.total_inv[:, :].rearrange("p (t a) -> p t a", a=1).to_broadcast([P, TILES, E]),
                          ALU.mult).then_inc(self.soft, 1)
        count = dve.to_reg(S * b + 6)
        dve.wait_ge(self.x_loaded, X_LOADS)
        dve.wait_ge(self.soft, count)
        for t in range(TILES):
            dve.max(self.top[:, t, :], self.probs[:, t, 0:E]).then_inc(self.top_done, 1)
        dve.wait_ge(self.top_done, T * b + TILES)
        dve.tensor_copy(self.taken[:, :, 0:K], self.top[:, :, 0:K]).then_inc(self.top_done, 1)
        count = dve.to_reg(T * b + TILES + 1)
        dve.wait_ge(self.x_loaded, X_LOADS)
        dve.wait_ge(self.top_done, count)
        for t in range(TILES):
            dve.match_replace(self.left[:, t, :], self.taken[:, t, :], self.probs[:, t, :], 0.0)\
               .then_inc(self.top_done, 1)
        dve.wait_ge(self.top_done, T * b + 2 * TILES + 1)
        dve.tensor_tensor(self.coef[:, :, :], self.probs[:, :, 0:E], self.left[:, :, 0:E], ALU.subtract)\
           .then_inc(self.top_done, 1)
        dve.wait_ge(self.top_done, T * b + T)
        dve.tensor_copy(self.coef_parts[:, :, 0, :], self.coef[:, :, :]).then_inc(self.split, 1)
        dve.wait_ge(self.split, 4 * b + 1)
        dve.tensor_tensor(self.coef_rest[:, :, :], self.coef[:, :, :], self.coef_parts[:, :, 0, :],
                          ALU.subtract).then_inc(self.split, 1)
        dve.wait_ge(self.split, 4 * b + 2)
        dve.tensor_copy(self.coef_parts[:, :, 1, :], self.coef_rest[:, :, :]).then_inc(self.split, 1)
        dve.wait_ge(self.split, 4 * b + 3)
        dve.tensor_tensor(self.coef_parts[:, :, 2, :], self.coef_rest[:, :, :], self.coef_parts[:, :, 1, :],
                          ALU.subtract).then_inc(self.split, 1)

    def move_xT(self, act, b, p):
        act.wait_ge(self.xT_moved, b + 1)
        act.activation(self.xnT[p][:, :], self.bank[:, :], ACT.Copy).then_inc(self.xnT_done, 1)

    def exponents(self, act, b):
        act.wait_ge(self.soft, self.SOFT * b + 3)
        act.activation(self.exps[:, :, :], self.shifted[:, :, :], ACT.Exp).then_inc(self.exp_done, 1)

    def move_coef(self, act, b, p):
        act.wait_ge(self.coef_moved, b + 1)
        act.activation(self.coefT[p][0:3 * self.E, :], self.bank[:, :].bitcast(BF16)[0:3 * self.E, 0:TOK], ACT.Copy)\
           .then_inc(self.coefT_done, 1)

    def move_x(self, pe, b, first=False):
        if not first:
            pe.wait_ge(self.coefT_done, b)
        for t in range(TILES):
            pe.wait_ge(self.xn_done, 4 * b + t + 1)
            mm = pe.transpose(self.bank[:, t * P:(t + 1) * P], self.xn[:, t, :], self.ident[:, :])
        mm.then_inc(self.xT_moved, 1)

    def take_logits(self, pe, b, p):
        pe.wait_ge(self.xnT_done, b + 1)
        for t in range(TILES):
            mm = pe.matmul(self.bank[:, t * self.E:(t + 1) * self.E], self.xnT[p][:, t * P:(t + 1) * P],
                           self.w_router[:, :], start=True, stop=True)
        mm.then_inc(self.logits_done, 1)

    def move_parts(self, pe, b):
        count = pe.to_reg(4 * b + 4)
        pe.wait_ge(self.x_loaded, X_LOADS)
        pe.wait_ge(self.split, count)
        for t in range(TILES):
            mm = pe.transpose(self.bank[:, :].bitcast(BF16)[0:3 * self.E, t * P:(t + 1) * P],
                              self.coef_parts[:, t, :, :].rearrange("p i e -> p (i e)"), self.ident_bf[:, :])
        mm.then_inc(self.coef_moved, 1)


def fill_selectors(pool, selectors, experts, width, done):
    pool.memset(selectors[:, :], 0.0).then_inc(done, 1)
    view = selectors[:, :].rearrange("r (e w) -> r e w", w=width)
    for i in range(3):
        pool.wait_ge(done, i + 1)
        pool.affine_select(out=view, in_=view, compare_op=ALU.not_equal, fill=1.0, base=-i * experts,
                           pattern=[[-1, experts], [0, width]], channel_multiplier=1).then_inc(done, 1)


def swiglu_experts_layer(nc, x, x_loaded, ident, ident_bf, minus_half, w, weights_loaded, weights_count):
    E, K, D = 8, 2, 64
    PAIRS = E * D // P
    STEPS = PAIRS + 1

    with ExitStack() as ctx:
        def sb(name, shape, dt=FP32):
            return ctx.enter_context(nc.sbuf_tensor("sw_" + name, shape, dt))

        def sem(name):
            return ctx.enter_context(nc.semaphore("sw_" + name))

        banks = [ctx.enter_context(nc.psum_tensor(f"sw_bank{i}", [P, TOK], FP32)) for i in range(8)]
        gate_bank, up_bank, out_bank, coef_bank = banks[1:3], banks[3:5], banks[5:7], banks[7]
        r = Router(nc, ctx, "swr", x, x_loaded, ident, ident_bf, minus_half, E, K, w["router"], None, banks[0])
        norm_out = Norm(sb, sem, "norm_out", minus_half, x_loaded)
        selectors = sb("selectors", [P, E * D], BF16)
        tanh_gate = sb("tanh_gate", [P, 2, TOK])
        gated = sb("gated", [P, 2, TOK])
        hidden = sb("hidden", [P, 2, TOK])
        weighed = sb("weighed", [P, 2, TOK])
        yn = sb("yn", [P, TILES, C])

        filled = sem("filled")
        selectors_done = sem("selectors_done")
        gate_up = sem("gate_up")
        coef_spread = sem("coef_spread")
        tanh_done = sem("tanh_done")
        gated_done = sem("gated_done")
        hidden_done = sem("hidden_done")
        weighed_done = sem("weighed_done")
        summed = sem("summed")
        yn_done = sem("yn_done")
        x_added = sem("x_added")

        with nc.Block() as block:

            @block.gpsimd
            def _(pool):
                fill_selectors(pool, selectors, E, D, selectors_done)

                def add(b):
                    pool.wait_ge(yn_done, 4 * b + 4)
                    xs = x[:, bass.ds(4 * b, TILES), :]
                    pool.tensor_tensor(xs, xs, yn[:, :, :], ALU.add).then_inc(x_added, 1)

                def body(b, last=False):
                    if not last:
                        r.norm.take_power(pool, b + 1)
                    norm_out.take_power(pool, b)
                    add(b)

                r.norm.take_power(pool, 0)
                with pool.Fori(0, SEQS - 1) as b:
                    body(b)
                body(SEQS - 1, last=True)

            @block.scalar
            def _(act):
                def tanh(b, i, first):
                    n = b * STEPS + i
                    act.wait_ge(gate_up, n + 1)
                    if not first or i >= 2:
                        act.wait_ge(gated_done, n - 1)
                    act.activation(tanh_gate[:, i % 2, :], gate_bank[i % 2][:, :], ACT.Tanh, scale=0.5)\
                       .then_inc(tanh_done, 1)

                def body(b, p, first=False, last=False):
                    for i in range(STEPS):
                        tanh(b, i, first)
                        if not last:
                            if i == 0:
                                r.move_xT(act, b + 1, 1 - p)
                            if i == 2:
                                r.exponents(act, b + 1)
                            if i == 4:
                                r.move_coef(act, b + 1, 1 - p)

                act.wait_ge(filled, 2)
                r.move_xT(act, 0, 0)
                r.exponents(act, 0)
                r.move_coef(act, 0, 0)
                body(0, 0, first=True)
                with act.Fori(0, (SEQS - 2) // 2) as pair:
                    b = 2 * pair + 1
                    body(b, 1)
                    body(b + 1, 0)
                body(SEQS - 1, 1, last=True)

            @block.tensor
            def _(pe):
                def gate_and_up(b, p, i, first):
                    n = b * STEPS + i
                    if not first or i >= 2:
                        pe.wait_ge(hidden_done, n - 1)
                    cols = slice((i - 1) * P, i * P)
                    for bank, name in ((gate_bank, "gate"), (up_bank, "up")):
                        lhs = w["shared_" + name][:, :] if i == 0 else w[name][:, cols]
                        mm = pe.matmul(bank[i % 2][:, :], lhs, r.xnT[p][:, :], start=True, stop=True)
                    mm.then_inc(gate_up, 1)
                    if i >= 1:
                        m = b * PAIRS + i - 1
                        if i == 1:
                            pe.wait_ge(r.coefT_done, b + 1)
                        if not first or i >= 2:
                            pe.wait_ge(weighed_done, m)
                        pe.matmul(coef_bank[:, :], selectors[:, cols], r.coefT[p][:, :], start=True, stop=True)\
                          .then_inc(coef_spread, 1)

                def down(b, o, i, first, second):
                    if i == 0:
                        pe.wait_ge(hidden_done, b * STEPS + 1)
                        if not first and not second:
                            pe.wait_ge(yn_done, 4 * b - 4)
                    else:
                        pe.wait_ge(weighed_done, b * PAIRS + i)
                    h = hidden if i == 0 else weighed
                    rhs = w["shared_down"][:, :] if i == 0 else w["down"][:, i - 1, :]
                    for t in range(TILES):
                        mm = pe.matmul(out_bank[o][:, t * P:(t + 1) * P], h[:, i % 2, t * P:(t + 1) * P], rhs,
                                       start=(i == 0 and t == 0), stop=(i == STEPS - 1), skip_group_check=True)
                    mm.then_inc(summed, 1)

                def body(b, p, first=False, last=False, second=False):
                    for i in range(STEPS + 1):
                        if i < STEPS:
                            gate_and_up(b, p, i, first)
                        if i >= 1:
                            down(b, p, i - 1, first, second)
                        if not last:
                            if i == 0:
                                r.move_x(pe, b + 1)
                            if i == 1:
                                r.take_logits(pe, b + 1, 1 - p)
                            if i == 4:
                                r.move_parts(pe, b + 1)

                pe.wait_ge(weights_loaded, weights_count)
                pe.wait_ge(selectors_done, 4)
                r.move_x(pe, 0, first=True)
                r.take_logits(pe, 0, 0)
                r.move_parts(pe, 0)
                body(0, 0, first=True)
                body(1, 1, second=True)
                with pe.Fori(0, (SEQS - 4) // 2) as pair:
                    b = 2 * pair + 2
                    body(b, 0)
                    body(b + 1, 1)
                body(SEQS - 2, 0)
                body(SEQS - 1, 1, last=True)

            @block.vector
            def _(dve):
                def hide(b, i, first):
                    n = b * STEPS + i
                    s = i % 2
                    dve.wait_ge(tanh_done, n + 1)
                    dve.scalar_tensor_tensor(out=gated[:, s, :], in0=tanh_gate[:, s, :], scalar=1.0,
                                             in1=gate_bank[s][:, :], op0=ALU.add, op1=ALU.mult)\
                       .then_inc(gated_done, 1)
                    dve.wait_ge(gated_done, n + 1)
                    if i == 0 and not first:
                        dve.wait_ge(summed, b * STEPS - STEPS + 1)
                    dve.scalar_tensor_tensor(out=hidden[:, s, :], in0=gated[:, s, :], scalar=0.5,
                                             in1=up_bank[s][:, :], op0=ALU.mult, op1=ALU.mult)\
                       .then_inc(hidden_done, 1)
                    if i >= 1:
                        m = b * PAIRS + i - 1
                        dve.wait_ge(hidden_done, n + 1)
                        dve.wait_ge(coef_spread, m + 1)
                        if not first or i >= 3:
                            dve.wait_ge(summed, n - 1)
                        dve.tensor_tensor(weighed[:, s, :], hidden[:, s, :], coef_bank[:, :], ALU.mult)\
                           .then_inc(weighed_done, 1)

                def out_tile(o):
                    return lambda t: out_bank[o][:, t * P:(t + 1) * P]

                def body(b, p, first=False, last=False):
                    if not last:
                        r.take_moments(dve, b + 1)
                    hide(b, 0, first)
                    if not last:
                        r.normalize(dve, b + 1)
                    hide(b, 1, first)
                    hide(b, 2, first)
                    if not last:
                        r.shift(dve, b + 1)
                    hide(b, 3, first)
                    if not last:
                        r.choose(dve, b + 1)
                    hide(b, 4, first)
                    dve.wait_ge(summed, STEPS * b + STEPS)
                    norm_out.take_moments(dve, b, out_tile(p))
                    if not first:
                        dve.wait_ge(x_added, b)
                    norm_out.apply(dve, b, lambda t: yn[:, t, :], out_tile(p), yn_done)

                r.fill(dve, filled)
                r.take_moments(dve, 0)
                r.normalize(dve, 0, first=True)
                r.shift(dve, 0)
                r.choose(dve, 0)
                body(0, 0, first=True)
                with dve.Fori(0, (SEQS - 2) // 2) as pair:
                    b = 2 * pair + 1
                    body(b, 1)
                    body(b + 1, 0)
                body(SEQS - 1, 1, last=True)


def relu_experts_layer(nc, x, x_loaded, ident, ident_bf, minus_half, w, weights_loaded, weights_count):
    E, K = 15, 3
    STEPS = E + 1
    HIDDEN = 3
    ONES = 96

    with ExitStack() as ctx:
        def sb(name, shape, dt=FP32):
            return ctx.enter_context(nc.sbuf_tensor("re_" + name, shape, dt))

        def sem(name):
            return ctx.enter_context(nc.semaphore("re_" + name))

        banks = [ctx.enter_context(nc.psum_tensor(f"re_bank{i}", [P, TOK], FP32)) for i in range(8)]
        hidden_bank, coef_bank, out_bank = banks[1:4], banks[4:6], banks[6:8]
        r = Router(nc, ctx, "rer", x, x_loaded, ident, ident_bf, minus_half, E, K, w["router"], w["b_router"], banks[0])
        norm_out = Norm(sb, sem, "norm_out", minus_half, x_loaded)
        selectors = sb("selectors", [P, E * P], BF16)
        b2_rest = sb("b2_rest", [P, C])
        b2_parts = sb("b2_parts", [P, 3, C], BF16)
        hidden = sb("hidden", [P, HIDDEN, TOK])
        weighed = sb("weighed", [P, HIDDEN, TOK])
        yn = sb("yn", [P, TILES, C])

        filled = sem("filled")
        b2_split = sem("b2_split")
        selectors_done = sem("selectors_done")
        first_product = sem("first_product")
        coef_spread = sem("coef_spread")
        hidden_done = sem("hidden_done")
        weighed_done = sem("weighed_done")
        summed = sem("summed")
        yn_done = sem("yn_done")
        x_added = sem("x_added")

        with nc.Block() as block:

            @block.gpsimd
            def _(pool):
                fill_selectors(pool, selectors, E, P, selectors_done)

                def add(b):
                    pool.wait_ge(yn_done, 4 * b + 4)
                    xs = x[:, bass.ds(4 * b, TILES), :]
                    pool.tensor_tensor(xs, xs, yn[:, :, :], ALU.add).then_inc(x_added, 1)

                def body(b, last=False):
                    if not last:
                        r.norm.take_power(pool, b + 1)
                    norm_out.take_power(pool, b)
                    add(b)

                r.norm.take_power(pool, 0)
                with pool.Fori(0, SEQS - 1) as b:
                    body(b)
                body(SEQS - 1, last=True)

            @block.scalar
            def _(act):
                def relu(b, i, first):
                    n = b * STEPS + i
                    act.wait_ge(first_product, n + 1)
                    if not first or i >= HIDDEN:
                        act.wait_ge(summed, n + 1 - HIDDEN)
                    act.activation(hidden[:, i % HIDDEN, :], hidden_bank[i % HIDDEN][:, :], ACT.Relu,
                                   bias=w["b1"][:, i:i + 1]).then_inc(hidden_done, 1)

                def body(b, p, first=False, last=False):
                    for i in range(STEPS):
                        relu(b, i, first)
                        if not last:
                            if i == 2:
                                r.move_xT(act, b + 1, 1 - p)
                            if i == 5:
                                r.exponents(act, b + 1)
                            if i == 12:
                                r.move_coef(act, b + 1, 1 - p)

                act.wait_ge(filled, 3)
                act.wait_ge(weights_loaded, weights_count)
                r.move_xT(act, 0, 0)
                r.exponents(act, 0)
                r.move_coef(act, 0, 0)
                body(0, 0, first=True)
                with act.Fori(0, (SEQS - 2) // 2) as pair:
                    b = 2 * pair + 1
                    body(b, 1)
                    body(b + 1, 0)
                body(SEQS - 1, 1, last=True)

            @block.tensor
            def _(pe):
                def expert(b, p, i, first):
                    n = b * STEPS + i
                    if not first or i >= HIDDEN:
                        pe.wait_ge(hidden_done, n + 1 - HIDDEN)
                    pe.matmul(hidden_bank[i % HIDDEN][:, :], w["w1"][:, i, :], r.xnT[p][:, :],
                              start=True, stop=True).then_inc(first_product, 1)
                    if i >= 1:
                        m = b * E + i - 1
                        if i == 1:
                            pe.wait_ge(r.coefT_done, b + 1)
                        if not first or i >= 3:
                            pe.wait_ge(weighed_done, m - 1)
                        pe.matmul(coef_bank[i % 2][:, :], selectors[:, (i - 1) * P:i * P], r.coefT[p][:, :],
                                  start=True, stop=True).then_inc(coef_spread, 1)

                def biases(b, p, first, second):
                    pe.wait_ge(r.coefT_done, b + 1)
                    if not first and not second:
                        pe.wait_ge(yn_done, 4 * b - 4)
                    for t in range(TILES):
                        for i in range(3):
                            pe.matmul(out_bank[p][:, t * P:(t + 1) * P], r.coefT[p][:, t * P:(t + 1) * P],
                                      b2_parts[:, i, :], start=(t == 0 and i == 0), stop=False,
                                      skip_group_check=True)

                def second_product(b, p, i, first):
                    if i == 0:
                        pe.wait_ge(hidden_done, b * STEPS + 1)
                    else:
                        pe.wait_ge(weighed_done, b * E + i)
                    h = hidden if i == 0 else weighed
                    for t in range(TILES):
                        mm = pe.matmul(out_bank[p][:, t * P:(t + 1) * P], h[:, i % HIDDEN, t * P:(t + 1) * P],
                                       w["w2"][:, i, :], start=False, stop=(i == STEPS - 1),
                                       skip_group_check=True)
                    mm.then_inc(summed, 1)

                def body(b, p, first=False, last=False, second=False):
                    for i in range(STEPS + 1):
                        if i < STEPS:
                            expert(b, p, i, first)
                        if i == 1:
                            biases(b, p, first, second)
                        if i >= 1:
                            second_product(b, p, i - 1, first)
                        if not last:
                            if i == 2:
                                r.move_x(pe, b + 1)
                            if i == 4:
                                r.take_logits(pe, b + 1, 1 - p)
                            if i == 12:
                                r.move_parts(pe, b + 1)

                pe.wait_ge(weights_loaded, weights_count)
                pe.wait_ge(selectors_done, 4)
                pe.wait_ge(b2_split, 5)
                r.move_x(pe, 0, first=True)
                r.take_logits(pe, 0, 0)
                r.move_parts(pe, 0)
                body(0, 0, first=True)
                body(1, 1, second=True)
                with pe.Fori(0, (SEQS - 4) // 2) as pair:
                    b = 2 * pair + 2
                    body(b, 0)
                    body(b + 1, 1)
                body(SEQS - 2, 0)
                body(SEQS - 1, 1, last=True)

            @block.vector
            def _(dve):
                def weigh(b, i, first):
                    n, m = b * STEPS + i, b * E + i - 1
                    dve.wait_ge(hidden_done, n + 1)
                    dve.wait_ge(coef_spread, m + 1)
                    if not first or i >= HIDDEN + 1:
                        dve.wait_ge(summed, n + 1 - HIDDEN)
                    dve.tensor_tensor(weighed[:, i % HIDDEN, :], hidden[:, i % HIDDEN, :],
                                      coef_bank[i % 2][:, :], ALU.mult).then_inc(weighed_done, 1)

                def out_tile(o):
                    return lambda t: out_bank[o][:, t * P:(t + 1) * P]

                def finish(b, p, first):
                    dve.wait_ge(summed, STEPS * b + STEPS)
                    norm_out.take_moments(dve, b, out_tile(p))
                    if not first:
                        dve.wait_ge(x_added, b)
                    norm_out.apply(dve, b, lambda t: yn[:, t, :], out_tile(p), yn_done)

                def body(b, p, first=False, last=False):
                    for i in range(1, STEPS):
                        weigh(b, i, first)
                        if not last:
                            if i == 1:
                                r.take_moments(dve, b + 1)
                            if i == 2:
                                r.normalize(dve, b + 1)
                            if i == 5:
                                r.shift(dve, b + 1)
                            if i == 7:
                                r.choose(dve, b + 1)
                    finish(b, p, first)

                r.fill(dve, filled)
                dve.wait_ge(filled, 2)
                for coefT in r.coefT:
                    last = dve.memset(coefT[ONES:ONES + 1, :], 1.0)
                last.then_inc(filled, 1)
                dve.wait_ge(weights_loaded, weights_count)
                dve.tensor_copy(b2_parts[:, 0, :], w["b2_rows"][:, :]).then_inc(b2_split, 1)
                dve.wait_ge(b2_split, 1)
                dve.tensor_tensor(b2_rest[:, :], w["b2_rows"][:, :], b2_parts[:, 0, :], ALU.subtract)\
                   .then_inc(b2_split, 1)
                dve.wait_ge(b2_split, 2)
                dve.tensor_copy(b2_parts[:, 1, :], b2_rest[:, :]).then_inc(b2_split, 1)
                dve.wait_ge(b2_split, 3)
                dve.tensor_tensor(b2_parts[:, 2, :], b2_rest[:, :], b2_parts[:, 1, :], ALU.subtract)\
                   .then_inc(b2_split, 2)
                r.take_moments(dve, 0)
                r.normalize(dve, 0, first=True)
                r.shift(dve, 0)
                r.choose(dve, 0)
                body(0, 0, first=True)
                with dve.Fori(0, (SEQS - 2) // 2) as pair:
                    b = 2 * pair + 1
                    body(b, 1)
                    body(b + 1, 0)
                body(SEQS - 1, 1, last=True)


def rwkv_layer(nc, x, x_loaded, ident, minus_half, w, weights_loaded, weights_count):
    F = 512
    FCH = F // P
    START = -1e38

    with ExitStack() as ctx:
        def sb(name, shape, dt=FP32):
            return ctx.enter_context(nc.sbuf_tensor("rk_" + name, shape, dt))

        def sem(name):
            return ctx.enter_context(nc.semaphore("rk_" + name))

        banks = [ctx.enter_context(nc.psum_tensor(f"rk_bank{i}", [P, TOK], FP32)) for i in range(8)]
        xT_bank, k_bank, v_bank, r_bank, x1_bank = banks[0:5]
        f_bank, kv_bank = banks[5:7], banks[7]
        norm_x = Norm(sb, sem, "norm_x", minus_half, x_loaded)
        norm_1 = Norm(sb, sem, "norm_1", minus_half, x_loaded)
        norm_3 = Norm(sb, sem, "norm_3", minus_half, x_loaded)
        xs = sb("xs", [P, TILES, C])
        var_2 = sb("var_2", [P, TILES])
        rstd_2 = sb("rstd_2", [P, TILES])
        xhat = sb("xhat", [P, TILES, C])
        xnT = sb("xnT", [C, 1 + TOK])
        step = sb("step", [C, TOK])
        xk = sb("xk", [C, TOK])
        xv = sb("xv", [C, TOK])
        xr = sb("xr", [C, TOK])
        tanh_r = sb("tanh_r", [C, TOK])
        decay = sb("decay", [C, 1])
        exp_decay = sb("exp_decay", [C, 1])
        top = sb("top", [C, 1 + TOK])
        numer = sb("numer", [C, 1 + TOK])
        denom = sb("denom", [C, 1 + TOK])
        now_max = sb("now_max", [C, TOK])
        args = sb("args", [C, 4, TOK])
        exps = sb("exps", [C, 4, TOK])
        enter_v = sb("enter_v", [C, TOK])
        now_v = sb("now_v", [C, TOK])
        past_v = sb("past_v", [C, TOK])
        past_1 = sb("past_1", [C, TOK])
        sum_v = sb("sum_v", [C, TOK])
        sum_1 = sb("sum_1", [C, TOK])
        sum_inv = sb("sum_inv", [C, TOK])
        wkv = sb("wkv", [C, TOK])
        gated = sb("gated", [C, TOK])
        x1 = sb("x1", [P, TILES, C])
        xhat2 = sb("xhat2", [P, TILES, C])
        xn2T = sb("xn2T", [C, 1 + TOK])
        step2 = sb("step2", [C, TOK])
        xk2 = sb("xk2", [C, TOK])
        xr2 = sb("xr2", [C, TOK])
        relu = sb("relu", [P, FCH, TOK])
        square = sb("square", [P, FCH, TOK])
        tanh_g = sb("tanh_g", [P, TOK])
        kv_gated = sb("kv_gated", [P, TOK])
        out3 = sb("out3", [P, TILES, C])
        yn = sb("yn", [P, TILES, C])

        filled = sem("filled")
        decay_done = sem("decay_done")
        xs_done = sem("xs_done")
        var_2_done = sem("var_2_done")
        rstd_2_done = sem("rstd_2_done")
        xhat_done = sem("xhat_done")
        xT_moved = sem("xT_moved")
        xnT_done = sem("xnT_done")
        step_done = sem("step_done")
        mixed = sem("mixed")
        kvr_done = sem("kvr_done")
        tanh_done = sem("tanh_done")
        top_done = sem("top_done")
        args_done = sem("args_done")
        exps_done = sem("exps_done")
        scans = sem("scans")
        now_v_done = sem("now_v_done")
        past_done = sem("past_done")
        sums_done = sem("sums_done")
        gated_done = sem("gated_done")
        x1_projected = sem("x1_projected")
        x1_done = sem("x1_done")
        xhat2_done = sem("xhat2_done")
        x2T_moved = sem("x2T_moved")
        xn2T_done = sem("xn2T_done")
        step2_done = sem("step2_done")
        mixed2 = sem("mixed2")
        f_done = sem("f_done")
        relu_done = sem("relu_done")
        square_done = sem("square_done")
        gate_projected = sem("gate_projected")
        kv_done = sem("kv_done")
        tanh_g_done = sem("tanh_g_done")
        kv_gated_done = sem("kv_gated_done")
        out3_done = sem("out3_done")
        yn_done = sem("yn_done")
        x_added = sem("x_added")

        def tiles(ap):
            return ap.rearrange("p (t c) -> p t c", t=TILES)

        def x_tile(b):
            return lambda t: x[:, bass.ds(4 * b + t, 1), :].rearrange("p a c -> p (a c)")

        with nc.Block() as block:

            @block.gpsimd
            def _(pool):
                def second_power(b):
                    pool.wait_ge(var_2_done, 3 * b + 3)
                    pool.tensor_tensor(rstd_2[:, :], var_2[:, :], minus_half[:, :], ALU.pow)\
                        .then_inc(rstd_2_done, 1)

                def past(b):
                    pool.wait_ge(exps_done, 4 * b + 3)
                    pool.wait_ge(scans, 3 * b + 2)
                    pool.tensor_tensor(past_v[:, :], exps[:, 2, :], numer[:, 0:TOK], ALU.mult)\
                        .then_inc(past_done, 1)
                    pool.wait_ge(scans, 3 * b + 3)
                    pool.tensor_tensor(past_1[:, :], exps[:, 2, :], denom[:, 0:TOK], ALU.mult)\
                        .then_inc(past_done, 1)

                def add(b):
                    pool.wait_ge(yn_done, 4 * b + 4)
                    xs_ = x[:, bass.ds(4 * b, TILES), :]
                    pool.tensor_tensor(xs_, xs_, yn[:, :, :], ALU.add).then_inc(x_added, 1)

                def front(b):
                    norm_x.take_power(pool, b)
                    second_power(b)

                def body(b, last=False):
                    if not last:
                        norm_x.take_power(pool, b + 1)
                    norm_1.take_power(pool, b)
                    if not last:
                        second_power(b + 1)
                    norm_3.take_power(pool, b)
                    if not last:
                        past(b + 1)
                    add(b)

                front(0)
                past(0)
                with pool.Fori(0, SEQS - 1) as b:
                    body(b)
                body(SEQS - 1, last=True)

            @block.scalar
            def _(act):
                def move_xT(b):
                    act.wait_ge(xT_moved, b + 1)
                    act.activation(xnT[:, 1:1 + TOK], xT_bank[:, :], ACT.Identity, scale=w["g1"][:, :],
                                   bias=w["b1"][:, :]).then_inc(xnT_done, 1)

                def gate_r(b):
                    act.wait_ge(kvr_done, 3 * b + 1)
                    act.activation(tanh_r[:, :], r_bank[:, :], ACT.Tanh, scale=0.5).then_inc(tanh_done, 1)

                def exponents(b):
                    for n in range(4):
                        act.wait_ge(args_done, 5 * b + 2 + n)
                        act.activation(exps[:, n, :], args[:, n, :], ACT.Exp).then_inc(exps_done, 1)

                def move_x2T(b):
                    act.wait_ge(x2T_moved, b + 1)
                    act.activation(xn2T[:, 1:1 + TOK], x1_bank[:, :], ACT.Identity, scale=w["g2"][:, :],
                                   bias=w["b2"][:, :]).then_inc(xn2T_done, 1)

                def squares(b):
                    for f in range(FCH):
                        n = b * FCH + f
                        act.wait_ge(f_done, n + 1)
                        act.activation(relu[:, f, :], f_bank[f % 2][:, :], ACT.Relu).then_inc(relu_done, 1)
                        act.wait_ge(relu_done, n + 1)
                        act.activation(square[:, f, :], relu[:, f, :], ACT.Square).then_inc(square_done, 1)

                def gate_g(b):
                    act.wait_ge(gate_projected, b + 1)
                    act.activation(tanh_g[:, :], x1_bank[:, :], ACT.Tanh, scale=0.5).then_inc(tanh_g_done, 1)

                def body(b, last=False):
                    if not last:
                        move_xT(b + 1)
                    move_x2T(b)
                    if not last:
                        gate_r(b + 1)
                    gate_g(b)
                    squares(b)
                    if not last:
                        exponents(b + 1)

                act.wait_ge(weights_loaded, weights_count)
                act.activation(exp_decay[:, :], w["decay"][:, :], ACT.Exp).then_inc(decay_done, 1)
                move_xT(0)
                gate_r(0)
                exponents(0)
                with act.Fori(0, SEQS - 1) as b:
                    body(b)
                body(SEQS - 1, last=True)

            @block.tensor
            def _(pe):
                def move_x(b):
                    pe.wait_ge(xhat_done, b + 1)
                    for t in range(TILES):
                        mm = pe.transpose(xT_bank[:, t * P:(t + 1) * P], xhat[:, t, :], ident[:, :])
                    mm.then_inc(xT_moved, 1)

                def project_kvr(b):
                    for n, (name, bank, src) in enumerate((("wr", r_bank, xr), ("wk", k_bank, xk), ("wv", v_bank, xv))):
                        pe.wait_ge(mixed, 3 * b + n + 1)
                        pe.matmul(bank[:, :], w[name][:, :], src[:, :], start=True, stop=True)\
                          .then_inc(kvr_done, 1)

                def project_x1(b):
                    pe.wait_ge(gated_done, b + 1)
                    for t in range(TILES):
                        mm = pe.matmul(x1_bank[:, t * P:(t + 1) * P], gated[:, t * P:(t + 1) * P],
                                       w["wo"][:, :], start=True, stop=True)
                    mm.then_inc(x1_projected, 1)

                def move_x1(b):
                    for t in range(TILES):
                        pe.wait_ge(xhat2_done, 4 * b + t + 1)
                        mm = pe.transpose(x1_bank[:, t * P:(t + 1) * P], xhat2[:, t, :], ident[:, :])
                    mm.then_inc(x2T_moved, 1)

                def ffn(b):
                    pe.wait_ge(mixed2, 2 * b + 1)
                    for t in range(TILES):
                        mm = pe.matmul(x1_bank[:, t * P:(t + 1) * P], xr2[:, t * P:(t + 1) * P],
                                       w["wr_ffn"][:, :], start=True, stop=True)
                    mm.then_inc(gate_projected, 1)
                    pe.wait_ge(mixed2, 2 * b + 2)
                    for f in range(FCH + 1):
                        if f < FCH:
                            if f >= 2:
                                pe.wait_ge(relu_done, b * FCH + f - 1)
                            pe.matmul(f_bank[f % 2][:, :], w["wk_ffn"][:, f * P:(f + 1) * P], xk2[:, :],
                                      start=True, stop=True).then_inc(f_done, 1)
                        if f >= 1:
                            pe.wait_ge(square_done, b * FCH + f)
                            for t in range(TILES):
                                mm = pe.matmul(kv_bank[:, t * P:(t + 1) * P],
                                               square[:, f - 1, t * P:(t + 1) * P], w["wv_ffn"][:, f - 1, :],
                                               start=(f == 1 and t == 0), stop=(f == FCH),
                                               skip_group_check=True)
                    mm.then_inc(kv_done, 1)

                def body(b, last=False):
                    project_x1(b)
                    if not last:
                        move_x(b + 1)
                    move_x1(b)
                    if not last:
                        project_kvr(b + 1)
                    ffn(b)

                pe.wait_ge(weights_loaded, weights_count)
                move_x(0)
                project_kvr(0)
                with pe.Fori(0, SEQS - 1) as b:
                    body(b)
                body(SEQS - 1, last=True)

            @block.vector
            def _(dve):
                def second_variance(b):
                    dve.wait_ge(norm_x.rstd_done, b + 1)
                    dve.tensor_tensor(var_2[:, :], norm_x.rstd[:, :], norm_x.rstd[:, :], ALU.mult)\
                       .then_inc(var_2_done, 1)
                    dve.wait_ge(var_2_done, 3 * b + 1)
                    dve.tensor_tensor(var_2[:, :], var_2[:, :], norm_x.moments[:, :, 1], ALU.mult)\
                       .then_inc(var_2_done, 1)
                    dve.wait_ge(var_2_done, 3 * b + 2)
                    dve.tensor_scalar(var_2[:, :], var_2[:, :], EPS, None, ALU.add).then_inc(var_2_done, 1)

                def scale_xs(b):
                    dve.wait_ge(rstd_2_done, b + 1)
                    dve.wait_ge(xs_done, 4 * b + 4)
                    dve.tensor_tensor(xhat[:, :, :], xs[:, :, :],
                                      rstd_2[:, :].rearrange("p (t a) -> p t a", a=1).to_broadcast([P, TILES, C]),
                                      ALU.mult).then_inc(xhat_done, 1)

                def mix(b):
                    dve.wait_ge(xnT_done, b + 1)
                    dve.tensor_tensor(step[:, :], xnT[:, 1:1 + TOK], xnT[:, 0:TOK], ALU.subtract)\
                       .then_inc(step_done, 1)
                    dve.wait_ge(step_done, b + 1)
                    for out, name in ((xr, "mix_r"), (xk, "mix_k"), (xv, "mix_v")):
                        dve.scalar_tensor_tensor(out=out[:, :], in0=step[:, :], scalar=w[name][:, :],
                                                 in1=xnT[:, 0:TOK], op0=ALU.mult, op1=ALU.add)\
                           .then_inc(mixed, 1)

                def recurrence_args(b):
                    k, u = k_bank, w["first"][:, :]
                    dve.wait_ge(kvr_done, 3 * b + 2)
                    dve.tensor_tensor_scan(top[:, 1:1 + TOK], decay[:, :].to_broadcast([C, TOK]), k[:, :],
                                           START, ALU.add, ALU.max).then_inc(top_done, 1)
                    dve.wait_ge(top_done, b + 1)
                    dve.scalar_tensor_tensor(out=now_max[:, :], in0=k[:, :], scalar=u, in1=top[:, 0:TOK],
                                             op0=ALU.add, op1=ALU.max).then_inc(args_done, 1)
                    dve.scalar_tensor_tensor(out=args[:, 0, :], in0=top[:, 0:TOK], scalar=decay[:, :],
                                             in1=top[:, 1:1 + TOK], op0=ALU.add, op1=ALU.subtract)\
                       .then_inc(args_done, 1)
                    dve.tensor_tensor(args[:, 1, :], k[:, :], top[:, 1:1 + TOK], ALU.subtract)\
                       .then_inc(args_done, 1)
                    dve.wait_ge(args_done, 5 * b + 1)
                    dve.tensor_tensor(args[:, 2, :], top[:, 0:TOK], now_max[:, :], ALU.subtract)\
                       .then_inc(args_done, 1)
                    dve.scalar_tensor_tensor(out=args[:, 3, :], in0=k[:, :], scalar=u, in1=now_max[:, :],
                                             op0=ALU.add, op1=ALU.subtract).then_inc(args_done, 1)

                def recurrence(b):
                    dve.wait_ge(exps_done, 4 * b + 2)
                    dve.wait_ge(kvr_done, 3 * b + 3)
                    dve.tensor_tensor(enter_v[:, :], exps[:, 1, :], v_bank[:, :], ALU.mult).then_inc(scans, 1)
                    dve.wait_ge(scans, 3 * b + 1)
                    dve.tensor_tensor_scan(numer[:, 1:1 + TOK], exps[:, 0, :], enter_v[:, :], 0.0,
                                           ALU.mult, ALU.add).then_inc(scans, 1)
                    dve.tensor_tensor_scan(denom[:, 1:1 + TOK], exps[:, 0, :], exps[:, 1, :], 0.0,
                                           ALU.mult, ALU.add).then_inc(scans, 1)
                    dve.wait_ge(exps_done, 4 * b + 4)
                    dve.tensor_tensor(now_v[:, :], exps[:, 3, :], v_bank[:, :], ALU.mult).then_inc(now_v_done, 1)

                def output(b, first=False):
                    dve.wait_ge(past_done, 2 * b + 2)
                    dve.tensor_tensor(sum_1[:, :], past_1[:, :], exps[:, 3, :], ALU.add).then_inc(sums_done, 1)
                    dve.wait_ge(now_v_done, b + 1)
                    dve.tensor_tensor(sum_v[:, :], past_v[:, :], now_v[:, :], ALU.add).then_inc(sums_done, 1)
                    dve.wait_ge(sums_done, 4 * b + 1)
                    dve.reciprocal(sum_inv[:, :], sum_1[:, :]).then_inc(sums_done, 1)
                    dve.wait_ge(sums_done, 4 * b + 3)
                    dve.tensor_tensor(wkv[:, :], sum_v[:, :], sum_inv[:, :], ALU.mult).then_inc(sums_done, 1)
                    dve.wait_ge(sums_done, 4 * b + 4)
                    dve.wait_ge(tanh_done, b + 1)
                    dve.scalar_tensor_tensor(out=gated[:, :], in0=tanh_r[:, :], scalar=1.0, in1=wkv[:, :],
                                             op0=ALU.add, op1=ALU.mult).then_inc(gated_done, 1)

                def add_x1(b):
                    dve.wait_ge(x1_projected, b + 1)
                    dve.scalar_tensor_tensor(out=x1[:, :, :], in0=tiles(x1_bank[:, :]), scalar=0.5,
                                             in1=xs[:, :, :], op0=ALU.mult, op1=ALU.add).then_inc(x1_done, 1)

                def mix2(b):
                    dve.wait_ge(xn2T_done, b + 1)
                    dve.tensor_tensor(step2[:, :], xn2T[:, 1:1 + TOK], xn2T[:, 0:TOK], ALU.subtract)\
                       .then_inc(step2_done, 1)
                    dve.wait_ge(step2_done, b + 1)
                    for out, name in ((xr2, "ffn_mix_r"), (xk2, "ffn_mix_k")):
                        dve.scalar_tensor_tensor(out=out[:, :], in0=step2[:, :], scalar=w[name][:, :],
                                                 in1=xn2T[:, 0:TOK], op0=ALU.mult, op1=ALU.add)\
                           .then_inc(mixed2, 1)

                def add_ffn(b):
                    dve.wait_ge(kv_done, b + 1)
                    dve.wait_ge(tanh_g_done, b + 1)
                    dve.scalar_tensor_tensor(out=kv_gated[:, :], in0=tanh_g[:, :], scalar=1.0, in1=kv_bank[:, :],
                                             op0=ALU.add, op1=ALU.mult).then_inc(kv_gated_done, 1)
                    dve.wait_ge(kv_gated_done, b + 1)
                    dve.scalar_tensor_tensor(out=out3[:, :, :], in0=tiles(kv_gated[:, :]), scalar=0.5,
                                             in1=x1[:, :, :], op0=ALU.mult, op1=ALU.add).then_inc(out3_done, 1)

                def body(b, first=False, last=False):
                    if not last:
                        norm_x.take_moments(dve, b + 1, x_tile(b + 1))
                    add_x1(b)
                    dve.wait_ge(x1_done, b + 1)
                    norm_1.take_moments(dve, b, lambda t: x1[:, t, :])
                    if not last:
                        second_variance(b + 1)
                        norm_x.apply(dve, b + 1, lambda t: xs[:, t, :], x_tile(b + 1), xs_done)
                    norm_1.apply(dve, b, lambda t: xhat2[:, t, :], lambda t: x1[:, t, :], xhat2_done)
                    if not last:
                        scale_xs(b + 1)
                    mix2(b)
                    if not last:
                        mix(b + 1)
                        recurrence_args(b + 1)
                    add_ffn(b)
                    dve.wait_ge(out3_done, b + 1)
                    norm_3.take_moments(dve, b, lambda t: out3[:, t, :])
                    if not last:
                        recurrence(b + 1)
                    if not first:
                        dve.wait_ge(x_added, b)
                    norm_3.apply(dve, b, lambda t: yn[:, t, :], lambda t: out3[:, t, :], yn_done)
                    if not last:
                        output(b + 1)

                for col, value in ((xnT, 0.0), (xn2T, 0.0), (top, START), (numer, 0.0), (denom, 0.0)):
                    dve.memset(col[:, 0:1], value).then_inc(filled, 1)
                dve.wait_ge(filled, 5)
                dve.wait_ge(decay_done, 1)
                dve.tensor_scalar(decay[:, :], exp_decay[:, :], -1.0, None, ALU.mult).then_inc(decay_done, 1)
                norm_x.take_moments(dve, 0, x_tile(0))
                second_variance(0)
                norm_x.apply(dve, 0, lambda t: xs[:, t, :], x_tile(0), xs_done)
                scale_xs(0)
                mix(0)
                dve.wait_ge(decay_done, 2)
                recurrence_args(0)
                recurrence(0)
                output(0)
                body(0, first=True)
                with dve.Fori(1, SEQS - 1) as b:
                    body(b)
                body(SEQS - 1, last=True)


INPUTS = ['L0_attn_x', 'L0_attn_W_qkv', 'L0_attn_W_proj', 'L0_attn_b_proj', 'L0_ffn_router', 'L0_ffn_experts_gate',
          'L0_ffn_experts_up', 'L0_ffn_experts_down', 'L0_ffn_shared_gate', 'L0_ffn_shared_up', 'L0_ffn_shared_down',
          'L1_attn_ln1_g', 'L1_attn_ln1_b', 'L1_attn_ln2_g', 'L1_attn_ln2_b', 'L1_attn_att_mix_k', 'L1_attn_att_mix_v',
          'L1_attn_att_mix_r', 'L1_attn_time_decay', 'L1_attn_time_first', 'L1_attn_Wk', 'L1_attn_Wv', 'L1_attn_Wr',
          'L1_attn_Wo', 'L1_attn_ffn_mix_k', 'L1_attn_ffn_mix_r', 'L1_attn_Wk_ffn', 'L1_attn_Wr_ffn', 'L1_attn_Wv_ffn',
          'L1_ffn_router_W', 'L1_ffn_router_b', 'L1_ffn_sW1', 'L1_ffn_sb1', 'L1_ffn_sW2', 'L1_ffn_sb2', 'L1_ffn_eW1',
          'L1_ffn_eb1', 'L1_ffn_eW2', 'L1_ffn_eb2']


def sandwich_kernel(nc, a, out):
    E0, D0, E1 = 8, 64, 15

    with ExitStack() as ctx:
        def sb(name, shape, dt=FP32):
            return ctx.enter_context(nc.sbuf_tensor(name, shape, dt))

        def sem(name):
            return ctx.enter_context(nc.semaphore(name))

        x = sb("x_tokens", [P, SEQS * TILES, C])
        ident = sb("ident", [P, P])
        ident_bf = sb("ident_bf", [P, P], BF16)
        minus_half = sb("minus_half", [P, TILES])
        x_loaded = sem("x_loaded")
        constants = sem("constants")
        x_stored = sem("x_stored")
        weights_0a, weights_0f, weights_1a, weights_1f = (sem("weights_" + n) for n in ("0a", "0f", "1a", "1f"))
        x_view = a['L0_attn_x'].rearrange("b (t p) c -> p (b t) c", p=P)
        out_view = out.rearrange("b (t p) c -> p (b t) c", p=P)

        def row(v):
            return v.rearrange("(a c) -> a c", a=1)

        def column(v):
            return v.rearrange("(c a) -> c a", a=1)

        def load(queue, items, done):
            for dst, src in items:
                queue.dma_start(dst, src).then_inc(done, 16)
            return 16 * len(items)

        w_qkv, w_proj, b_proj = sb("w_qkv", [C, 3 * C]), sb("w_proj", [C, C]), sb("b_proj", [P, C])
        w0 = {"router": sb("router0", [C, E0]), "gate": sb("gate0", [C, E0 * D0]), "up": sb("up0", [C, E0 * D0]),
              "down": sb("down0", [P, E0 * D0 // P, C]), "shared_gate": sb("shared_gate", [C, P]),
              "shared_up": sb("shared_up", [C, P]), "shared_down": sb("shared_down", [P, C])}
        columns = ("g1", "b1", "g2", "b2", "mix_k", "mix_v", "mix_r", "decay", "first", "ffn_mix_k", "ffn_mix_r")
        w1 = {n: sb("rwkv_" + n, [C, 1]) for n in columns}
        w1.update({n: sb("rwkv_" + n, [C, C]) for n in ("wk", "wv", "wr", "wo", "wr_ffn")})
        w1["wk_ffn"] = sb("rwkv_wk_ffn", [C, 4 * C])
        w1["wv_ffn"] = sb("rwkv_wv_ffn", [P, 4, C])
        w2 = {"router": sb("router1", [C, E1]), "b_router": sb("b_router", [P, E1]), "w1": sb("w1", [C, E1 + 1, P]),
              "b1": sb("b1", [P, E1 + 1]), "w2": sb("w2", [P, E1 + 1, C]), "b2_rows": sb("b2_rows", [P, C])}

        items_0a = [(w_qkv[:, :], a['L0_attn_W_qkv']), (w_proj[:, :], a['L0_attn_W_proj']),
                    (b_proj[:, :], row(a['L0_attn_b_proj']).to_broadcast([P, C]))]
        items_0f = [(w0["router"][:, :], a['L0_ffn_router']),
                    (w0["gate"][:, :].rearrange("h (e d) -> h e d", d=D0), a['L0_ffn_experts_gate'].rearrange("e h d -> h e d")),
                    (w0["up"][:, :].rearrange("h (e d) -> h e d", d=D0), a['L0_ffn_experts_up'].rearrange("e h d -> h e d")),
                    (w0["down"][:, :, :], a['L0_ffn_experts_down'].rearrange("(q e) d h -> (e d) q h", e=2)),
                    (w0["shared_gate"][:, :], a['L0_ffn_shared_gate']), (w0["shared_up"][:, :], a['L0_ffn_shared_up']),
                    (w0["shared_down"][:, :], a['L0_ffn_shared_down'])]
        vectors = dict(g1='ln1_g', b1='ln1_b', g2='ln2_g', b2='ln2_b', decay='time_decay', first='time_first')
        mixes = dict(mix_k='att_mix_k', mix_v='att_mix_v', mix_r='att_mix_r', ffn_mix_k='ffn_mix_k', ffn_mix_r='ffn_mix_r')
        matrices = dict(wk='Wk', wv='Wv', wr='Wr', wo='Wo', wr_ffn='Wr_ffn', wk_ffn='Wk_ffn')
        items_1a = [(w1[n][:, :], column(a['L1_attn_' + v])) for n, v in vectors.items()]
        items_1a += [(w1[n][:, :], a['L1_attn_' + v].rearrange("a b c -> c (a b)")) for n, v in mixes.items()]
        items_1a += [(w1[n][:, :], a['L1_attn_' + v]) for n, v in matrices.items()]
        items_1a += [(w1["wv_ffn"][:, :, :], a['L1_attn_Wv_ffn'].rearrange("(f p) c -> p f c", p=P))]
        items_1f = [(w2["router"][:, :], a['L1_ffn_router_W']),
                    (w2["b_router"][:, :], row(a['L1_ffn_router_b']).to_broadcast([P, E1])),
                    (w2["w1"][:, 1:, :], a['L1_ffn_eW1'].rearrange("e d h -> d e h")),
                    (w2["w1"][:, 0, :], a['L1_ffn_sW1']),
                    (w2["w2"][:, 1:, :], a['L1_ffn_eW2'].rearrange("e h d -> h e d")),
                    (w2["w2"][:, 0, :], a['L1_ffn_sW2']),
                    (w2["b1"][:, 1:], a['L1_ffn_eb1']), (w2["b1"][:, 0:1], column(a['L1_ffn_sb1'])),
                    (w2["b2_rows"][96:97, :], row(a['L1_ffn_sb2']))]
        items_1f += [(w2["b2_rows"][i * E1:(i + 1) * E1, :], a['L1_ffn_eb2']) for i in range(3)]

        with nc.Block() as block:
            @block.sync
            def _(sp):
                sp.dma_start(x[:, 0:TILES, :], x_view[:, 0:TILES, :]).then_inc(x_loaded, 16)
                load(sp, items_0a, weights_0a)
                sp.dma_start(x[:, TILES:, :], x_view[:, TILES:, :]).then_inc(x_loaded, 16)
                load(sp, items_0f, weights_0f)
                sp.wait_ge(constants, 6)
                load(sp, items_1f, weights_1f)

            @block.scalar
            def _(act):
                load(act, items_1a, weights_1a)

            @block.gpsimd
            def _(pool):
                pool.memset(minus_half[:, :], -0.5).then_inc(constants, 1)
                pool.memset(ident[:, :], 0.0).then_inc(constants, 1)
                pool.memset(ident_bf[:, :], 0.0).then_inc(constants, 1)
                pool.wait_ge(constants, 3)
                for m in (ident, ident_bf):
                    pool.affine_select(out=m[:, :], in_=m[:, :], compare_op=ALU.not_equal, fill=1.0,
                                       base=0, pattern=[[-1, P]], channel_multiplier=1).then_inc(constants, 1)
                pool.memset(w2["b2_rows"][:, :], 0.0).then_inc(constants, 1)

        attention_layer(nc, x, ident, ident_bf, minus_half, w_qkv, w_proj, b_proj, x_loaded, weights_0a,
                        16 * len(items_0a))
        swiglu_experts_layer(nc, x, x_loaded, ident, ident_bf, minus_half, w0, weights_0f, 16 * len(items_0f))
        rwkv_layer(nc, x, x_loaded, ident, minus_half, w1, weights_1a, 16 * len(items_1a))
        relu_experts_layer(nc, x, x_loaded, ident, ident_bf, minus_half, w2, weights_1f, 16 * len(items_1f))
        with nc.Block() as block:
            @block.sync
            def _(sp):
                sp.dma_start(out_view, x[:, :, :]).then_inc(x_stored, 16)
                sp.wait_ge(x_stored, 16)


def lay_out(inputs):
    HEADS, D = 16, 8
    arrays = {n: np.asarray(inputs[n]) for n in INPUTS}
    w = arrays['L0_attn_W_qkv']
    q, k = (w[:, i * C:(i + 1) * C].reshape(C, HEADS, D).transpose(0, 2, 1).reshape(C, C) for i in range(2))
    arrays['L0_attn_W_qkv'] = np.concatenate([q, k, w[:, 2 * C:]], axis=1)
    for n in ('Wk', 'Wv', 'Wr', 'Wo', 'Wk_ffn', 'Wr_ffn', 'Wv_ffn'):
        arrays['L1_attn_' + n] = arrays['L1_attn_' + n].T
    arrays['L1_ffn_eb1'] = arrays['L1_ffn_eb1'].T
    return {n: np.ascontiguousarray(v) for n, v in arrays.items()}


def kernel(**inputs):
    import concourse.bacc as bacc
    from concourse.bass_utils import run_bass_kernel_spmd

    nc = bacc.Bacc("TRN2", target_bir_lowering=False, num_devices=1)
    arrays = lay_out(inputs)
    a = {n: nc.dram_tensor("in_" + n, v.shape, mybir.dt.from_np(v.dtype), kind="ExternalInput").ap()
         for n, v in arrays.items()}
    out = nc.dram_tensor("out", (SEQS, TOK, C), FP32, kind="ExternalOutput").ap()
    sandwich_kernel(nc, a, out)
    result = run_bass_kernel_spmd(nc, [{"in_" + n: v for n, v in arrays.items()}], core_ids=[0])
    return result.results[0]["out"]
```

```python
import numpy as np
import concourse.bass as bass
from concourse import mybir
from contextlib import ExitStack

FP32 = mybir.dt.float32
BF16 = mybir.dt.bfloat16
ALU = mybir.AluOpType
ACT = mybir.ActivationFunctionType
AX = mybir.AxisListType

P = 128
SEQS = 8
TILES = 4
TOK = TILES * P
C = 128
EPS = 1e-5
X_LOADS = 32
MASKED = -1e30


class Norm:

    def __init__(self, sb, sem, name, minus_half, x_loaded, eps=EPS):
        self.stats = sb(f"{name}_stats", [P, TILES, 6], FP32)
        self.moments = sb(f"{name}_moments", [P, TILES, 2], FP32)
        self.var_eps = sb(f"{name}_var_eps", [P, TILES], FP32)
        self.rstd = sb(f"{name}_rstd", [P, TILES], FP32)
        self.minus_half = minus_half
        self.eps = eps
        self.x_loaded = x_loaded
        self.stats_done = sem(f"{name}_stats_done")
        self.moments_done = sem(f"{name}_moments_done")
        self.var_done = sem(f"{name}_var_done")
        self.rstd_done = sem(f"{name}_rstd_done")

    def take_moments(self, dve, b, tile):
        for t in range(TILES):
            dve.bn_stats(self.stats[:, t, :], tile(t)).then_inc(self.stats_done, 1)
        count = dve.to_reg(b * TILES + TILES)
        dve.wait_ge(self.x_loaded, X_LOADS)
        dve.wait_ge(self.stats_done, count)
        for t in range(TILES):
            dve.bn_aggr(self.moments[:, t, :], self.stats[:, t, :]).then_inc(self.moments_done, 1)
        dve.wait_ge(self.moments_done, b * TILES + TILES)
        dve.tensor_scalar(self.var_eps[:, :], self.moments[:, :, 1], self.eps, None, ALU.add)\
           .then_inc(self.var_done, 1)

    def take_power(self, pool, b):
        pool.wait_ge(self.var_done, b + 1)
        pool.tensor_tensor(self.rstd[:, :], self.var_eps[:, :], self.minus_half[:, :], ALU.pow)\
            .then_inc(self.rstd_done, 1)

    def apply(self, dve, b, out, tile, done):
        dve.wait_ge(self.rstd_done, b + 1)
        for t in range(TILES):
            dve.tensor_scalar(out(t), tile(t), self.moments[:, t, 0:1], self.rstd[:, t:t + 1],
                              ALU.subtract, ALU.mult).then_inc(done, 1)


def attention_layer(nc, x, ident, ident_bf, minus_half, w_qkv, w_proj, b_proj, x_loaded, weights_loaded, weights_count):
    HEADS, D = 16, 8
    GROUP = TOK // P
    GROUPS = HEADS // GROUP
    UNITS = TILES * GROUPS
    SET = HEADS // 2
    TERMS_Q = ((0, 1, 4), (2, 3), (5,))
    TERMS_K = ((0, 2, 5), (1, 3), (4,))
    MAX_ROW = 64
    SCALE = float(D) ** -0.5
    LAG = 2
    HALF = UNITS // 2
    EARLY, LATE = 0, 8
    PROBS = 4

    with ExitStack() as ctx:
        def sb(name, shape, dt):
            return ctx.enter_context(nc.sbuf_tensor("at_" + name, shape, dt))

        def sem(name):
            return ctx.enter_context(nc.semaphore("at_" + name))

        banks = [ctx.enter_context(nc.psum_tensor(f"at_bank{i}", [P, TOK], FP32)) for i in range(8)]
        score_bank, key_bank, out_bank = banks[0:2], banks[2:4], banks[4:6]
        xqv_bank, ky_bank = banks[6:8]

        xn = sb("xn", [P, TILES, C], FP32)
        xnT = sb("xnT", [C, TOK], FP32)
        q_parts = [sb(f"q{i + 1}", [C, TOK], BF16) for i in range(3)]
        k_parts = [sb(f"k{i + 1}", [C, TOK], BF16) for i in range(3)]
        q_rest = sb("q_rest", [C, TOK], FP32)
        k_rest = sb("k_rest", [C, TOK], FP32)
        q_rows = [sb(f"q_rows{i}", [P, HEADS, TOK], BF16) for i in range(2)]
        k_rows = [sb(f"k_rows{i}", [P, HEADS, TOK], BF16) for i in range(2)]
        zero_rows = sb("zero_rows", [3, P], BF16)
        v_wide = [sb(f"v_wide{i}", [P, TILES, HEADS * P], FP32) for i in range(2)]
        probs = sb("probs", [P, PROBS, TOK], FP32)
        sums = sb("sums", [P, P], FP32)
        outT = sb("outT", [C, TOK], FP32)
        neg_max = sb("neg_max", [P, TILES, HEADS], FP32)
        max_rest = sb("max_rest", [P, TILES, HEADS], FP32)
        max_parts = sb("max_parts", [P, TILES, 3, HEADS], BF16)
        max_partsT = sb("max_partsT", [3 * HEADS, TOK], BF16)
        mask = sb("mask", [P, P], BF16)
        y = sb("y", [P, TILES, C], FP32)
        norm_in = Norm(sb, sem, "norm_in", minus_half, x_loaded)
        norm_out = Norm(sb, sem, "norm_out", minus_half, x_loaded)

        filled = sem("filled")
        mask_zeroed = sem("mask_zeroed")
        k_zeroed = sem("k_zeroed")
        v_zeroed = sem("v_zeroed")
        xn_done = sem("xn_done")
        xT_moved = sem("xT_moved")
        xnT_done = sem("xnT_done")
        qk_projected = sem("qk_projected")
        v_projected = sem("v_projected")
        part1_done = sem("part1_done")
        rest_done = sem("rest_done")
        part2_done = sem("part2_done")
        part3_done = sem("part3_done")
        rows_loaded = sem("rows_loaded")
        v_done = sem("v_done")
        scored = sem("scored")
        max_done = sem("max_done")
        max_split = sem("max_split")
        max_moved = sem("max_moved")
        maxT_done = sem("maxT_done")
        max_loaded = sem("max_loaded")
        key_scored = sem("key_scored")
        exp_done = sem("exp_done")
        probs_done = sem("probs_done")
        weighed = sem("weighed")
        sums_done = sem("sums_done")
        inverted = sem("inverted")
        outT_done = sem("outT_done")
        proj_done = sem("proj_done")
        y_done = sem("y_done")
        yn_done = sem("yn_done")
        x_added = sem("x_added")
        FILLS = 1 + 1 + 2 + 2 + 4

        def tile_of(ap, t):
            return ap[:, t * P:(t + 1) * P]

        def own_columns(wide, s, start):
            w = wide[:, :, s * SET * P + start:(s + 1) * SET * P]
            return bass.AP(w.tensor, w.offset, [w.ap[0], w.ap[1], [P + D, SET], [1, D]])

        with nc.Block() as block:

            @block.sync
            def _(sp):
                def send(parts, rows, terms):
                    for r in terms:
                        sp.dma_start(rows[r * D:(r + 1) * D, :, :], parts[:, :]).then_inc(rows_loaded, 16)

                def spread_early(b, p):
                    sp.wait_ge(part1_done, 2 * b + 1)
                    send(q_parts[0], q_rows[p], TERMS_Q[0])
                    sp.dma_start(q_rows[p][MAX_ROW:MAX_ROW + 3, :, :].rearrange("r h (t c) -> r (h t) c", t=TILES),
                                 zero_rows[:, :].rearrange("r (a c) -> r a c", a=1).to_broadcast([3, HEADS * TILES, P]))\
                      .then_inc(rows_loaded, 16)
                    sp.wait_ge(part1_done, 2 * b + 2)
                    send(k_parts[0], k_rows[p], TERMS_K[0])
                    sp.wait_ge(part2_done, 2 * b + 1)
                    send(q_parts[1], q_rows[p], TERMS_Q[1])
                    sp.wait_ge(part2_done, 2 * b + 2)
                    send(k_parts[1], k_rows[p], TERMS_K[1])

                def spread_late(b, p):
                    sp.wait_ge(part3_done, 2 * b + 1)
                    send(q_parts[2], q_rows[p], TERMS_Q[2])
                    sp.wait_ge(part3_done, 2 * b + 2)
                    send(k_parts[2], k_rows[p], TERMS_K[2])

                def send_max(b, p, half):
                    cols = slice(half * TOK // 2, (half + 1) * TOK // 2)
                    sp.wait_ge(maxT_done, 2 * b + half + 1)
                    for i in range(3):
                        sp.dma_start(q_rows[p][MAX_ROW + i:MAX_ROW + i + 1, :, cols],
                                     max_partsT[i * HEADS:(i + 1) * HEADS, cols])\
                          .then_inc(max_loaded, 16)

                def body(b, p, last=False):
                    if not last:
                        spread_early(b + 1, 1 - p)
                    if not last:
                        spread_late(b + 1, 1 - p)
                    send_max(b, p, 1)
                    if not last:
                        send_max(b + 1, 1 - p, 0)

                sp.wait_ge(filled, FILLS)
                spread_early(0, 0)
                spread_late(0, 0)
                send_max(0, 0, 0)
                body(0, 0)
                with sp.Fori(0, (SEQS - 2) // 2) as pair:
                    b = 2 * pair + 1
                    body(b, 1)
                    body(b + 1, 0)
                body(SEQS - 1, 1, last=True)

            @block.gpsimd
            def _(pool):
                pool.memset(zero_rows[:, :], 0.0).then_inc(filled, 1)
                pool.memset(mask[:, :], 0.0).then_inc(mask_zeroed, 1)
                pool.wait_ge(mask_zeroed, 1)
                pool.affine_select(out=mask[:, :], in_=mask[:, :], compare_op=ALU.is_ge, fill=MASKED,
                                   base=0, pattern=[[-1, P]], channel_multiplier=1).then_inc(filled, 1)

                def third_part(b, n):
                    parts, rest = ((q_parts, q_rest), (k_parts, k_rest))[n]
                    pool.wait_ge(part2_done, 2 * b + n + 1)
                    pool.tensor_tensor(parts[2][:, :], rest[:, :], parts[1][:, :], ALU.subtract)\
                        .then_inc(part3_done, 1)

                def mask_probs(b, u):
                    count = pool.to_reg(b * UNITS + u + 1)
                    pool.wait_ge(mask_zeroed, 1)
                    pool.wait_ge(exp_done, count)
                    slot = probs[:, u % PROBS, :]
                    pool.affine_select(out=slot, in_=slot, compare_op=ALU.is_ge, fill=0.0, base=0,
                                       pattern=[[0, GROUP], [1, P]], channel_multiplier=-1)\
                        .then_inc(probs_done, 1)

                def add_y(b):
                    pool.wait_ge(yn_done, 4 * b + 4)
                    xs = x[:, bass.ds(4 * b, TILES), :]
                    pool.tensor_tensor(xs, xs, y[:, :, :], ALU.add).then_inc(x_added, 1)

                def body(b, first=False, last=False, next_last=False):
                    for u in range(UNITS):
                        mask_probs(b, u)
                        if not last and u in (3, 4):
                            third_part(b + 1, u - 3)
                        if not first and u == 7:
                            norm_out.take_power(pool, b - 1)
                        if not first and u == 11:
                            add_y(b - 1)
                        if not last and not next_last and u == 14:
                            norm_in.take_power(pool, b + 2)

                for rows in q_rows:
                    pool.memset(rows[:, :, :].bitcast(FP32), 0.0).then_inc(filled, 1)
                norm_in.take_power(pool, 0)
                third_part(0, 0)
                third_part(0, 1)
                norm_in.take_power(pool, 1)
                body(0, first=True)
                with pool.Fori(1, SEQS - 2) as b:
                    body(b)
                body(SEQS - 2, next_last=True)
                body(SEQS - 1, last=True)
                norm_out.take_power(pool, SEQS - 1)
                add_y(SEQS - 1)

            @block.scalar
            def _(act):
                qk_bank = (xqv_bank, ky_bank)

                def move_xT(b):
                    act.wait_ge(xT_moved, b + 1)
                    act.activation(xnT[:, :], xqv_bank[:, :], ACT.Copy).then_inc(xnT_done, 1)

                def first_part(b, n):
                    act.wait_ge(qk_projected, 2 * b + n + 1)
                    act.activation((q_parts, k_parts)[n][0][:, :], qk_bank[n][:, :], ACT.Copy)\
                       .then_inc(part1_done, 1)

                def second_part(b, n):
                    act.wait_ge(rest_done, 2 * b + n + 1)
                    act.activation((q_parts, k_parts)[n][1][:, :], (q_rest, k_rest)[n][:, :], ACT.Copy)\
                       .then_inc(part2_done, 1)

                def spread_v(b, p):
                    act.wait_ge(v_projected, b + 1)
                    for s in range(2):
                        v = xqv_bank[:, :].rearrange("p (t s c) -> p t s c", t=TILES, s=2)[:, :, s, :]
                        act.activation(own_columns(v_wide[p], s, 0), v.rearrange("p t (h d) -> p t h d", d=D), ACT.Copy)\
                           .then_inc(v_done, 1)

                def move_max(b, half):
                    cols = slice(half * TOK // 2, (half + 1) * TOK // 2)
                    act.wait_ge(max_moved, 2 * b + half + 1)
                    act.activation(max_partsT[:, cols], score_bank[0][:, :].bitcast(BF16)[0:3 * HEADS, cols], ACT.Copy)\
                       .then_inc(maxT_done, 1)

                def exps(b, u, first):
                    act.wait_ge(key_scored, b * UNITS + u + 1)
                    if not first or u >= PROBS:
                        act.wait_ge(weighed, b * UNITS + u + 1 - PROBS)
                    act.activation(probs[:, u % PROBS, :], key_bank[u % 2][:, :], ACT.Exp, scale=SCALE)\
                       .then_inc(exp_done, 1)

                def body(b, p, first=False, last=False):
                    for u in range(UNITS):
                        if not last and u == 0:
                            move_xT(b + 1)
                        exps(b, u, first)
                        if not last and u in (1, 2):
                            first_part(b + 1, u - 1)
                        if not last and u in (2, 3):
                            second_part(b + 1, u - 2)
                        if u == 5:
                            move_max(b, 1)
                        if not last and u == 6:
                            spread_v(b + 1, 1 - p)
                        if not last and u == 13:
                            move_max(b + 1, 0)

                for i in range(2):
                    act.memzero(v_wide[i][:, :, :]).then_inc(v_zeroed, 1)
                move_xT(0)
                for n in range(2):
                    first_part(0, n)
                for n in range(2):
                    second_part(0, n)
                act.wait_ge(filled, FILLS)
                spread_v(0, 0)
                move_max(0, 0)
                body(0, 0, first=True)
                with act.Fori(0, (SEQS - 2) // 2) as pair:
                    b = 2 * pair + 1
                    body(b, 1)
                    body(b + 1, 0)
                body(SEQS - 1, 1, last=True)

            @block.tensor
            def _(pe):
                def move_x(b, first=False):
                    if not first:
                        pe.wait_ge(v_done, 2 * b)
                    for t in range(TILES):
                        pe.wait_ge(xn_done, 4 * b + t + 1)
                        mm = pe.transpose(tile_of(xqv_bank, t), xn[:, t, :], ident[:, :])
                    mm.then_inc(xT_moved, 1)

                def project_qk(b):
                    pe.wait_ge(xnT_done, b + 1)
                    for n, bank in enumerate((xqv_bank, ky_bank)):
                        pe.matmul(bank[:, :], w_qkv[:, n * C:(n + 1) * C], xnT[:, :],
                                  start=True, stop=True).then_inc(qk_projected, 1)

                def project_v(b):
                    pe.wait_ge(rest_done, 2 * b + 1)
                    for t in range(TILES):
                        mm = pe.matmul(tile_of(xqv_bank, t), tile_of(xnT, t), w_qkv[:, 2 * C:3 * C],
                                       start=True, stop=True)
                    mm.then_inc(v_projected, 1)

                def scores(b, p, u, first=False):
                    t, g = u // GROUPS, u % GROUPS
                    bank = score_bank[u % 2]
                    if u % HALF >= 2:
                        pe.wait_ge(max_done, b * UNITS + u - 1)
                    elif u % HALF == 0 and (u > 0 or not first):
                        pe.wait_ge(maxT_done, 2 * b + u // HALF)
                    pe.matmul(bank[:, :], ident_bf[:, :],
                              mask[:, :].rearrange("p (a k) -> p a k", a=1).to_broadcast([P, GROUP, P]),
                              start=True, stop=False, skip_group_check=True)
                    for j in range(GROUP):
                        h = g * GROUP + j
                        mm = pe.matmul(tile_of(bank, j), q_rows[p][:, h, t * P:(t + 1) * P],
                                       k_rows[p][:, h, t * P:(t + 1) * P], start=False, stop=True,
                                       skip_group_check=True)
                    mm.then_inc(scored, 1)

                def move_max(b, half):
                    count = pe.to_reg(8 * b + 4 * half + 4)
                    pe.wait_ge(weights_loaded, weights_count)
                    pe.wait_ge(max_split, count)
                    for t in range(half * TILES // 2, (half + 1) * TILES // 2):
                        mm = pe.transpose(score_bank[0][:, :].bitcast(BF16)[0:3 * HEADS, t * P:(t + 1) * P],
                                          max_parts[:, t, :, :].rearrange("p i h -> p (i h)"), ident_bf[:, :])
                    mm.then_inc(max_moved, 1)

                def key_scores(b, p, u, first):
                    t, g = u // GROUPS, u % GROUPS
                    if u % HALF == 0:
                        pe.wait_ge(max_loaded, 96 * b + 48 * (u // HALF + 1))
                    if not first or u >= 2:
                        pe.wait_ge(exp_done, b * UNITS + u - 1)
                    for j in range(GROUP):
                        h = g * GROUP + j
                        mm = pe.matmul(tile_of(key_bank[u % 2], j), k_rows[p][:, h, t * P:(t + 1) * P],
                                       q_rows[p][:, h, t * P:(t + 1) * P], start=True, stop=True)
                    mm.then_inc(key_scored, 1)

                def weigh(b, p, u, first=False):
                    t, g = u // GROUPS, u % GROUPS
                    pe.wait_ge(probs_done, b * UNITS + u + 1)
                    if u == 0:
                        pe.wait_ge(v_done, 2 * b + 2)
                    if g == 0 and (t >= 2 or not first):
                        pe.wait_ge(outT_done, b * 2 * TILES + 2 * (t - 1))
                    for j in range(GROUP):
                        h = g * GROUP + j
                        s = h // SET
                        mm = pe.matmul(tile_of(out_bank[t % 2], s), v_wide[p][:, t, h * P:(h + 1) * P],
                                       probs[:, u % PROBS, j * P:(j + 1) * P],
                                       start=(h % SET == 0), stop=(h % SET == SET - 1))
                    mm.then_inc(weighed, 1)

                def project_out(b, last=False):
                    if not last:
                        pe.wait_ge(rest_done, 2 * b + 6)
                    pe.wait_ge(outT_done, 2 * TILES * b + 2 * TILES)
                    for t in range(TILES):
                        mm = pe.matmul(tile_of(ky_bank, t), tile_of(outT, t), w_proj[:, :],
                                       start=True, stop=True)
                    mm.then_inc(proj_done, 1)

                def body(b, p, first=False, last=False):
                    for u in range(UNITS):
                        if not last and u == 0:
                            move_x(b + 1)
                        key_scores(b, p, u, first)
                        if u < HALF // 2:
                            scores(b, p, HALF + 2 * u)
                            scores(b, p, HALF + 2 * u + 1)
                        if not last and u == 1:
                            project_qk(b + 1)
                        if not last and u == 4:
                            project_v(b + 1)
                        if not first and u == 4:
                            project_out(b - 1, last)
                        if u == 5:
                            move_max(b, 1)
                        if u >= LAG:
                            weigh(b, p, u - LAG, first)
                        elif not first:
                            weigh(b - 1, 1 - p, UNITS - LAG + u)
                        if not last and LATE <= u < LATE + HALF // 2:
                            if u == LATE:
                                pe.wait_ge(rows_loaded, 208 * b + 416)
                            scores(b + 1, 1 - p, 2 * (u - LATE))
                            scores(b + 1, 1 - p, 2 * (u - LATE) + 1)
                        if not last and u == 13:
                            move_max(b + 1, 0)

                pe.wait_ge(weights_loaded, weights_count)
                move_x(0, first=True)
                project_qk(0)
                project_v(0)
                pe.wait_ge(filled, FILLS)
                pe.wait_ge(rows_loaded, 208)
                for u in range(HALF):
                    scores(0, 0, u, first=True)
                move_max(0, 0)
                body(0, 0, first=True)
                with pe.Fori(0, (SEQS - 2) // 2) as pair:
                    b = 2 * pair + 1
                    body(b, 1)
                    body(b + 1, 0)
                body(SEQS - 1, 1, last=True)
                for u in range(UNITS - LAG, UNITS):
                    weigh(SEQS - 1, 1, u)
                project_out(SEQS - 1, last=True)

            @block.vector
            def _(dve):
                def fill():
                    for rows in k_rows:
                        dve.memset(rows[:, :, :].bitcast(FP32), 0.0).then_inc(k_zeroed, 1)
                    for i in range(2):
                        dve.wait_ge(k_zeroed, i + 1)
                        dve.memset(k_rows[i][MAX_ROW:MAX_ROW + 32, :, :], 1.0).then_inc(filled, 1)
                    dve.wait_ge(v_zeroed, 2)
                    for s in range(2):
                        for i in range(2):
                            for t in range(TILES):
                                mm = dve.memset(own_columns(v_wide[i], s, P // 2)[:, t, :, :], 1.0)
                                if t == TILES - 1:
                                    mm.then_inc(filled, 1)

                def x_tile(b):
                    return lambda t: x[:, bass.ds(4 * b + t, 1), :].rearrange("p a c -> p (a c)")

                def apply_in(b, first=False):
                    if not first:
                        dve.wait_ge(xT_moved, b)
                    norm_in.apply(dve, b, lambda t: xn[:, t, :], x_tile(b), xn_done)

                def rest(b, n):
                    dve.wait_ge(part1_done, 2 * b + n + 1)
                    dve.tensor_tensor((q_rest, k_rest)[n][:, :], (xqv_bank, ky_bank)[n][:, :],
                                      (q_parts, k_parts)[n][0][:, :], ALU.subtract).then_inc(rest_done, 1)

                def maximum(b, u):
                    t, g = u // GROUPS, u % GROUPS
                    dve.wait_ge(scored, b * UNITS + u + 1)
                    dve.tensor_reduce(neg_max[:, t, g * GROUP:(g + 1) * GROUP],
                                      score_bank[u % 2][:, :].rearrange("p (j k) -> p j k", k=P),
                                      AX.X, ALU.max, negate=True).then_inc(max_done, 1)

                def split_max(b, half):
                    n = 8 * b + 4 * half
                    ts = slice(half * TILES // 2, (half + 1) * TILES // 2)
                    parts = [max_parts[:, ts, i, :] for i in range(3)]
                    dve.wait_ge(max_done, b * UNITS + (half + 1) * HALF)
                    dve.tensor_copy(parts[0], neg_max[:, ts, :]).then_inc(max_split, 1)
                    dve.wait_ge(max_split, n + 1)
                    dve.tensor_tensor(max_rest[:, ts, :], neg_max[:, ts, :], parts[0], ALU.subtract)\
                       .then_inc(max_split, 1)
                    dve.wait_ge(max_split, n + 2)
                    dve.tensor_copy(parts[1], max_rest[:, ts, :]).then_inc(max_split, 1)
                    dve.wait_ge(max_split, n + 3)
                    dve.tensor_tensor(parts[2], max_rest[:, ts, :], parts[1], ALU.subtract).then_inc(max_split, 1)

                def add_bias(b, first):
                    dve.wait_ge(proj_done, b + 1)
                    if not first:
                        dve.wait_ge(x_added, b)
                    dve.tensor_tensor(y[:, :, :], ky_bank[:, :].rearrange("p (t c) -> p t c", t=TILES),
                                      b_proj[:, :].rearrange("p (a c) -> p a c", a=1).to_broadcast([P, TILES, C]),
                                      ALU.add).then_inc(y_done, 1)

                def y_moments(b):
                    dve.wait_ge(y_done, b + 1)
                    norm_out.take_moments(dve, b, lambda t: y[:, t, :])

                def y_apply(b):
                    norm_out.apply(dve, b, lambda t: y[:, t, :], lambda t: y[:, t, :], yn_done)

                def scale_out(b, t, first=False):
                    n = b * TILES + t
                    o = out_bank[t % 2]
                    dve.wait_ge(weighed, UNITS * b + GROUPS * (t + 1))
                    if t > 0 or not first:
                        dve.wait_ge(outT_done, 2 * n)
                    for s in range(2):
                        dve.tensor_scalar(sums[s * 64:(s + 1) * 64, :], o[64:128, s * P:(s + 1) * P],
                                          1e-6, None, ALU.add).then_inc(sums_done, 1)
                    dve.wait_ge(sums_done, 2 * n + 2)
                    dve.reciprocal(sums[:, :], sums[:, :]).then_inc(inverted, 1)
                    dve.wait_ge(inverted, n + 1)
                    for s in range(2):
                        dve.tensor_tensor(outT[s * 64:(s + 1) * 64, t * P:(t + 1) * P],
                                          o[0:64, s * P:(s + 1) * P], sums[s * 64:(s + 1) * 64, :],
                                          ALU.mult).then_inc(outT_done, 1)

                def body(b, first=False, last=False, second=False, next_last=False):
                    for u in range(UNITS):
                        if u < HALF // 2:
                            maximum(b, HALF + 2 * u)
                            maximum(b, HALF + 2 * u + 1)
                        if not first and u == 1:
                            scale_out(b - 1, TILES - 1)
                        if not last and u in (1, 2):
                            rest(b + 1, u - 1)
                        if u == 3:
                            split_max(b, 1)
                        if not first and u == 4:
                            add_bias(b - 1, second)
                            y_moments(b - 1)
                        if u == 5:
                            if not first:
                                dve.wait_ge(proj_done, b)
                            scale_out(b, 0, first)
                        if not first and u == 7:
                            y_apply(b - 1)
                        if u == 9:
                            scale_out(b, 1)
                        if not last and LATE <= u < LATE + HALF // 2:
                            maximum(b + 1, 2 * (u - LATE))
                            maximum(b + 1, 2 * (u - LATE) + 1)
                        if not last and u == LATE + HALF // 2 - 1:
                            split_max(b + 1, 0)
                        if not last and not next_last and u == 12:
                            norm_in.take_moments(dve, b + 2, x_tile(b + 2))
                        if u == 13:
                            scale_out(b, 2)
                        if not last and not next_last and u == 14:
                            apply_in(b + 2)

                dve.wait_ge(x_loaded, X_LOADS)
                norm_in.take_moments(dve, 0, x_tile(0))
                apply_in(0, first=True)
                fill()
                for n in range(2):
                    rest(0, n)
                norm_in.take_moments(dve, 1, x_tile(1))
                for u in range(HALF):
                    maximum(0, u)
                split_max(0, 0)
                apply_in(1)
                body(0, first=True)
                body(1, second=True)
                with dve.Fori(2, SEQS - 2) as b:
                    body(b)
                body(SEQS - 2, next_last=True)
                body(SEQS - 1, last=True)
                scale_out(SEQS - 1, TILES - 1)
                add_bias(SEQS - 1, False)
                y_moments(SEQS - 1)
                y_apply(SEQS - 1)


class Router:

    def __init__(self, nc, ctx, name, x, x_loaded, ident, ident_bf, minus_half, experts, top_k, w_router, b_router, bank):
        def sb(n, shape, dt=FP32):
            return ctx.enter_context(nc.sbuf_tensor(f"{name}_{n}", shape, dt))

        def sem(n):
            return ctx.enter_context(nc.semaphore(f"{name}_{n}"))

        self.x, self.x_loaded, self.ident, self.ident_bf, self.bank = x, x_loaded, ident, ident_bf, bank
        self.E, self.K, self.w_router, self.b_router = experts, top_k, w_router, b_router
        self.PAD = 8 - top_k
        self.norm = Norm(sb, sem, "norm", minus_half, x_loaded)
        self.xn = sb("xn", [P, TILES, C])
        self.xnT = [sb(f"xnT{i}", [C, TOK]) for i in range(2)]
        self.logits = sb("logits", [P, TILES, experts])
        self.largest = sb("largest", [P, TILES])
        self.shifted = sb("shifted", [P, TILES, experts])
        self.exps = sb("exps", [P, TILES, experts])
        self.total = sb("total", [P, TILES])
        self.total_inv = sb("total_inv", [P, TILES])
        self.probs = sb("probs", [P, TILES, experts + self.PAD])
        self.top = sb("top", [P, TILES, 8])
        self.taken = sb("taken", [P, TILES, 8])
        self.left = sb("left", [P, TILES, experts + self.PAD])
        self.coef = sb("coef", [P, TILES, experts])
        self.coef_rest = sb("coef_rest", [P, TILES, experts])
        self.coef_parts = sb("coef_parts", [P, TILES, 3, experts], BF16)
        self.coefT = [sb(f"coefT{i}", [P, TOK], BF16) for i in range(2)]
        self.xn_done = sem("xn_done")
        self.xT_moved = sem("xT_moved")
        self.xnT_done = sem("xnT_done")
        self.logits_done = sem("logits_done")
        self.soft = sem("soft")
        self.exp_done = sem("exp_done")
        self.top_done = sem("top_done")
        self.split = sem("split")
        self.coef_moved = sem("coef_moved")
        self.coefT_done = sem("coefT_done")

    SOFT = 6

    def fill(self, dve, done):
        for j in range(self.PAD):
            dve.memset(self.probs[:, :, self.E + j:self.E + j + 1], -1.0 - j)
            last = dve.memset(self.taken[:, :, self.K + j:self.K + j + 1], -1.0 - j)
        last.then_inc(done, 1)
        for coefT in self.coefT:
            last = dve.memset(coefT[:, :].bitcast(FP32), 0.0)
        last.then_inc(done, 1)

    def x_tile(self, b):
        return lambda t: self.x[:, bass.ds(4 * b + t, 1), :].rearrange("p a c -> p (a c)")

    def take_moments(self, dve, b):
        self.norm.take_moments(dve, b, self.x_tile(b))

    def normalize(self, dve, b, first=False):
        if not first:
            dve.wait_ge(self.xT_moved, b)
        self.norm.apply(dve, b, lambda t: self.xn[:, t, :], self.x_tile(b), self.xn_done)

    def shift(self, dve, b):
        E, S = self.E, self.SOFT
        dve.wait_ge(self.logits_done, b + 1)
        logits = self.bank[:, 0:TILES * E].rearrange("p (t e) -> p t e", e=E)
        if self.b_router is not None:
            dve.tensor_tensor(self.logits[:, :, :], logits,
                              self.b_router[:, :].rearrange("p (a e) -> p a e", a=1).to_broadcast([P, TILES, E]),
                              ALU.add).then_inc(self.soft, 1)
        else:
            dve.tensor_copy(self.logits[:, :, :], logits).then_inc(self.soft, 1)
        dve.wait_ge(self.soft, S * b + 1)
        dve.tensor_reduce(self.largest[:, :], self.logits[:, :, :], AX.X, ALU.max).then_inc(self.soft, 1)
        dve.wait_ge(self.soft, S * b + 2)
        dve.tensor_tensor(self.shifted[:, :, :], self.logits[:, :, :],
                          self.largest[:, :].rearrange("p (t a) -> p t a", a=1).to_broadcast([P, TILES, E]),
                          ALU.subtract).then_inc(self.soft, 1)

    def choose(self, dve, b):
        E, K, S = self.E, self.K, self.SOFT
        T = 2 * TILES + 2
        dve.wait_ge(self.exp_done, b + 1)
        dve.tensor_reduce(self.total[:, :], self.exps[:, :, :], AX.X, ALU.add).then_inc(self.soft, 1)
        dve.wait_ge(self.soft, S * b + 4)
        dve.reciprocal(self.total_inv[:, :], self.total[:, :]).then_inc(self.soft, 1)
        dve.wait_ge(self.soft, S * b + 5)
        dve.tensor_tensor(self.probs[:, :, 0:E], self.exps[:, :, :],
                          self.total_inv[:, :].rearrange("p (t a) -> p t a", a=1).to_broadcast([P, TILES, E]),
                          ALU.mult).then_inc(self.soft, 1)
        count = dve.to_reg(S * b + 6)
        dve.wait_ge(self.x_loaded, X_LOADS)
        dve.wait_ge(self.soft, count)
        for t in range(TILES):
            dve.max(self.top[:, t, :], self.probs[:, t, 0:E]).then_inc(self.top_done, 1)
        dve.wait_ge(self.top_done, T * b + TILES)
        dve.tensor_copy(self.taken[:, :, 0:K], self.top[:, :, 0:K]).then_inc(self.top_done, 1)
        count = dve.to_reg(T * b + TILES + 1)
        dve.wait_ge(self.x_loaded, X_LOADS)
        dve.wait_ge(self.top_done, count)
        for t in range(TILES):
            dve.match_replace(self.left[:, t, :], self.taken[:, t, :], self.probs[:, t, :], 0.0)\
               .then_inc(self.top_done, 1)
        dve.wait_ge(self.top_done, T * b + 2 * TILES + 1)
        dve.tensor_tensor(self.coef[:, :, :], self.probs[:, :, 0:E], self.left[:, :, 0:E], ALU.subtract)\
           .then_inc(self.top_done, 1)
        dve.wait_ge(self.top_done, T * b + T)
        dve.tensor_copy(self.coef_parts[:, :, 0, :], self.coef[:, :, :]).then_inc(self.split, 1)
        dve.wait_ge(self.split, 4 * b + 1)
        dve.tensor_tensor(self.coef_rest[:, :, :], self.coef[:, :, :], self.coef_parts[:, :, 0, :],
                          ALU.subtract).then_inc(self.split, 1)
        dve.wait_ge(self.split, 4 * b + 2)
        dve.tensor_copy(self.coef_parts[:, :, 1, :], self.coef_rest[:, :, :]).then_inc(self.split, 1)
        dve.wait_ge(self.split, 4 * b + 3)
        dve.tensor_tensor(self.coef_parts[:, :, 2, :], self.coef_rest[:, :, :], self.coef_parts[:, :, 1, :],
                          ALU.subtract).then_inc(self.split, 1)

    def move_xT(self, act, b, p):
        act.wait_ge(self.xT_moved, b + 1)
        act.activation(self.xnT[p][:, :], self.bank[:, :], ACT.Copy).then_inc(self.xnT_done, 1)

    def exponents(self, act, b):
        act.wait_ge(self.soft, self.SOFT * b + 3)
        act.activation(self.exps[:, :, :], self.shifted[:, :, :], ACT.Exp).then_inc(self.exp_done, 1)

    def move_coef(self, act, b, p):
        act.wait_ge(self.coef_moved, b + 1)
        act.activation(self.coefT[p][0:3 * self.E, :], self.bank[:, :].bitcast(BF16)[0:3 * self.E, 0:TOK], ACT.Copy)\
           .then_inc(self.coefT_done, 1)

    def move_x(self, pe, b, first=False):
        if not first:
            pe.wait_ge(self.coefT_done, b)
        for t in range(TILES):
            pe.wait_ge(self.xn_done, 4 * b + t + 1)
            mm = pe.transpose(self.bank[:, t * P:(t + 1) * P], self.xn[:, t, :], self.ident[:, :])
        mm.then_inc(self.xT_moved, 1)

    def take_logits(self, pe, b, p):
        pe.wait_ge(self.xnT_done, b + 1)
        for t in range(TILES):
            mm = pe.matmul(self.bank[:, t * self.E:(t + 1) * self.E], self.xnT[p][:, t * P:(t + 1) * P],
                           self.w_router[:, :], start=True, stop=True)
        mm.then_inc(self.logits_done, 1)

    def move_parts(self, pe, b):
        count = pe.to_reg(4 * b + 4)
        pe.wait_ge(self.x_loaded, X_LOADS)
        pe.wait_ge(self.split, count)
        for t in range(TILES):
            mm = pe.transpose(self.bank[:, :].bitcast(BF16)[0:3 * self.E, t * P:(t + 1) * P],
                              self.coef_parts[:, t, :, :].rearrange("p i e -> p (i e)"), self.ident_bf[:, :])
        mm.then_inc(self.coef_moved, 1)


def fill_selectors(pool, selectors, experts, width, done):
    pool.memset(selectors[:, :], 0.0).then_inc(done, 1)
    view = selectors[:, :].rearrange("r (e w) -> r e w", w=width)
    for i in range(3):
        pool.wait_ge(done, i + 1)
        pool.affine_select(out=view, in_=view, compare_op=ALU.not_equal, fill=1.0, base=-i * experts,
                           pattern=[[-1, experts], [0, width]], channel_multiplier=1).then_inc(done, 1)


def swiglu_experts_layer(nc, x, x_loaded, ident, ident_bf, minus_half, w, weights_loaded, weights_count):
    E, K, D = 8, 2, 64
    PAIRS = E * D // P
    STEPS = PAIRS + 1
    LAG = 2

    with ExitStack() as ctx:
        def sb(name, shape, dt=FP32):
            return ctx.enter_context(nc.sbuf_tensor("sw_" + name, shape, dt))

        def sem(name):
            return ctx.enter_context(nc.semaphore("sw_" + name))

        banks = [ctx.enter_context(nc.psum_tensor(f"sw_bank{i}", [P, TOK], FP32)) for i in range(8)]
        gate_bank, up_bank, out_bank, coef_bank = banks[1:3], banks[3:5], banks[5:7], banks[7]
        r = Router(nc, ctx, "swr", x, x_loaded, ident, ident_bf, minus_half, E, K, w["router"], None, banks[0])
        norm_out = Norm(sb, sem, "norm_out", minus_half, x_loaded)
        selectors = sb("selectors", [P, E * D], BF16)
        tanh_gate = sb("tanh_gate", [P, 2, TOK])
        gated = sb("gated", [P, 2, TOK])
        hidden = sb("hidden", [P, 2, TOK])
        weighed = sb("weighed", [P, 2, TOK])
        yn = sb("yn", [P, TILES, C])

        filled = sem("filled")
        selectors_done = sem("selectors_done")
        gate_up = sem("gate_up")
        coef_spread = sem("coef_spread")
        tanh_done = sem("tanh_done")
        gated_done = sem("gated_done")
        hidden_done = sem("hidden_done")
        weighed_done = sem("weighed_done")
        summed = sem("summed")
        yn_done = sem("yn_done")
        x_added = sem("x_added")

        with nc.Block() as block:

            @block.gpsimd
            def _(pool):
                fill_selectors(pool, selectors, E, D, selectors_done)

                def add(b):
                    pool.wait_ge(yn_done, 4 * b + 4)
                    xs = x[:, bass.ds(4 * b, TILES), :]
                    pool.tensor_tensor(xs, xs, yn[:, :, :], ALU.add).then_inc(x_added, 1)

                def body(b, first=False, last=False, next_last=False):
                    if not first:
                        norm_out.take_power(pool, b - 1)
                        add(b - 1)
                    if not last and not next_last:
                        r.norm.take_power(pool, b + 2)

                r.norm.take_power(pool, 0)
                r.norm.take_power(pool, 1)
                body(0, first=True)
                with pool.Fori(1, SEQS - 2) as b:
                    body(b)
                body(SEQS - 2, next_last=True)
                body(SEQS - 1, last=True)
                norm_out.take_power(pool, SEQS - 1)
                add(SEQS - 1)

            @block.scalar
            def _(act):
                def tanh(b, p, i, first):
                    n, s = b * STEPS + i, (p + i) % 2
                    act.wait_ge(gate_up, n + 1)
                    if not first or i >= 2:
                        act.wait_ge(gated_done, n - 1)
                    act.activation(tanh_gate[:, s, :], gate_bank[s][:, :], ACT.Tanh, scale=0.5)\
                       .then_inc(tanh_done, 1)

                def body(b, p, first=False, last=False):
                    for i in range(STEPS):
                        tanh(b, p, i, first)
                        if not first and i == 0:
                            r.move_coef(act, b, p)
                        if not last and i == 1:
                            r.move_xT(act, b + 1, 1 - p)
                        if not last and i == 3:
                            r.exponents(act, b + 1)

                act.wait_ge(filled, 2)
                r.move_xT(act, 0, 0)
                r.exponents(act, 0)
                r.move_coef(act, 0, 0)
                body(0, 0, first=True)
                with act.Fori(0, (SEQS - 2) // 2) as pair:
                    b = 2 * pair + 1
                    body(b, 1)
                    body(b + 1, 0)
                body(SEQS - 1, 1, last=True)

            @block.tensor
            def _(pe):
                def gate_and_up(b, p, i, first):
                    n, s = b * STEPS + i, (p + i) % 2
                    if not first or i >= 2:
                        pe.wait_ge(hidden_done, n - 1)
                    for bank, name in ((gate_bank, "gate"), (up_bank, "up")):
                        lhs = w["shared_" + name][:, :] if i == 0 else w[name][:, (i - 1) * P:i * P]
                        mm = pe.matmul(bank[s][:, :], lhs, r.xnT[p][:, :], start=True, stop=True)
                    mm.then_inc(gate_up, 1)

                def spread(b, p, i, first):
                    m = b * PAIRS + i - 1
                    if i == 1:
                        pe.wait_ge(r.coefT_done, b + 1)
                    if not first or i >= 2:
                        pe.wait_ge(weighed_done, m)
                    pe.matmul(coef_bank[:, :], selectors[:, (i - 1) * P:i * P], r.coefT[p][:, :], start=True, stop=True)\
                      .then_inc(coef_spread, 1)

                def down(b, p, i, first=False, second=False):
                    if i == 0:
                        pe.wait_ge(hidden_done, b * STEPS + 1)
                        if not first and not second:
                            pe.wait_ge(yn_done, 4 * b - 4)
                    else:
                        pe.wait_ge(weighed_done, b * PAIRS + i)
                    rhs = w["shared_down"][:, :] if i == 0 else w["down"][:, i - 1, :]
                    for t in range(TILES):
                        mm = pe.matmul(out_bank[p][:, t * P:(t + 1) * P], weighed[:, (p + i) % 2, t * P:(t + 1) * P], rhs,
                                       start=(i == 0 and t == 0), stop=(i == STEPS - 1), skip_group_check=True)
                    mm.then_inc(summed, 1)

                def body(b, p, first=False, last=False, second=False):
                    for i in range(STEPS):
                        gate_and_up(b, p, i, first)
                        if i >= LAG:
                            down(b, p, i - LAG, first, second)
                        elif not first:
                            down(b - 1, 1 - p, STEPS - LAG + i)
                        if not first and i == 0:
                            r.move_parts(pe, b)
                        if i >= 1:
                            spread(b, p, i, first)
                        if not last and i == 1:
                            r.move_x(pe, b + 1)
                        if not last and i == 2:
                            r.take_logits(pe, b + 1, 1 - p)

                pe.wait_ge(weights_loaded, weights_count)
                pe.wait_ge(selectors_done, 4)
                r.move_x(pe, 0, first=True)
                r.take_logits(pe, 0, 0)
                r.move_parts(pe, 0)
                body(0, 0, first=True)
                body(1, 1, second=True)
                with pe.Fori(0, (SEQS - 4) // 2) as pair:
                    b = 2 * pair + 2
                    body(b, 0)
                    body(b + 1, 1)
                body(SEQS - 2, 0)
                body(SEQS - 1, 1, last=True)
                for i in range(STEPS - LAG, STEPS):
                    down(SEQS - 1, 1, i)

            @block.vector
            def _(dve):
                def hide(b, p, i, first):
                    n, s = b * STEPS + i, (p + i) % 2
                    dve.wait_ge(tanh_done, n + 1)
                    dve.scalar_tensor_tensor(out=gated[:, s, :], in0=tanh_gate[:, s, :], scalar=1.0,
                                             in1=gate_bank[s][:, :], op0=ALU.add, op1=ALU.mult)\
                       .then_inc(gated_done, 1)
                    dve.wait_ge(gated_done, n + 1)
                    if i == 0 and not first:
                        dve.wait_ge(summed, n - 1)
                    out = weighed if i == 0 else hidden
                    dve.scalar_tensor_tensor(out=out[:, s, :], in0=gated[:, s, :], scalar=0.5,
                                             in1=up_bank[s][:, :], op0=ALU.mult, op1=ALU.mult)\
                       .then_inc(hidden_done, 1)
                    if i >= 1:
                        m = b * PAIRS + i - 1
                        dve.wait_ge(hidden_done, n + 1)
                        dve.wait_ge(coef_spread, m + 1)
                        if not first or i >= 2:
                            dve.wait_ge(summed, n - 1)
                        dve.tensor_tensor(weighed[:, s, :], hidden[:, s, :], coef_bank[:, :], ALU.mult)\
                           .then_inc(weighed_done, 1)

                def out_tile(o):
                    return lambda t: out_bank[o][:, t * P:(t + 1) * P]

                def out_moments(b, p):
                    dve.wait_ge(summed, STEPS * b + STEPS)
                    norm_out.take_moments(dve, b, out_tile(p))

                def out_apply(b, p, first=False):
                    if not first:
                        dve.wait_ge(x_added, b)
                    norm_out.apply(dve, b, lambda t: yn[:, t, :], out_tile(p), yn_done)

                def body(b, p, first=False, last=False, second=False, next_last=False):
                    if not last:
                        r.normalize(dve, b + 1)
                    for i in range(STEPS):
                        hide(b, p, i, first)
                        if not first and i == 1:
                            out_moments(b - 1, 1 - p)
                        if not first and i == 2:
                            out_apply(b - 1, 1 - p, second)
                        if not last and i == 2:
                            r.shift(dve, b + 1)
                        if not last and i == 3:
                            r.choose(dve, b + 1)
                    if not last and not next_last:
                        r.take_moments(dve, b + 2)

                r.fill(dve, filled)
                r.take_moments(dve, 0)
                r.normalize(dve, 0, first=True)
                r.take_moments(dve, 1)
                r.shift(dve, 0)
                r.choose(dve, 0)
                body(0, 0, first=True)
                body(1, 1, second=True)
                with dve.Fori(0, (SEQS - 4) // 2) as pair:
                    b = 2 * pair + 2
                    body(b, 0)
                    body(b + 1, 1)
                body(SEQS - 2, 0, next_last=True)
                body(SEQS - 1, 1, last=True)
                out_moments(SEQS - 1, 1)
                out_apply(SEQS - 1, 1)


def relu_experts_layer(nc, x, x_loaded, ident, ident_bf, minus_half, w, weights_loaded, weights_count):
    E, K = 15, 3
    STEPS = E + 1
    HIDDEN = 4
    COEFS = 3
    LAG = 2
    ONES = 96

    with ExitStack() as ctx:
        def sb(name, shape, dt=FP32):
            return ctx.enter_context(nc.sbuf_tensor("re_" + name, shape, dt))

        def sem(name):
            return ctx.enter_context(nc.semaphore("re_" + name))

        banks = [ctx.enter_context(nc.psum_tensor(f"re_bank{i}", [P, TOK], FP32)) for i in range(8)]
        hidden_bank, coef_bank, out_bank = banks[1:3], banks[3:6], banks[6:8]
        r = Router(nc, ctx, "rer", x, x_loaded, ident, ident_bf, minus_half, E, K, w["router"], w["b_router"], banks[0])
        norm_out = Norm(sb, sem, "norm_out", minus_half, x_loaded)
        selectors = sb("selectors", [P, E * P], BF16)
        b2_rest = sb("b2_rest", [P, C])
        b2_parts = sb("b2_parts", [P, 3, C], BF16)
        hidden = sb("hidden", [P, HIDDEN, TOK])
        weighed = sb("weighed", [P, HIDDEN, TOK])
        yn = sb("yn", [P, TILES, C])

        filled = sem("filled")
        b2_split = sem("b2_split")
        selectors_done = sem("selectors_done")
        first_product = sem("first_product")
        coef_spread = sem("coef_spread")
        hidden_done = sem("hidden_done")
        weighed_done = sem("weighed_done")
        summed = sem("summed")
        yn_done = sem("yn_done")
        x_added = sem("x_added")

        with nc.Block() as block:

            @block.gpsimd
            def _(pool):
                fill_selectors(pool, selectors, E, P, selectors_done)

                def add(b):
                    pool.wait_ge(yn_done, 4 * b + 4)
                    xs = x[:, bass.ds(4 * b, TILES), :]
                    pool.tensor_tensor(xs, xs, yn[:, :, :], ALU.add).then_inc(x_added, 1)

                def body(b, first=False, last=False, next_last=False):
                    if not first:
                        norm_out.take_power(pool, b - 1)
                        add(b - 1)
                    if not last and not next_last:
                        r.norm.take_power(pool, b + 2)

                r.norm.take_power(pool, 0)
                r.norm.take_power(pool, 1)
                body(0, first=True)
                with pool.Fori(1, SEQS - 2) as b:
                    body(b)
                body(SEQS - 2, next_last=True)
                body(SEQS - 1, last=True)
                norm_out.take_power(pool, SEQS - 1)
                add(SEQS - 1)

            @block.scalar
            def _(act):
                def relu(b, i, first):
                    n = b * STEPS + i
                    act.wait_ge(first_product, n + 1)
                    if not first or i >= HIDDEN:
                        act.wait_ge(summed, n + 1 - HIDDEN)
                    act.activation(hidden[:, i % HIDDEN, :], hidden_bank[i % 2][:, :], ACT.Relu,
                                   bias=w["b1"][:, i:i + 1]).then_inc(hidden_done, 1)

                def body(b, p, first=False, last=False):
                    for i in range(STEPS):
                        relu(b, i, first)
                        if not last:
                            if i == 2:
                                r.move_xT(act, b + 1, 1 - p)
                            if i == 5:
                                r.exponents(act, b + 1)
                            if i == 12:
                                r.move_coef(act, b + 1, 1 - p)

                act.wait_ge(filled, 3)
                act.wait_ge(weights_loaded, weights_count)
                r.move_xT(act, 0, 0)
                r.exponents(act, 0)
                r.move_coef(act, 0, 0)
                body(0, 0, first=True)
                with act.Fori(0, (SEQS - 2) // 2) as pair:
                    b = 2 * pair + 1
                    body(b, 1)
                    body(b + 1, 0)
                body(SEQS - 1, 1, last=True)

            @block.tensor
            def _(pe):
                def first_product_of(b, p, i, first):
                    if not first or i >= 2:
                        pe.wait_ge(hidden_done, b * STEPS + i - 1)
                    pe.matmul(hidden_bank[i % 2][:, :], w["w1"][:, i, :], r.xnT[p][:, :],
                              start=True, stop=True).then_inc(first_product, 1)

                def spread(b, p, i, first):
                    m = b * E + i - 1
                    if not first or i > COEFS:
                        pe.wait_ge(weighed_done, m + 1 - COEFS)
                    pe.matmul(coef_bank[(i - 1) % COEFS][:, :], selectors[:, (i - 1) * P:i * P], r.coefT[p][:, :],
                              start=True, stop=True).then_inc(coef_spread, 1)

                def biases(b, p, first, second):
                    pe.wait_ge(r.coefT_done, b + 1)
                    if not first and not second:
                        pe.wait_ge(yn_done, 4 * b - 4)
                    for t in range(TILES):
                        for i in range(3):
                            pe.matmul(out_bank[p][:, t * P:(t + 1) * P], r.coefT[p][:, t * P:(t + 1) * P],
                                      b2_parts[:, i, :], start=(t == 0 and i == 0), stop=False,
                                      skip_group_check=True)

                def second_product(b, p, i):
                    if i == 0:
                        pe.wait_ge(hidden_done, b * STEPS + 1)
                    else:
                        pe.wait_ge(weighed_done, b * E + i)
                    h = hidden if i == 0 else weighed
                    for t in range(TILES):
                        mm = pe.matmul(out_bank[p][:, t * P:(t + 1) * P], h[:, i % HIDDEN, t * P:(t + 1) * P],
                                       w["w2"][:, i, :], start=False, stop=(i == STEPS - 1),
                                       skip_group_check=True)
                    mm.then_inc(summed, 1)

                def body(b, p, first=False, last=False, second=False):
                    for i in range(STEPS):
                        first_product_of(b, p, i, first)
                        if i == 1:
                            biases(b, p, first, second)
                        if i >= 1:
                            spread(b, p, i, first)
                        if i >= LAG:
                            second_product(b, p, i - LAG)
                        elif not first:
                            second_product(b - 1, 1 - p, STEPS - LAG + i)
                        if not last:
                            if i == 2:
                                r.move_x(pe, b + 1)
                            if i == 4:
                                r.take_logits(pe, b + 1, 1 - p)
                            if i == 12:
                                r.move_parts(pe, b + 1)

                pe.wait_ge(weights_loaded, weights_count)
                pe.wait_ge(selectors_done, 4)
                pe.wait_ge(b2_split, 5)
                r.move_x(pe, 0, first=True)
                r.take_logits(pe, 0, 0)
                r.move_parts(pe, 0)
                body(0, 0, first=True)
                body(1, 1, second=True)
                with pe.Fori(0, (SEQS - 4) // 2) as pair:
                    b = 2 * pair + 2
                    body(b, 0)
                    body(b + 1, 1)
                body(SEQS - 2, 0)
                body(SEQS - 1, 1, last=True)
                for i in range(STEPS - LAG, STEPS):
                    second_product(SEQS - 1, 1, i)

            @block.vector
            def _(dve):
                def weigh(b, i, first):
                    n, m = b * STEPS + i, b * E + i - 1
                    dve.wait_ge(hidden_done, n + 1)
                    dve.wait_ge(coef_spread, m + 1)
                    if not first or i >= HIDDEN + 1:
                        dve.wait_ge(summed, n + 1 - HIDDEN)
                    dve.tensor_tensor(weighed[:, i % HIDDEN, :], hidden[:, i % HIDDEN, :],
                                      coef_bank[(i - 1) % COEFS][:, :], ALU.mult).then_inc(weighed_done, 1)

                def out_tile(o):
                    return lambda t: out_bank[o][:, t * P:(t + 1) * P]

                def finish(b, p, first=False):
                    dve.wait_ge(summed, STEPS * b + STEPS)
                    norm_out.take_moments(dve, b, out_tile(p))
                    if not first:
                        dve.wait_ge(x_added, b)
                    norm_out.apply(dve, b, lambda t: yn[:, t, :], out_tile(p), yn_done)

                def body(b, p, first=False, last=False, second=False, next_last=False):
                    if not last:
                        r.normalize(dve, b + 1)
                    for i in range(1, STEPS):
                        weigh(b, i, first)
                        if not first and i == 2:
                            finish(b - 1, 1 - p, second)
                        if not last and i == 5:
                            r.shift(dve, b + 1)
                        if not last and i == 7:
                            r.choose(dve, b + 1)
                    if not last and not next_last:
                        r.take_moments(dve, b + 2)

                r.fill(dve, filled)
                dve.wait_ge(filled, 2)
                for coefT in r.coefT:
                    last = dve.memset(coefT[ONES:ONES + 1, :], 1.0)
                last.then_inc(filled, 1)
                dve.wait_ge(weights_loaded, weights_count)
                dve.tensor_copy(b2_parts[:, 0, :], w["b2_rows"][:, :]).then_inc(b2_split, 1)
                dve.wait_ge(b2_split, 1)
                dve.tensor_tensor(b2_rest[:, :], w["b2_rows"][:, :], b2_parts[:, 0, :], ALU.subtract)\
                   .then_inc(b2_split, 1)
                dve.wait_ge(b2_split, 2)
                dve.tensor_copy(b2_parts[:, 1, :], b2_rest[:, :]).then_inc(b2_split, 1)
                dve.wait_ge(b2_split, 3)
                dve.tensor_tensor(b2_parts[:, 2, :], b2_rest[:, :], b2_parts[:, 1, :], ALU.subtract)\
                   .then_inc(b2_split, 2)
                r.take_moments(dve, 0)
                r.normalize(dve, 0, first=True)
                r.take_moments(dve, 1)
                r.shift(dve, 0)
                r.choose(dve, 0)
                body(0, 0, first=True)
                body(1, 1, second=True)
                with dve.Fori(0, (SEQS - 4) // 2) as pair:
                    b = 2 * pair + 2
                    body(b, 0)
                    body(b + 1, 1)
                body(SEQS - 2, 0, next_last=True)
                body(SEQS - 1, 1, last=True)
                finish(SEQS - 1, 1)


def rwkv_layer(nc, x, x_loaded, ident, minus_half, w, weights_loaded, weights_count):
    F = 512
    FCH = F // P
    START = -1e38

    with ExitStack() as ctx:
        def sb(name, shape, dt=FP32):
            return ctx.enter_context(nc.sbuf_tensor("rk_" + name, shape, dt))

        def sem(name):
            return ctx.enter_context(nc.semaphore("rk_" + name))

        banks = [ctx.enter_context(nc.psum_tensor(f"rk_bank{i}", [P, TOK], FP32)) for i in range(8)]
        xT_bank, k_bank, v_bank, r_bank, x1_bank = banks[0:5]
        f_bank, kv_bank = banks[5:7], banks[7]
        norm_x = Norm(sb, sem, "norm_x", minus_half, x_loaded)
        norm_1 = Norm(sb, sem, "norm_1", minus_half, x_loaded)
        norm_3 = Norm(sb, sem, "norm_3", minus_half, x_loaded)
        xs = sb("xs", [P, TILES, C])
        var_2 = sb("var_2", [P, TILES])
        rstd_2 = sb("rstd_2", [P, TILES])
        xhat = sb("xhat", [P, TILES, C])
        xnT = sb("xnT", [C, 1 + TOK])
        step = sb("step", [C, TOK])
        xk = sb("xk", [C, TOK])
        xv = sb("xv", [C, TOK])
        xr = sb("xr", [C, TOK])
        tanh_r = sb("tanh_r", [C, TOK])
        decay = sb("decay", [C, 1])
        exp_decay = sb("exp_decay", [C, 1])
        top = sb("top", [C, 1 + TOK])
        numer = sb("numer", [C, 1 + TOK])
        denom = sb("denom", [C, 1 + TOK])
        now_max = sb("now_max", [C, TOK])
        args = sb("args", [C, 4, TOK])
        exps = sb("exps", [C, 4, TOK])
        enter_v = sb("enter_v", [C, TOK])
        now_v = sb("now_v", [C, TOK])
        past_v = sb("past_v", [C, TOK])
        past_1 = sb("past_1", [C, TOK])
        sum_v = sb("sum_v", [C, TOK])
        sum_1 = sb("sum_1", [C, TOK])
        sum_inv = sb("sum_inv", [C, TOK])
        wkv = sb("wkv", [C, TOK])
        gated = sb("gated", [C, TOK])
        x1 = sb("x1", [P, TILES, C])
        xhat2 = sb("xhat2", [P, TILES, C])
        xn2T = sb("xn2T", [C, 1 + TOK])
        step2 = sb("step2", [C, TOK])
        xk2 = sb("xk2", [C, TOK])
        xr2 = sb("xr2", [C, TOK])
        relu = sb("relu", [P, FCH, TOK])
        square = sb("square", [P, FCH, TOK])
        tanh_g = sb("tanh_g", [P, TOK])
        kv_gated = sb("kv_gated", [P, TOK])
        out3 = sb("out3", [P, TILES, C])
        yn = sb("yn", [P, TILES, C])

        filled = sem("filled")
        decay_done = sem("decay_done")
        xs_done = sem("xs_done")
        var_2_done = sem("var_2_done")
        rstd_2_done = sem("rstd_2_done")
        xhat_done = sem("xhat_done")
        xT_moved = sem("xT_moved")
        xnT_done = sem("xnT_done")
        step_done = sem("step_done")
        mixed = sem("mixed")
        kvr_done = sem("kvr_done")
        tanh_done = sem("tanh_done")
        top_done = sem("top_done")
        args_done = sem("args_done")
        exps_done = sem("exps_done")
        scans = sem("scans")
        now_v_done = sem("now_v_done")
        past_done = sem("past_done")
        sums_done = sem("sums_done")
        gated_done = sem("gated_done")
        x1_projected = sem("x1_projected")
        x1_done = sem("x1_done")
        xhat2_done = sem("xhat2_done")
        x2T_moved = sem("x2T_moved")
        xn2T_done = sem("xn2T_done")
        step2_done = sem("step2_done")
        mixed2 = sem("mixed2")
        f_done = sem("f_done")
        relu_done = sem("relu_done")
        square_done = sem("square_done")
        gate_projected = sem("gate_projected")
        kv_done = sem("kv_done")
        tanh_g_done = sem("tanh_g_done")
        kv_gated_done = sem("kv_gated_done")
        out3_done = sem("out3_done")
        yn_done = sem("yn_done")
        x_added = sem("x_added")

        def tiles(ap):
            return ap.rearrange("p (t c) -> p t c", t=TILES)

        def x_tile(b):
            return lambda t: x[:, bass.ds(4 * b + t, 1), :].rearrange("p a c -> p (a c)")

        with nc.Block() as block:

            @block.gpsimd
            def _(pool):
                def second_power(b):
                    pool.wait_ge(var_2_done, 3 * b + 3)
                    pool.tensor_tensor(rstd_2[:, :], var_2[:, :], minus_half[:, :], ALU.pow)\
                        .then_inc(rstd_2_done, 1)

                def past(b):
                    pool.wait_ge(exps_done, 4 * b + 3)
                    pool.wait_ge(scans, 3 * b + 1)
                    pool.tensor_tensor(past_1[:, :], exps[:, 2, :], denom[:, 0:TOK], ALU.mult)\
                        .then_inc(past_done, 1)
                    pool.wait_ge(scans, 3 * b + 3)
                    pool.tensor_tensor(past_v[:, :], exps[:, 2, :], numer[:, 0:TOK], ALU.mult)\
                        .then_inc(past_done, 1)

                def add(b):
                    pool.wait_ge(yn_done, 4 * b + 4)
                    xs_ = x[:, bass.ds(4 * b, TILES), :]
                    pool.tensor_tensor(xs_, xs_, yn[:, :, :], ALU.add).then_inc(x_added, 1)

                def body(b, first=False, last=False, next_last=False):
                    norm_1.take_power(pool, b)
                    if not last:
                        second_power(b + 1)
                    if not first:
                        add(b - 1)
                    if not last and not next_last:
                        norm_x.take_power(pool, b + 2)
                    if not last:
                        past(b + 1)
                    norm_3.take_power(pool, b)

                norm_x.take_power(pool, 0)
                second_power(0)
                norm_x.take_power(pool, 1)
                past(0)
                body(0, first=True)
                with pool.Fori(1, SEQS - 2) as b:
                    body(b)
                body(SEQS - 2, next_last=True)
                body(SEQS - 1, last=True)
                add(SEQS - 1)

            @block.scalar
            def _(act):
                def move_xT(b):
                    act.wait_ge(xT_moved, b + 1)
                    act.activation(xnT[:, 1:1 + TOK], xT_bank[:, :], ACT.Identity, scale=w["g1"][:, :],
                                   bias=w["b1"][:, :]).then_inc(xnT_done, 1)

                def gate_r(b):
                    act.wait_ge(kvr_done, 3 * b + 3)
                    act.activation(tanh_r[:, :], r_bank[:, :], ACT.Tanh, scale=0.5).then_inc(tanh_done, 1)

                def exponent(b, n):
                    act.wait_ge(args_done, 5 * b + 2 + n)
                    act.activation(exps[:, n, :], args[:, n, :], ACT.Exp).then_inc(exps_done, 1)

                def move_x2T(b):
                    act.wait_ge(x2T_moved, b + 1)
                    act.activation(xn2T[:, 1:1 + TOK], x1_bank[:, :], ACT.Identity, scale=w["g2"][:, :],
                                   bias=w["b2"][:, :]).then_inc(xn2T_done, 1)

                def squares(b):
                    for f in range(FCH):
                        n = b * FCH + f
                        act.wait_ge(f_done, n + 1)
                        act.activation(relu[:, f, :], f_bank[f % 2][:, :], ACT.Relu).then_inc(relu_done, 1)
                        act.wait_ge(relu_done, n + 1)
                        act.activation(square[:, f, :], relu[:, f, :], ACT.Square).then_inc(square_done, 1)

                def gate_g(b):
                    act.wait_ge(gate_projected, b + 1)
                    act.activation(tanh_g[:, :], x1_bank[:, :], ACT.Tanh, scale=0.5).then_inc(tanh_g_done, 1)

                def body(b, last=False):
                    move_x2T(b)
                    if not last:
                        move_xT(b + 1)
                        exponent(b + 1, 0)
                        gate_r(b + 1)
                        exponent(b + 1, 1)
                    gate_g(b)
                    if not last:
                        exponent(b + 1, 2)
                        exponent(b + 1, 3)
                    squares(b)

                act.wait_ge(weights_loaded, weights_count)
                act.activation(exp_decay[:, :], w["decay"][:, :], ACT.Exp).then_inc(decay_done, 1)
                move_xT(0)
                gate_r(0)
                for n in range(4):
                    exponent(0, n)
                with act.Fori(0, SEQS - 1) as b:
                    body(b)
                body(SEQS - 1, last=True)

            @block.tensor
            def _(pe):
                def move_x(b):
                    pe.wait_ge(xhat_done, b + 1)
                    for t in range(TILES):
                        mm = pe.transpose(xT_bank[:, t * P:(t + 1) * P], xhat[:, t, :], ident[:, :])
                    mm.then_inc(xT_moved, 1)

                def project_kvr(b):
                    for n, (name, bank, src) in enumerate((("wk", k_bank, xk), ("wv", v_bank, xv), ("wr", r_bank, xr))):
                        pe.wait_ge(mixed, 3 * b + n + 1)
                        pe.matmul(bank[:, :], w[name][:, :], src[:, :], start=True, stop=True)\
                          .then_inc(kvr_done, 1)

                def project_x1(b):
                    pe.wait_ge(gated_done, b + 1)
                    for t in range(TILES):
                        mm = pe.matmul(x1_bank[:, t * P:(t + 1) * P], gated[:, t * P:(t + 1) * P],
                                       w["wo"][:, :], start=True, stop=True)
                    mm.then_inc(x1_projected, 1)

                def move_x1(b):
                    for t in range(TILES):
                        pe.wait_ge(xhat2_done, 4 * b + t + 1)
                        mm = pe.transpose(x1_bank[:, t * P:(t + 1) * P], xhat2[:, t, :], ident[:, :])
                    mm.then_inc(x2T_moved, 1)

                def ffn(b):
                    pe.wait_ge(mixed2, 2 * b + 1)
                    for t in range(TILES):
                        mm = pe.matmul(x1_bank[:, t * P:(t + 1) * P], xr2[:, t * P:(t + 1) * P],
                                       w["wr_ffn"][:, :], start=True, stop=True)
                    mm.then_inc(gate_projected, 1)
                    pe.wait_ge(mixed2, 2 * b + 2)
                    for f in range(FCH + 1):
                        if f < FCH:
                            if f >= 2:
                                pe.wait_ge(relu_done, b * FCH + f - 1)
                            pe.matmul(f_bank[f % 2][:, :], w["wk_ffn"][:, f * P:(f + 1) * P], xk2[:, :],
                                      start=True, stop=True).then_inc(f_done, 1)
                        if f >= 1:
                            pe.wait_ge(square_done, b * FCH + f)
                            for t in range(TILES):
                                mm = pe.matmul(kv_bank[:, t * P:(t + 1) * P],
                                               square[:, f - 1, t * P:(t + 1) * P], w["wv_ffn"][:, f - 1, :],
                                               start=(f == 1 and t == 0), stop=(f == FCH),
                                               skip_group_check=True)
                    mm.then_inc(kv_done, 1)

                def body(b, last=False):
                    project_x1(b)
                    move_x1(b)
                    if not last:
                        move_x(b + 1)
                    if not last:
                        project_kvr(b + 1)
                    ffn(b)

                pe.wait_ge(weights_loaded, weights_count)
                move_x(0)
                project_kvr(0)
                with pe.Fori(0, SEQS - 1) as b:
                    body(b)
                body(SEQS - 1, last=True)

            @block.vector
            def _(dve):
                def second_variance(b):
                    dve.wait_ge(norm_x.rstd_done, b + 1)
                    dve.tensor_tensor(var_2[:, :], norm_x.rstd[:, :], norm_x.rstd[:, :], ALU.mult)\
                       .then_inc(var_2_done, 1)
                    dve.wait_ge(var_2_done, 3 * b + 1)
                    dve.tensor_tensor(var_2[:, :], var_2[:, :], norm_x.moments[:, :, 1], ALU.mult)\
                       .then_inc(var_2_done, 1)
                    dve.wait_ge(var_2_done, 3 * b + 2)
                    dve.tensor_scalar(var_2[:, :], var_2[:, :], EPS, None, ALU.add).then_inc(var_2_done, 1)

                def scale_xs(b):
                    dve.wait_ge(rstd_2_done, b + 1)
                    dve.wait_ge(xs_done, 4 * b + 4)
                    dve.tensor_tensor(xhat[:, :, :], xs[:, :, :],
                                      rstd_2[:, :].rearrange("p (t a) -> p t a", a=1).to_broadcast([P, TILES, C]),
                                      ALU.mult).then_inc(xhat_done, 1)

                def mix(b):
                    dve.wait_ge(xnT_done, b + 1)
                    dve.tensor_tensor(step[:, :], xnT[:, 1:1 + TOK], xnT[:, 0:TOK], ALU.subtract)\
                       .then_inc(step_done, 1)
                    dve.wait_ge(step_done, b + 1)
                    for out, name in ((xk, "mix_k"), (xv, "mix_v"), (xr, "mix_r")):
                        dve.scalar_tensor_tensor(out=out[:, :], in0=step[:, :], scalar=w[name][:, :],
                                                 in1=xnT[:, 0:TOK], op0=ALU.mult, op1=ALU.add)\
                           .then_inc(mixed, 1)

                def recurrence_args(b):
                    k, u = k_bank, w["first"][:, :]
                    dve.wait_ge(kvr_done, 3 * b + 1)
                    dve.tensor_tensor_scan(top[:, 1:1 + TOK], decay[:, :].to_broadcast([C, TOK]), k[:, :],
                                           START, ALU.add, ALU.max).then_inc(top_done, 1)
                    dve.wait_ge(top_done, b + 1)
                    dve.scalar_tensor_tensor(out=now_max[:, :], in0=k[:, :], scalar=u, in1=top[:, 0:TOK],
                                             op0=ALU.add, op1=ALU.max).then_inc(args_done, 1)
                    dve.scalar_tensor_tensor(out=args[:, 0, :], in0=top[:, 0:TOK], scalar=decay[:, :],
                                             in1=top[:, 1:1 + TOK], op0=ALU.add, op1=ALU.subtract)\
                       .then_inc(args_done, 1)
                    dve.tensor_tensor(args[:, 1, :], k[:, :], top[:, 1:1 + TOK], ALU.subtract)\
                       .then_inc(args_done, 1)
                    dve.wait_ge(args_done, 5 * b + 1)
                    dve.tensor_tensor(args[:, 2, :], top[:, 0:TOK], now_max[:, :], ALU.subtract)\
                       .then_inc(args_done, 1)
                    dve.scalar_tensor_tensor(out=args[:, 3, :], in0=k[:, :], scalar=u, in1=now_max[:, :],
                                             op0=ALU.add, op1=ALU.subtract).then_inc(args_done, 1)

                def recurrence(b):
                    dve.wait_ge(exps_done, 4 * b + 2)
                    dve.tensor_tensor_scan(denom[:, 1:1 + TOK], exps[:, 0, :], exps[:, 1, :], 0.0,
                                           ALU.mult, ALU.add).then_inc(scans, 1)
                    dve.wait_ge(kvr_done, 3 * b + 2)
                    dve.tensor_tensor(enter_v[:, :], exps[:, 1, :], v_bank[:, :], ALU.mult).then_inc(scans, 1)
                    dve.wait_ge(scans, 3 * b + 2)
                    dve.tensor_tensor_scan(numer[:, 1:1 + TOK], exps[:, 0, :], enter_v[:, :], 0.0,
                                           ALU.mult, ALU.add).then_inc(scans, 1)
                    dve.wait_ge(exps_done, 4 * b + 4)
                    dve.tensor_tensor(now_v[:, :], exps[:, 3, :], v_bank[:, :], ALU.mult).then_inc(now_v_done, 1)

                def output(b):
                    dve.wait_ge(past_done, 2 * b + 1)
                    dve.tensor_tensor(sum_1[:, :], past_1[:, :], exps[:, 3, :], ALU.add).then_inc(sums_done, 1)
                    dve.wait_ge(sums_done, 4 * b + 1)
                    dve.reciprocal(sum_inv[:, :], sum_1[:, :]).then_inc(sums_done, 1)
                    dve.wait_ge(past_done, 2 * b + 2)
                    dve.wait_ge(now_v_done, b + 1)
                    dve.tensor_tensor(sum_v[:, :], past_v[:, :], now_v[:, :], ALU.add).then_inc(sums_done, 1)
                    dve.wait_ge(sums_done, 4 * b + 3)
                    dve.tensor_tensor(wkv[:, :], sum_v[:, :], sum_inv[:, :], ALU.mult).then_inc(sums_done, 1)
                    dve.wait_ge(sums_done, 4 * b + 4)
                    dve.wait_ge(tanh_done, b + 1)
                    dve.scalar_tensor_tensor(out=gated[:, :], in0=tanh_r[:, :], scalar=1.0, in1=wkv[:, :],
                                             op0=ALU.add, op1=ALU.mult).then_inc(gated_done, 1)

                def add_x1(b):
                    dve.wait_ge(x1_projected, b + 1)
                    dve.scalar_tensor_tensor(out=x1[:, :, :], in0=tiles(x1_bank[:, :]), scalar=0.5,
                                             in1=xs[:, :, :], op0=ALU.mult, op1=ALU.add).then_inc(x1_done, 1)

                def mix2(b):
                    dve.wait_ge(xn2T_done, b + 1)
                    dve.tensor_tensor(step2[:, :], xn2T[:, 1:1 + TOK], xn2T[:, 0:TOK], ALU.subtract)\
                       .then_inc(step2_done, 1)
                    dve.wait_ge(step2_done, b + 1)
                    for out, name in ((xr2, "ffn_mix_r"), (xk2, "ffn_mix_k")):
                        dve.scalar_tensor_tensor(out=out[:, :], in0=step2[:, :], scalar=w[name][:, :],
                                                 in1=xn2T[:, 0:TOK], op0=ALU.mult, op1=ALU.add)\
                           .then_inc(mixed2, 1)

                def add_ffn(b):
                    dve.wait_ge(kv_done, b + 1)
                    dve.wait_ge(tanh_g_done, b + 1)
                    dve.scalar_tensor_tensor(out=kv_gated[:, :], in0=tanh_g[:, :], scalar=1.0, in1=kv_bank[:, :],
                                             op0=ALU.add, op1=ALU.mult).then_inc(kv_gated_done, 1)
                    dve.wait_ge(kv_gated_done, b + 1)
                    dve.scalar_tensor_tensor(out=out3[:, :, :], in0=tiles(kv_gated[:, :]), scalar=0.5,
                                             in1=x1[:, :, :], op0=ALU.mult, op1=ALU.add).then_inc(out3_done, 1)

                def apply_3(b, first):
                    if not first:
                        dve.wait_ge(x_added, b)
                    norm_3.apply(dve, b, lambda t: yn[:, t, :], lambda t: out3[:, t, :], yn_done)

                def body(b, first=False, last=False, second=False, next_last=False):
                    add_x1(b)
                    dve.wait_ge(x1_done, b + 1)
                    norm_1.take_moments(dve, b, lambda t: x1[:, t, :])
                    if not last:
                        second_variance(b + 1)
                    if not first:
                        apply_3(b - 1, second)
                    if not last:
                        norm_x.apply(dve, b + 1, lambda t: xs[:, t, :], x_tile(b + 1), xs_done)
                    norm_1.apply(dve, b, lambda t: xhat2[:, t, :], lambda t: x1[:, t, :], xhat2_done)
                    if not last:
                        scale_xs(b + 1)
                    mix2(b)
                    if not last:
                        mix(b + 1)
                    if not last and not next_last:
                        norm_x.take_moments(dve, b + 2, x_tile(b + 2))
                    if not last:
                        recurrence_args(b + 1)
                        recurrence(b + 1)
                        output(b + 1)
                    add_ffn(b)
                    dve.wait_ge(out3_done, b + 1)
                    norm_3.take_moments(dve, b, lambda t: out3[:, t, :])

                for col, value in ((xnT, 0.0), (xn2T, 0.0), (top, START), (numer, 0.0), (denom, 0.0)):
                    dve.memset(col[:, 0:1], value).then_inc(filled, 1)
                dve.wait_ge(filled, 5)
                dve.wait_ge(decay_done, 1)
                dve.tensor_scalar(decay[:, :], exp_decay[:, :], -1.0, None, ALU.mult).then_inc(decay_done, 1)
                norm_x.take_moments(dve, 0, x_tile(0))
                second_variance(0)
                norm_x.apply(dve, 0, lambda t: xs[:, t, :], x_tile(0), xs_done)
                scale_xs(0)
                mix(0)
                norm_x.take_moments(dve, 1, x_tile(1))
                dve.wait_ge(decay_done, 2)
                recurrence_args(0)
                recurrence(0)
                output(0)
                body(0, first=True)
                body(1, second=True)
                with dve.Fori(2, SEQS - 2) as b:
                    body(b)
                body(SEQS - 2, next_last=True)
                body(SEQS - 1, last=True)
                apply_3(SEQS - 1, False)


INPUTS = ['L0_attn_x', 'L0_attn_W_qkv', 'L0_attn_W_proj', 'L0_attn_b_proj', 'L0_ffn_router', 'L0_ffn_experts_gate',
          'L0_ffn_experts_up', 'L0_ffn_experts_down', 'L0_ffn_shared_gate', 'L0_ffn_shared_up', 'L0_ffn_shared_down',
          'L1_attn_ln1_g', 'L1_attn_ln1_b', 'L1_attn_ln2_g', 'L1_attn_ln2_b', 'L1_attn_att_mix_k', 'L1_attn_att_mix_v',
          'L1_attn_att_mix_r', 'L1_attn_time_decay', 'L1_attn_time_first', 'L1_attn_Wk', 'L1_attn_Wv', 'L1_attn_Wr',
          'L1_attn_Wo', 'L1_attn_ffn_mix_k', 'L1_attn_ffn_mix_r', 'L1_attn_Wk_ffn', 'L1_attn_Wr_ffn', 'L1_attn_Wv_ffn',
          'L1_ffn_router_W', 'L1_ffn_router_b', 'L1_ffn_sW1', 'L1_ffn_sb1', 'L1_ffn_sW2', 'L1_ffn_sb2', 'L1_ffn_eW1',
          'L1_ffn_eb1', 'L1_ffn_eW2', 'L1_ffn_eb2']


def sandwich_kernel(nc, a, out):
    E0, D0, E1 = 8, 64, 15

    with ExitStack() as ctx:
        def sb(name, shape, dt=FP32):
            return ctx.enter_context(nc.sbuf_tensor(name, shape, dt))

        def sem(name):
            return ctx.enter_context(nc.semaphore(name))

        x = sb("x_tokens", [P, SEQS * TILES, C])
        ident = sb("ident", [P, P])
        ident_bf = sb("ident_bf", [P, P], BF16)
        minus_half = sb("minus_half", [P, TILES])
        x_loaded = sem("x_loaded")
        constants = sem("constants")
        x_stored = sem("x_stored")
        weights_0a, weights_0f, weights_1a, weights_1f = (sem("weights_" + n) for n in ("0a", "0f", "1a", "1f"))
        x_view = a['L0_attn_x'].rearrange("b (t p) c -> p (b t) c", p=P)
        out_view = out.rearrange("b (t p) c -> p (b t) c", p=P)

        def row(v):
            return v.rearrange("(a c) -> a c", a=1)

        def column(v):
            return v.rearrange("(c a) -> c a", a=1)

        def load(queue, items, done):
            for dst, src in items:
                queue.dma_start(dst, src).then_inc(done, 16)
            return 16 * len(items)

        w_qkv, w_proj, b_proj = sb("w_qkv", [C, 3 * C]), sb("w_proj", [C, C]), sb("b_proj", [P, C])
        w0 = {"router": sb("router0", [C, E0]), "gate": sb("gate0", [C, E0 * D0]), "up": sb("up0", [C, E0 * D0]),
              "down": sb("down0", [P, E0 * D0 // P, C]), "shared_gate": sb("shared_gate", [C, P]),
              "shared_up": sb("shared_up", [C, P]), "shared_down": sb("shared_down", [P, C])}
        columns = ("g1", "b1", "g2", "b2", "mix_k", "mix_v", "mix_r", "decay", "first", "ffn_mix_k", "ffn_mix_r")
        w1 = {n: sb("rwkv_" + n, [C, 1]) for n in columns}
        w1.update({n: sb("rwkv_" + n, [C, C]) for n in ("wk", "wv", "wr", "wo", "wr_ffn")})
        w1["wk_ffn"] = sb("rwkv_wk_ffn", [C, 4 * C])
        w1["wv_ffn"] = sb("rwkv_wv_ffn", [P, 4, C])
        w2 = {"router": sb("router1", [C, E1]), "b_router": sb("b_router", [P, E1]), "w1": sb("w1", [C, E1 + 1, P]),
              "b1": sb("b1", [P, E1 + 1]), "w2": sb("w2", [P, E1 + 1, C]), "b2_rows": sb("b2_rows", [P, C])}

        items_0a = [(w_qkv[:, :], a['L0_attn_W_qkv']), (w_proj[:, :], a['L0_attn_W_proj']),
                    (b_proj[:, :], row(a['L0_attn_b_proj']).to_broadcast([P, C]))]
        items_0f = [(w0["router"][:, :], a['L0_ffn_router']),
                    (w0["gate"][:, :].rearrange("h (e d) -> h e d", d=D0), a['L0_ffn_experts_gate'].rearrange("e h d -> h e d")),
                    (w0["up"][:, :].rearrange("h (e d) -> h e d", d=D0), a['L0_ffn_experts_up'].rearrange("e h d -> h e d")),
                    (w0["down"][:, :, :], a['L0_ffn_experts_down'].rearrange("(q e) d h -> (e d) q h", e=2)),
                    (w0["shared_gate"][:, :], a['L0_ffn_shared_gate']), (w0["shared_up"][:, :], a['L0_ffn_shared_up']),
                    (w0["shared_down"][:, :], a['L0_ffn_shared_down'])]
        vectors = dict(g1='ln1_g', b1='ln1_b', g2='ln2_g', b2='ln2_b', decay='time_decay', first='time_first')
        mixes = dict(mix_k='att_mix_k', mix_v='att_mix_v', mix_r='att_mix_r', ffn_mix_k='ffn_mix_k', ffn_mix_r='ffn_mix_r')
        matrices = dict(wk='Wk', wv='Wv', wr='Wr', wo='Wo', wr_ffn='Wr_ffn', wk_ffn='Wk_ffn')
        items_1a = [(w1[n][:, :], column(a['L1_attn_' + v])) for n, v in vectors.items()]
        items_1a += [(w1[n][:, :], a['L1_attn_' + v].rearrange("a b c -> c (a b)")) for n, v in mixes.items()]
        items_1a += [(w1[n][:, :], a['L1_attn_' + v]) for n, v in matrices.items()]
        items_1a += [(w1["wv_ffn"][:, :, :], a['L1_attn_Wv_ffn'].rearrange("(f p) c -> p f c", p=P))]
        items_1f = [(w2["router"][:, :], a['L1_ffn_router_W']),
                    (w2["b_router"][:, :], row(a['L1_ffn_router_b']).to_broadcast([P, E1])),
                    (w2["w1"][:, 1:, :], a['L1_ffn_eW1'].rearrange("e d h -> d e h")),
                    (w2["w1"][:, 0, :], a['L1_ffn_sW1']),
                    (w2["w2"][:, 1:, :], a['L1_ffn_eW2'].rearrange("e h d -> h e d")),
                    (w2["w2"][:, 0, :], a['L1_ffn_sW2']),
                    (w2["b1"][:, 1:], a['L1_ffn_eb1']), (w2["b1"][:, 0:1], column(a['L1_ffn_sb1'])),
                    (w2["b2_rows"][96:97, :], row(a['L1_ffn_sb2']))]
        items_1f += [(w2["b2_rows"][i * E1:(i + 1) * E1, :], a['L1_ffn_eb2']) for i in range(3)]

        with nc.Block() as block:
            @block.sync
            def _(sp):
                sp.dma_start(x[:, 0:TILES, :], x_view[:, 0:TILES, :]).then_inc(x_loaded, 16)
                load(sp, items_0a, weights_0a)
                sp.dma_start(x[:, TILES:, :], x_view[:, TILES:, :]).then_inc(x_loaded, 16)
                load(sp, items_0f, weights_0f)
                sp.wait_ge(constants, 6)
                load(sp, items_1f, weights_1f)

            @block.scalar
            def _(act):
                load(act, items_1a, weights_1a)

            @block.gpsimd
            def _(pool):
                pool.memset(minus_half[:, :], -0.5).then_inc(constants, 1)
                pool.memset(ident[:, :], 0.0).then_inc(constants, 1)
                pool.memset(ident_bf[:, :], 0.0).then_inc(constants, 1)
                pool.wait_ge(constants, 3)
                for m in (ident, ident_bf):
                    pool.affine_select(out=m[:, :], in_=m[:, :], compare_op=ALU.not_equal, fill=1.0,
                                       base=0, pattern=[[-1, P]], channel_multiplier=1).then_inc(constants, 1)
                pool.memset(w2["b2_rows"][:, :], 0.0).then_inc(constants, 1)

        attention_layer(nc, x, ident, ident_bf, minus_half, w_qkv, w_proj, b_proj, x_loaded, weights_0a,
                        16 * len(items_0a))
        swiglu_experts_layer(nc, x, x_loaded, ident, ident_bf, minus_half, w0, weights_0f, 16 * len(items_0f))
        rwkv_layer(nc, x, x_loaded, ident, minus_half, w1, weights_1a, 16 * len(items_1a))
        relu_experts_layer(nc, x, x_loaded, ident, ident_bf, minus_half, w2, weights_1f, 16 * len(items_1f))
        with nc.Block() as block:
            @block.sync
            def _(sp):
                sp.dma_start(out_view, x[:, :, :]).then_inc(x_stored, 16)
                sp.wait_ge(x_stored, 16)


def lay_out(inputs):
    HEADS, D = 16, 8
    arrays = {n: np.asarray(inputs[n]) for n in INPUTS}
    w = arrays['L0_attn_W_qkv']
    q, k = (w[:, i * C:(i + 1) * C].reshape(C, HEADS, D).transpose(0, 2, 1).reshape(C, C) for i in range(2))
    arrays['L0_attn_W_qkv'] = np.concatenate([q, k, w[:, 2 * C:]], axis=1)
    for n in ('Wk', 'Wv', 'Wr', 'Wo', 'Wk_ffn', 'Wr_ffn', 'Wv_ffn'):
        arrays['L1_attn_' + n] = arrays['L1_attn_' + n].T
    arrays['L1_ffn_eb1'] = arrays['L1_ffn_eb1'].T
    return {n: np.ascontiguousarray(v) for n, v in arrays.items()}


def kernel(**inputs):
    import concourse.bacc as bacc
    from concourse.bass_utils import run_bass_kernel_spmd

    nc = bacc.Bacc("TRN2", target_bir_lowering=False, num_devices=1)
    arrays = lay_out(inputs)
    a = {n: nc.dram_tensor("in_" + n, v.shape, mybir.dt.from_np(v.dtype), kind="ExternalInput").ap()
         for n, v in arrays.items()}
    out = nc.dram_tensor("out", (SEQS, TOK, C), FP32, kind="ExternalOutput").ap()
    sandwich_kernel(nc, a, out)
    result = run_bass_kernel_spmd(nc, [{"in_" + n: v for n, v in arrays.items()}], core_ids=[0])
    return result.results[0]["out"]
```

```python
import numpy as np
import concourse.bass as bass
from concourse import mybir
from contextlib import ExitStack

FP32 = mybir.dt.float32
BF16 = mybir.dt.bfloat16
FP32R = mybir.dt.float32r
ALU = mybir.AluOpType
ACT = mybir.ActivationFunctionType
AX = mybir.AxisListType

P = 128
SEQS = 8
TILES = 4
TOK = TILES * P
C = 128
EPS = 1e-5
X_LOAD = 16
MASKED = -1e30


class Norm:

    def __init__(self, sb, sem, name, minus_half, x_loaded, eps=EPS):
        self.stats = sb(f"{name}_stats", [P, TILES, 6], FP32)
        self.moments = sb(f"{name}_moments", [P, TILES, 2], FP32)
        self.var_eps = sb(f"{name}_var_eps", [P, TILES], FP32)
        self.rstd = sb(f"{name}_rstd", [P, TILES], FP32)
        self.minus_half = minus_half
        self.eps = eps
        self.x_loaded = x_loaded
        self.taken = sem(f"{name}_taken")
        self.var_done = sem(f"{name}_var_done")
        self.rstd_done = sem(f"{name}_rstd_done")

    def take_moments(self, dve, b, tile):
        for t in range(TILES):
            dve.bn_stats(self.stats[:, t, :], tile(t)).then_inc(self.taken, 1)
        count = dve.to_reg(2 * TILES * b + TILES)
        dve.wait_ge(self.x_loaded, X_LOAD)
        dve.wait_ge(self.taken, count)
        for t in range(TILES):
            dve.bn_aggr(self.moments[:, t, :], self.stats[:, t, :]).then_inc(self.taken, 1)
        dve.wait_ge(self.taken, 2 * TILES * b + 2 * TILES)
        dve.tensor_scalar(self.var_eps[:, :], self.moments[:, :, 1], self.eps, None, ALU.add)\
           .then_inc(self.var_done, 1)

    def take_power(self, pool, b):
        pool.wait_ge(self.var_done, b + 1)
        pool.tensor_tensor(self.rstd[:, :], self.var_eps[:, :], self.minus_half[:, :], ALU.pow)\
            .then_inc(self.rstd_done, 1)

    def apply(self, dve, b, out, tile, done):
        dve.wait_ge(self.rstd_done, b + 1)
        for t in range(TILES):
            dve.tensor_scalar(out(t), tile(t), self.moments[:, t, 0:1], self.rstd[:, t:t + 1],
                              ALU.subtract, ALU.mult).then_inc(done, 1)


class NormOnAct(Norm):

    def __init__(self, sb, sem, name, minus_half, x_loaded, applied, eps=EPS):
        super().__init__(sb, sem, name, minus_half, x_loaded, eps)
        self.minus_mean = sb(f"{name}_minus_mean", [P, TILES], FP32)
        self.shift = sb(f"{name}_shift", [P, TILES], FP32)
        self.applied = applied

    def take_moments(self, dve, b, tile):
        if not isinstance(b, int) or b > 0:
            dve.wait_ge(self.rstd_done, 2 * b)
        super().take_moments(dve, b, tile)
        dve.tensor_scalar(self.minus_mean[:, :], self.moments[:, :, 0], -1.0, None, ALU.mult)\
           .then_inc(self.var_done, 1)

    def take_power(self, pool, b):
        pool.wait_ge(self.var_done, 2 * b + 2)
        if not isinstance(b, int) or b > 0:
            pool.wait_ge(self.applied, TILES * b)
        pool.tensor_tensor(self.rstd[:, :], self.var_eps[:, :], self.minus_half[:, :], ALU.pow)\
            .then_inc(self.rstd_done, 1)
        pool.wait_ge(self.rstd_done, 2 * b + 1)
        pool.tensor_tensor(self.shift[:, :], self.minus_mean[:, :], self.rstd[:, :], ALU.mult)\
            .then_inc(self.rstd_done, 1)

    def apply(self, act, b, out, tile, tiles=range(TILES)):
        act.wait_ge(self.rstd_done, 2 * b + 2)
        for t in tiles:
            act.activation(out(t), tile(t), ACT.Identity, scale=self.rstd[:, t:t + 1],
                           bias=self.shift[:, t:t + 1]).then_inc(self.applied, 1)


def attention_layer(nc, banks, x, x_first, x_loaded, ident, ident_bf, minus_half, w_qkv, w_proj, b_proj,
                    weights_loaded, weights_count, constants, constants_count,
                    fill_constants, load_first, load_next, load_last):
    HEADS, D = 16, 8
    GROUP = TOK // P
    GROUPS = HEADS // GROUP
    UNITS = TILES * GROUPS
    SET = HEADS // 2
    TERMS_Q = ((0, 1, 4), (2, 3), (5,))
    TERMS_K = ((0, 2, 5), (1, 3), (4,))
    MAX_ROW = 64
    SCALE = float(D) ** -0.5
    LAG = 2
    HALF = UNITS // 2
    LATE = 8
    PROBS = 4

    with ExitStack() as ctx:
        def sb(name, shape, dt):
            return ctx.enter_context(nc.sbuf_tensor("at_" + name, shape, dt))

        def sem(name):
            return ctx.enter_context(nc.semaphore("at_" + name))

        score_bank, key_bank, out_bank = banks[0:2], banks[2:4], banks[4:6]
        xqv_bank, ky_bank = banks[6:8]

        xn = sb("xn", [P, TILES, C], FP32)
        xnT = sb("xnT", [C, TOK], FP32)
        q_parts = [sb(f"q{i + 1}", [C, TOK], BF16) for i in range(3)]
        k_parts = [sb(f"k{i + 1}", [C, TOK], BF16) for i in range(3)]
        q_rest = sb("q_rest", [C, TOK], FP32)
        k_rest = sb("k_rest", [C, TOK], FP32)
        q_rows = [sb(f"q_rows{i}", [P, HEADS, TOK], BF16) for i in range(2)]
        k_rows = [sb(f"k_rows{i}", [P, HEADS, TOK], BF16) for i in range(2)]
        zero_rows = sb("zero_rows", [3, P], BF16)
        v_wide = [sb(f"v_wide{i}", [P, TILES, HEADS * P], FP32) for i in range(2)]
        probs = sb("probs", [P, PROBS, TOK], FP32)
        sums = sb("sums", [P, P], FP32)
        outT = sb("outT", [C, TOK], FP32)
        neg_max = sb("neg_max", [P, TILES, HEADS], FP32)
        max_rest = sb("max_rest", [P, TILES, HEADS], FP32)
        max_parts = sb("max_parts", [P, TILES, 3, HEADS], BF16)
        max_partsT = sb("max_partsT", [3 * HEADS, TOK], BF16)
        mask = sb("mask", [P, P], BF16)
        y = sb("y", [P, TILES, C], FP32)
        norm_in = Norm(sb, sem, "norm_in", minus_half, x_first)
        norm_out = Norm(sb, sem, "norm_out", minus_half, x_loaded)

        filled_even = sem("filled_even")
        filled_odd = sem("filled_odd")
        mask_zeroed = sem("mask_zeroed")
        k_zeroed = sem("k_zeroed")
        k_odd_zeroed = sem("k_odd_zeroed")
        v_zeroed = sem("v_zeroed")
        v_filled = sem("v_filled")
        xn_done = sem("xn_done")
        xT_moved = sem("xT_moved")
        xnT_done = sem("xnT_done")
        qk_projected = sem("qk_projected")
        v_projected = sem("v_projected")
        part1_done = sem("part1_done")
        rest_done = sem("rest_done")
        part2_done = sem("part2_done")
        part3_done = sem("part3_done")
        rows_loaded = sem("rows_loaded")
        v_done = sem("v_done")
        scored = sem("scored")
        max_done = sem("max_done")
        max_split = sem("max_split")
        max_moved = sem("max_moved")
        maxT_done = sem("maxT_done")
        max_loaded = sem("max_loaded")
        key_scored = sem("key_scored")
        exp_done = sem("exp_done")
        probs_done = sem("probs_done")
        weighed = sem("weighed")
        sums_done = sem("sums_done")
        inverted = sem("inverted")
        outT_done = sem("outT_done")
        proj_done = sem("proj_done")
        y_done = sem("y_done")
        yn_done = sem("yn_done")
        x_added = sem("x_added")
        EVEN_FILLS, ODD_FILLS = 4, 2
        BF16_ONES = float(np.uint32(0x3f803f80).view(np.float32))

        def tile_of(ap, t):
            return ap[:, t * P:(t + 1) * P]

        def own_columns(wide, s, start):
            w = wide[:, :, s * SET * P + start:(s + 1) * SET * P]
            return bass.AP(w.tensor, w.offset, [w.ap[0], w.ap[1], [P + D, SET], [1, D]])

        with nc.Block() as block:

            @block.sync
            def _(sp):
                def send(parts, rows, terms):
                    for r in terms:
                        sp.dma_start(rows[r * D:(r + 1) * D, :, :], parts[:, :]).then_inc(rows_loaded, 16)

                def spread_early(b, p):
                    sp.wait_ge(part1_done, 2 * b + 1)
                    send(q_parts[0], q_rows[p], TERMS_Q[0])
                    sp.dma_start(q_rows[p][MAX_ROW:MAX_ROW + 3, :, :].rearrange("r h (t c) -> r (h t) c", t=TILES),
                                 zero_rows[:, :].rearrange("r (a c) -> r a c", a=1).to_broadcast([3, HEADS * TILES, P]))\
                      .then_inc(rows_loaded, 16)
                    sp.wait_ge(part1_done, 2 * b + 2)
                    send(k_parts[0], k_rows[p], TERMS_K[0])
                    sp.wait_ge(part2_done, 2 * b + 1)
                    send(q_parts[1], q_rows[p], TERMS_Q[1])
                    sp.wait_ge(part2_done, 2 * b + 2)
                    send(k_parts[1], k_rows[p], TERMS_K[1])

                def spread_late(b, p):
                    sp.wait_ge(part3_done, 2 * b + 1)
                    send(q_parts[2], q_rows[p], TERMS_Q[2])
                    sp.wait_ge(part3_done, 2 * b + 2)
                    send(k_parts[2], k_rows[p], TERMS_K[2])

                def send_max(b, p, half):
                    cols = slice(half * TOK // 2, (half + 1) * TOK // 2)
                    sp.wait_ge(maxT_done, 2 * b + half + 1)
                    for i in range(3):
                        sp.dma_start(q_rows[p][MAX_ROW + i:MAX_ROW + i + 1, :, cols],
                                     max_partsT[i * HEADS:(i + 1) * HEADS, cols])\
                          .then_inc(max_loaded, 16)

                def body(b, p, last=False):
                    if not last:
                        spread_early(b + 1, 1 - p)
                    if not last:
                        spread_late(b + 1, 1 - p)
                    send_max(b, p, 1)
                    if not last:
                        send_max(b + 1, 1 - p, 0)

                load_first(sp)
                sp.wait_ge(filled_even, EVEN_FILLS)
                spread_early(0, 0)
                spread_late(0, 0)
                send_max(0, 0, 0)
                sp.wait_ge(filled_odd, ODD_FILLS)
                body(0, 0)
                sp.wait_ge(constants, constants_count)
                load_next(sp)
                with sp.Fori(0, (SEQS - 2) // 2) as pair:
                    b = 2 * pair + 1
                    body(b, 1)
                    body(b + 1, 0)
                body(SEQS - 1, 1, last=True)
                load_last(sp)

            @block.gpsimd
            def _(pool):
                def fill_rows(rows, start, end, value, done):
                    pool.memset(rows[start:end, :, :].bitcast(FP32), value).then_inc(done, 1)

                fill_constants(pool)
                fill_rows(q_rows[0], 0, P, 0.0, filled_even)
                pool.memset(zero_rows[:, :], 0.0).then_inc(filled_even, 1)
                pool.memset(mask[:, :], 0.0).then_inc(mask_zeroed, 1)
                pool.wait_ge(mask_zeroed, 1)
                pool.affine_select(out=mask[:, :], in_=mask[:, :], compare_op=ALU.is_ge, fill=MASKED,
                                   base=0, pattern=[[-1, P]], channel_multiplier=1).then_inc(filled_even, 1)

                def third_part(b, n):
                    parts, rest = ((q_parts, q_rest), (k_parts, k_rest))[n]
                    pool.wait_ge(part2_done, 2 * b + n + 1)
                    pool.tensor_tensor(parts[2][:, :], rest[:, :], parts[1][:, :], ALU.subtract)\
                        .then_inc(part3_done, 1)

                def mask_probs(b, u):
                    count = pool.to_reg(b * UNITS + u + 1)
                    pool.wait_ge(mask_zeroed, 1)
                    pool.wait_ge(exp_done, count)
                    slot = probs[:, u % PROBS, :]
                    pool.affine_select(out=slot, in_=slot, compare_op=ALU.is_ge, fill=0.0, base=0,
                                       pattern=[[0, GROUP], [1, P]], channel_multiplier=-1)\
                        .then_inc(probs_done, 1)

                def add_y(b):
                    pool.wait_ge(yn_done, 4 * b + 4)
                    xs = x[:, bass.ds(4 * b, TILES), :]
                    pool.tensor_tensor(xs, xs, y[:, :, :], ALU.add).then_inc(x_added, 1)

                def body(b, first=False, last=False, next_last=False):
                    for u in range(UNITS):
                        mask_probs(b, u)
                        if not last and u in (3, 4):
                            third_part(b + 1, u - 3)
                        if not first and u == 7:
                            norm_out.take_power(pool, b - 1)
                        if not first and u == 11:
                            add_y(b - 1)
                        if not last and not next_last and u == 14:
                            norm_in.take_power(pool, b + 2)

                norm_in.take_power(pool, 0)
                fill_rows(k_rows[1], 0, P, 0.0, k_odd_zeroed)
                third_part(0, 0)
                third_part(0, 1)
                norm_in.take_power(pool, 1)
                fill_rows(q_rows[1], 0, P, 0.0, filled_odd)
                pool.wait_ge(k_odd_zeroed, 1)
                pool.wait_ge(filled_odd, 1)
                fill_rows(k_rows[1], MAX_ROW, MAX_ROW + 32, BF16_ONES, filled_odd)
                pool.wait_ge(filled_odd, ODD_FILLS)
                body(0, first=True)
                with pool.Fori(1, SEQS - 2) as b:
                    body(b)
                body(SEQS - 2, next_last=True)
                body(SEQS - 1, last=True)
                norm_out.take_power(pool, SEQS - 1)
                add_y(SEQS - 1)

            @block.scalar
            def _(act):
                qk_bank = (xqv_bank, ky_bank)

                def move_xT(b):
                    act.wait_ge(xT_moved, b + 1)
                    act.activation(xnT[:, :], xqv_bank[:, :], ACT.Copy).then_inc(xnT_done, 1)

                def first_part(b, n):
                    act.wait_ge(qk_projected, 2 * b + n + 1)
                    act.activation((q_parts, k_parts)[n][0][:, :], qk_bank[n][:, :], ACT.Copy)\
                       .then_inc(part1_done, 1)

                def second_part(b, n):
                    act.wait_ge(rest_done, 2 * b + n + 1)
                    act.activation((q_parts, k_parts)[n][1][:, :], (q_rest, k_rest)[n][:, :], ACT.Copy)\
                       .then_inc(part2_done, 1)

                def spread_v(b, p):
                    act.wait_ge(v_projected, b + 1)
                    for s in range(2):
                        v = xqv_bank[:, :].rearrange("p (t s c) -> p t s c", t=TILES, s=2)[:, :, s, :]
                        act.activation(own_columns(v_wide[p], s, 0), v.rearrange("p t (h d) -> p t h d", d=D), ACT.Copy)\
                           .then_inc(v_done, 1)

                def move_max(b, half):
                    cols = slice(half * TOK // 2, (half + 1) * TOK // 2)
                    act.wait_ge(max_moved, 2 * b + half + 1)
                    act.activation(max_partsT[:, cols], score_bank[0][:, :].bitcast(BF16)[0:3 * HEADS, cols], ACT.Copy)\
                       .then_inc(maxT_done, 1)

                def exps(b, u, first):
                    act.wait_ge(key_scored, b * UNITS + u + 1)
                    if not first or u >= PROBS:
                        act.wait_ge(weighed, b * UNITS + u + 1 - PROBS)
                    act.activation(probs[:, u % PROBS, :], key_bank[u % 2][:, :], ACT.Exp, scale=SCALE)\
                       .then_inc(exp_done, 1)

                def body(b, p, first=False, last=False):
                    for u in range(UNITS):
                        if not last and u == 0:
                            move_xT(b + 1)
                        exps(b, u, first)
                        if not last and u in (1, 2):
                            first_part(b + 1, u - 1)
                        if not last and u in (2, 3):
                            second_part(b + 1, u - 2)
                        if u == 5:
                            move_max(b, 1)
                        if not last and u == 6:
                            spread_v(b + 1, 1 - p)
                        if not last and u == 13:
                            move_max(b + 1, 0)

                act.memzero(v_wide[0][:, :, :]).then_inc(v_zeroed, 1)
                move_xT(0)
                for n in range(2):
                    first_part(0, n)
                for n in range(2):
                    second_part(0, n)
                act.wait_ge(v_zeroed, 1)
                spread_v(0, 0)
                act.memzero(v_wide[1][:, :, :]).then_inc(v_zeroed, 1)
                move_max(0, 0)
                act.wait_ge(v_zeroed, 2)
                body(0, 0, first=True)
                with act.Fori(0, (SEQS - 2) // 2) as pair:
                    b = 2 * pair + 1
                    body(b, 1)
                    body(b + 1, 0)
                body(SEQS - 1, 1, last=True)

            @block.tensor
            def _(pe):
                def move_x(b, first=False):
                    if not first:
                        pe.wait_ge(v_done, 2 * b)
                    for t in range(TILES):
                        pe.wait_ge(xn_done, 4 * b + t + 1)
                        mm = pe.transpose(tile_of(xqv_bank, t), xn[:, t, :], ident[:, :])
                    mm.then_inc(xT_moved, 1)

                def project_qk(b):
                    pe.wait_ge(xnT_done, b + 1)
                    for n, bank in enumerate((xqv_bank, ky_bank)):
                        pe.matmul(bank[:, :], w_qkv[:, n * C:(n + 1) * C], xnT[:, :],
                                  start=True, stop=True).then_inc(qk_projected, 1)

                def project_v(b):
                    pe.wait_ge(rest_done, 2 * b + 1)
                    for t in range(TILES):
                        mm = pe.matmul(tile_of(xqv_bank, t), tile_of(xnT, t), w_qkv[:, 2 * C:3 * C],
                                       start=True, stop=True)
                    mm.then_inc(v_projected, 1)

                def scores(b, p, u, first=False):
                    t, g = u // GROUPS, u % GROUPS
                    bank = score_bank[u % 2]
                    if u % HALF >= 2:
                        pe.wait_ge(max_done, b * UNITS + u - 1)
                    elif u % HALF == 0 and (u > 0 or not first):
                        pe.wait_ge(maxT_done, 2 * b + u // HALF)
                    pe.matmul(bank[:, :], ident_bf[:, :],
                              mask[:, :].rearrange("p (a k) -> p a k", a=1).to_broadcast([P, GROUP, P]),
                              start=True, stop=False, skip_group_check=True)
                    for j in range(GROUP):
                        h = g * GROUP + j
                        mm = pe.matmul(tile_of(bank, j), q_rows[p][:, h, t * P:(t + 1) * P],
                                       k_rows[p][:, h, t * P:(t + 1) * P], start=False, stop=True,
                                       skip_group_check=True)
                    mm.then_inc(scored, 1)

                def move_max(b, half):
                    count = pe.to_reg(8 * b + 4 * half + 4)
                    pe.wait_ge(weights_loaded, weights_count)
                    pe.wait_ge(max_split, count)
                    for t in range(half * TILES // 2, (half + 1) * TILES // 2):
                        mm = pe.transpose(score_bank[0][:, :].bitcast(BF16)[0:3 * HEADS, t * P:(t + 1) * P],
                                          max_parts[:, t, :, :].rearrange("p i h -> p (i h)"), ident_bf[:, :])
                    mm.then_inc(max_moved, 1)

                def key_scores(b, p, u, first):
                    t, g = u // GROUPS, u % GROUPS
                    if u % HALF == 0:
                        pe.wait_ge(max_loaded, 96 * b + 48 * (u // HALF + 1))
                    if not first or u >= 2:
                        pe.wait_ge(exp_done, b * UNITS + u - 1)
                    for j in range(GROUP):
                        h = g * GROUP + j
                        mm = pe.matmul(tile_of(key_bank[u % 2], j), k_rows[p][:, h, t * P:(t + 1) * P],
                                       q_rows[p][:, h, t * P:(t + 1) * P], start=True, stop=True)
                    mm.then_inc(key_scored, 1)

                def weigh(b, p, u, first=False):
                    t, g = u // GROUPS, u % GROUPS
                    pe.wait_ge(probs_done, b * UNITS + u + 1)
                    if u == 0:
                        pe.wait_ge(v_done, 2 * b + 2)
                    if g == 0 and (t >= 2 or not first):
                        pe.wait_ge(outT_done, b * 2 * TILES + 2 * (t - 1))
                    for j in range(GROUP):
                        h = g * GROUP + j
                        s = h // SET
                        mm = pe.matmul(tile_of(out_bank[t % 2], s), v_wide[p][:, t, h * P:(h + 1) * P],
                                       probs[:, u % PROBS, j * P:(j + 1) * P],
                                       start=(h % SET == 0), stop=(h % SET == SET - 1))
                    mm.then_inc(weighed, 1)

                def project_out(b, last=False):
                    if not last:
                        pe.wait_ge(rest_done, 2 * b + 6)
                    pe.wait_ge(outT_done, 2 * TILES * b + 2 * TILES)
                    for t in range(TILES):
                        mm = pe.matmul(tile_of(ky_bank, t), tile_of(outT, t), w_proj[:, :],
                                       start=True, stop=True)
                    mm.then_inc(proj_done, 1)

                def body(b, p, first=False, last=False):
                    for u in range(UNITS):
                        if not last and u == 0:
                            move_x(b + 1)
                        key_scores(b, p, u, first)
                        if u < HALF // 2:
                            scores(b, p, HALF + 2 * u)
                            scores(b, p, HALF + 2 * u + 1)
                        if not last and u == 1:
                            project_qk(b + 1)
                        if not last and u == 4:
                            project_v(b + 1)
                        if not first and u == 4:
                            project_out(b - 1, last)
                        if u == 5:
                            move_max(b, 1)
                        if u >= LAG:
                            weigh(b, p, u - LAG, first)
                        elif not first:
                            weigh(b - 1, 1 - p, UNITS - LAG + u)
                        if not last and LATE <= u < LATE + HALF // 2:
                            if u == LATE:
                                pe.wait_ge(rows_loaded, 208 * b + 416)
                            scores(b + 1, 1 - p, 2 * (u - LATE))
                            scores(b + 1, 1 - p, 2 * (u - LATE) + 1)
                        if not last and u == 13:
                            move_max(b + 1, 0)

                pe.wait_ge(constants, constants_count)
                move_x(0, first=True)
                pe.wait_ge(weights_loaded, weights_count)
                project_qk(0)
                project_v(0)
                pe.wait_ge(filled_even, EVEN_FILLS)
                pe.wait_ge(rows_loaded, 208)
                for u in range(HALF):
                    scores(0, 0, u, first=True)
                move_max(0, 0)
                pe.wait_ge(v_filled, 1)
                body(0, 0, first=True)
                pe.wait_ge(v_filled, 2)
                with pe.Fori(0, (SEQS - 2) // 2) as pair:
                    b = 2 * pair + 1
                    body(b, 1)
                    body(b + 1, 0)
                body(SEQS - 1, 1, last=True)
                for u in range(UNITS - LAG, UNITS):
                    weigh(SEQS - 1, 1, u)
                project_out(SEQS - 1, last=True)

            @block.vector
            def _(dve):
                def fill_v(i):
                    dve.wait_ge(v_zeroed, i + 1)
                    for s in range(2):
                        for t in range(TILES):
                            last = dve.memset(own_columns(v_wide[i], s, P // 2)[:, t, :, :], 1.0)
                    last.then_inc(v_filled, 1)

                def x_tile(b):
                    return lambda t: x[:, bass.ds(4 * b + t, 1), :].rearrange("p a c -> p (a c)")

                def apply_in(b, first=False):
                    if not first:
                        dve.wait_ge(xT_moved, b)
                    norm_in.apply(dve, b, lambda t: xn[:, t, :], x_tile(b), xn_done)

                def rest(b, n):
                    dve.wait_ge(part1_done, 2 * b + n + 1)
                    dve.tensor_tensor((q_rest, k_rest)[n][:, :], (xqv_bank, ky_bank)[n][:, :],
                                      (q_parts, k_parts)[n][0][:, :], ALU.subtract).then_inc(rest_done, 1)

                def maximum(b, u):
                    t, g = u // GROUPS, u % GROUPS
                    dve.wait_ge(scored, b * UNITS + u + 1)
                    dve.tensor_reduce(neg_max[:, t, g * GROUP:(g + 1) * GROUP],
                                      score_bank[u % 2][:, :].rearrange("p (j k) -> p j k", k=P),
                                      AX.X, ALU.max, negate=True).then_inc(max_done, 1)

                def split_max(b, half):
                    n = 8 * b + 4 * half
                    ts = slice(half * TILES // 2, (half + 1) * TILES // 2)
                    parts = [max_parts[:, ts, i, :] for i in range(3)]
                    dve.wait_ge(max_done, b * UNITS + (half + 1) * HALF)
                    dve.tensor_copy(parts[0], neg_max[:, ts, :]).then_inc(max_split, 1)
                    dve.wait_ge(max_split, n + 1)
                    dve.tensor_tensor(max_rest[:, ts, :], neg_max[:, ts, :], parts[0], ALU.subtract)\
                       .then_inc(max_split, 1)
                    dve.wait_ge(max_split, n + 2)
                    dve.tensor_copy(parts[1], max_rest[:, ts, :]).then_inc(max_split, 1)
                    dve.wait_ge(max_split, n + 3)
                    dve.tensor_tensor(parts[2], max_rest[:, ts, :], parts[1], ALU.subtract).then_inc(max_split, 1)

                def add_bias(b, first):
                    dve.wait_ge(proj_done, b + 1)
                    if not first:
                        dve.wait_ge(x_added, b)
                    dve.tensor_tensor(y[:, :, :], ky_bank[:, :].rearrange("p (t c) -> p t c", t=TILES),
                                      b_proj[:, :].rearrange("p (a c) -> p a c", a=1).to_broadcast([P, TILES, C]),
                                      ALU.add).then_inc(y_done, 1)

                def y_moments(b):
                    dve.wait_ge(y_done, b + 1)
                    norm_out.take_moments(dve, b, lambda t: y[:, t, :])

                def y_apply(b):
                    norm_out.apply(dve, b, lambda t: y[:, t, :], lambda t: y[:, t, :], yn_done)

                def scale_out(b, t, first=False):
                    n = b * TILES + t
                    o = out_bank[t % 2]
                    dve.wait_ge(weighed, UNITS * b + GROUPS * (t + 1))
                    if t > 0 or not first:
                        dve.wait_ge(outT_done, 2 * n)
                    for s in range(2):
                        dve.tensor_scalar(sums[s * 64:(s + 1) * 64, :], o[64:128, s * P:(s + 1) * P],
                                          1e-6, None, ALU.add).then_inc(sums_done, 1)
                    dve.wait_ge(sums_done, 2 * n + 2)
                    dve.reciprocal(sums[:, :], sums[:, :]).then_inc(inverted, 1)
                    dve.wait_ge(inverted, n + 1)
                    for s in range(2):
                        dve.tensor_tensor(outT[s * 64:(s + 1) * 64, t * P:(t + 1) * P],
                                          o[0:64, s * P:(s + 1) * P], sums[s * 64:(s + 1) * 64, :],
                                          ALU.mult).then_inc(outT_done, 1)

                def body(b, first=False, last=False, second=False, next_last=False):
                    for u in range(UNITS):
                        if u < HALF // 2:
                            maximum(b, HALF + 2 * u)
                            maximum(b, HALF + 2 * u + 1)
                        if not first and u == 1:
                            scale_out(b - 1, TILES - 1)
                        if not last and u in (1, 2):
                            rest(b + 1, u - 1)
                        if u == 3:
                            split_max(b, 1)
                        if not first and u == 4:
                            add_bias(b - 1, second)
                            y_moments(b - 1)
                        if u == 5:
                            if not first:
                                dve.wait_ge(proj_done, b)
                            scale_out(b, 0, first)
                        if not first and u == 7:
                            y_apply(b - 1)
                        if u == 9:
                            scale_out(b, 1)
                        if not last and LATE <= u < LATE + HALF // 2:
                            maximum(b + 1, 2 * (u - LATE))
                            maximum(b + 1, 2 * (u - LATE) + 1)
                        if not last and u == LATE + HALF // 2 - 1:
                            split_max(b + 1, 0)
                        if not last and not next_last and u == 12:
                            norm_in.take_moments(dve, b + 2, x_tile(b + 2))
                        if u == 13:
                            scale_out(b, 2)
                        if not last and not next_last and u == 14:
                            apply_in(b + 2)

                dve.memset(k_rows[0][:, :, :].bitcast(FP32), 0.0).then_inc(k_zeroed, 1)
                dve.wait_ge(x_first, X_LOAD)
                norm_in.take_moments(dve, 0, x_tile(0))
                apply_in(0, first=True)
                dve.wait_ge(k_zeroed, 1)
                dve.memset(k_rows[0][MAX_ROW:MAX_ROW + 32, :, :].bitcast(FP32), BF16_ONES).then_inc(filled_even, 1)
                for n in range(2):
                    rest(0, n)
                dve.wait_ge(x_loaded, X_LOAD)
                norm_in.take_moments(dve, 1, x_tile(1))
                fill_v(0)
                for u in range(HALF):
                    maximum(0, u)
                split_max(0, 0)
                apply_in(1)
                fill_v(1)
                dve.wait_ge(weights_loaded, weights_count)
                body(0, first=True)
                body(1, second=True)
                with dve.Fori(2, SEQS - 2) as b:
                    body(b)
                body(SEQS - 2, next_last=True)
                body(SEQS - 1, last=True)
                scale_out(SEQS - 1, TILES - 1)
                add_bias(SEQS - 1, False)
                y_moments(SEQS - 1)
                y_apply(SEQS - 1)


class Router:

    def __init__(self, nc, ctx, name, x, x_loaded, ident, ident_bf, minus_half, experts, top_k,
                 w_router, b_router, bank):
        def sb(n, shape, dt=FP32):
            return ctx.enter_context(nc.sbuf_tensor(f"{name}_{n}", shape, dt))

        def sem(n):
            return ctx.enter_context(nc.semaphore(f"{name}_{n}"))

        self.x, self.x_loaded, self.ident, self.ident_bf, self.bank = x, x_loaded, ident, ident_bf, bank
        self.E, self.K, self.w_router, self.b_router = experts, top_k, w_router, b_router
        self.PAD = 8 - top_k
        self.xn_done = sem("xn_done")
        self.norm = NormOnAct(sb, sem, "norm", minus_half, x_loaded, self.xn_done)
        self.xn = sb("xn", [P, TILES, C])
        self.xnT = sb("xnT", [C, TOK])
        self.x_high = [sb(f"x_high{i}", [C, TOK], FP32R) for i in range(2)]
        self.x_low = [sb(f"x_low{i}", [C, TOK], FP32R) for i in range(2)]
        self.logits = sb("logits", [P, TILES, experts])
        self.largest = sb("largest", [P, TILES])
        self.shifted = sb("shifted", [P, TILES, experts])
        self.exps = sb("exps", [P, TILES, experts])
        self.total = sb("total", [P, TILES])
        self.total_inv = sb("total_inv", [P, TILES])
        self.probs = sb("probs", [P, TILES, experts + self.PAD])
        self.top = sb("top", [P, TILES, 8])
        self.taken = sb("taken", [P, TILES, 8])
        self.left = sb("left", [P, TILES, experts + self.PAD])
        self.coef = sb("coef", [P, TILES, experts])
        self.coef_rest = sb("coef_rest", [P, TILES, experts])
        self.coef_parts = sb("coef_parts", [P, TILES, 3, experts], BF16)
        self.coefT = [sb(f"coefT{i}", [P, TOK], BF16) for i in range(2)]
        self.xT_moved = sem("xT_moved")
        self.xnT_done = sem("xnT_done")
        self.x_low_done = sem("x_low_done")
        self.logits_done = sem("logits_done")
        self.soft = sem("soft")
        self.exp_done = sem("exp_done")
        self.top_done = sem("top_done")
        self.split = sem("split")
        self.coef_moved = sem("coef_moved")
        self.coefT_done = sem("coefT_done")

    SOFT = 6

    def fill(self, dve, done):
        for j in range(self.PAD):
            dve.memset(self.probs[:, :, self.E + j:self.E + j + 1], -1.0 - j)
            last = dve.memset(self.taken[:, :, self.K + j:self.K + j + 1], -1.0 - j)
        last.then_inc(done, 1)
        for coefT in self.coefT:
            last = dve.memset(coefT[:, :].bitcast(FP32), 0.0)
        last.then_inc(done, 1)

    def x_tile(self, b):
        return lambda t: self.x[:, bass.ds(4 * b + t, 1), :].rearrange("p a c -> p (a c)")

    def take_moments(self, dve, b):
        self.norm.take_moments(dve, b, self.x_tile(b))

    def shift(self, dve, b):
        E, S = self.E, self.SOFT
        dve.wait_ge(self.logits_done, b + 1)
        logits = self.bank[:, 0:TILES * E].rearrange("p (t e) -> p t e", e=E)
        if self.b_router is not None:
            dve.tensor_tensor(self.logits[:, :, :], logits,
                              self.b_router[:, :].rearrange("p (a e) -> p a e", a=1).to_broadcast([P, TILES, E]),
                              ALU.add).then_inc(self.soft, 1)
        else:
            dve.tensor_copy(self.logits[:, :, :], logits).then_inc(self.soft, 1)
        dve.wait_ge(self.soft, S * b + 1)
        dve.tensor_reduce(self.largest[:, :], self.logits[:, :, :], AX.X, ALU.max).then_inc(self.soft, 1)
        dve.wait_ge(self.soft, S * b + 2)
        dve.tensor_tensor(self.shifted[:, :, :], self.logits[:, :, :],
                          self.largest[:, :].rearrange("p (t a) -> p t a", a=1).to_broadcast([P, TILES, E]),
                          ALU.subtract).then_inc(self.soft, 1)

    def choose(self, dve, b):
        self.divide(dve, b)
        self.take_top(dve, b)
        self.split_coefs(dve, b)

    def divide(self, dve, b):
        E, S = self.E, self.SOFT
        dve.wait_ge(self.exp_done, b + 1)
        dve.tensor_reduce(self.total[:, :], self.exps[:, :, :], AX.X, ALU.add).then_inc(self.soft, 1)
        dve.wait_ge(self.soft, S * b + 4)
        dve.reciprocal(self.total_inv[:, :], self.total[:, :]).then_inc(self.soft, 1)
        dve.wait_ge(self.soft, S * b + 5)
        dve.tensor_tensor(self.probs[:, :, 0:E], self.exps[:, :, :],
                          self.total_inv[:, :].rearrange("p (t a) -> p t a", a=1).to_broadcast([P, TILES, E]),
                          ALU.mult).then_inc(self.soft, 1)

    def take_top(self, dve, b):
        E, K, S = self.E, self.K, self.SOFT
        T = 2 * TILES + 2
        count = dve.to_reg(S * b + 6)
        dve.wait_ge(self.x_loaded, X_LOAD)
        dve.wait_ge(self.soft, count)
        for t in range(TILES):
            dve.max(self.top[:, t, :], self.probs[:, t, 0:E]).then_inc(self.top_done, 1)
        dve.wait_ge(self.top_done, T * b + TILES)
        dve.tensor_copy(self.taken[:, :, 0:K], self.top[:, :, 0:K]).then_inc(self.top_done, 1)
        count = dve.to_reg(T * b + TILES + 1)
        dve.wait_ge(self.x_loaded, X_LOAD)
        dve.wait_ge(self.top_done, count)
        for t in range(TILES):
            dve.match_replace(self.left[:, t, :], self.taken[:, t, :], self.probs[:, t, :], 0.0)\
               .then_inc(self.top_done, 1)

    def split_coefs(self, dve, b):
        E = self.E
        T = 2 * TILES + 2
        dve.wait_ge(self.top_done, T * b + 2 * TILES + 1)
        dve.tensor_tensor(self.coef[:, :, :], self.probs[:, :, 0:E], self.left[:, :, 0:E], ALU.subtract)\
           .then_inc(self.top_done, 1)
        dve.wait_ge(self.top_done, T * b + T)
        dve.tensor_copy(self.coef_parts[:, :, 0, :], self.coef[:, :, :]).then_inc(self.split, 1)
        dve.wait_ge(self.split, 4 * b + 1)
        dve.tensor_tensor(self.coef_rest[:, :, :], self.coef[:, :, :], self.coef_parts[:, :, 0, :],
                          ALU.subtract).then_inc(self.split, 1)
        dve.wait_ge(self.split, 4 * b + 2)
        dve.tensor_copy(self.coef_parts[:, :, 1, :], self.coef_rest[:, :, :]).then_inc(self.split, 1)
        dve.wait_ge(self.split, 4 * b + 3)
        dve.tensor_tensor(self.coef_parts[:, :, 2, :], self.coef_rest[:, :, :], self.coef_parts[:, :, 1, :],
                          ALU.subtract).then_inc(self.split, 1)

    def split_x(self, pool, b, p):
        pool.wait_ge(self.xnT_done, 2 * b + 2)
        pool.tensor_tensor(self.x_low[p][:, :], self.xnT[:, :], self.x_high[p][:, :].bitcast(FP32), ALU.subtract)\
            .then_inc(self.x_low_done, 1)

    def normalize(self, act, b, first=False, tiles=range(TILES)):
        if not first:
            act.wait_ge(self.xT_moved, b)
        self.norm.apply(act, b, lambda t: self.xn[:, t, :], self.x_tile(b), tiles)

    def move_xT(self, act, b, p):
        act.wait_ge(self.xT_moved, b + 1)
        act.activation(self.xnT[:, :], self.bank[:, :], ACT.Copy).then_inc(self.xnT_done, 1)
        act.activation(self.x_high[p][:, :], self.bank[:, :], ACT.Copy).then_inc(self.xnT_done, 1)

    def exponents(self, act, b):
        act.wait_ge(self.soft, self.SOFT * b + 3)
        act.activation(self.exps[:, :, :], self.shifted[:, :, :], ACT.Exp).then_inc(self.exp_done, 1)

    def move_coef(self, act, b, p):
        act.wait_ge(self.coef_moved, b + 1)
        act.activation(self.coefT[p][0:3 * self.E, :], self.bank[:, :].bitcast(BF16)[0:3 * self.E, 0:TOK], ACT.Copy)\
           .then_inc(self.coefT_done, 1)

    def move_x(self, pe, b, first=False):
        if not first:
            pe.wait_ge(self.coefT_done, b)
        for t in range(TILES):
            pe.wait_ge(self.xn_done, 4 * b + t + 1)
            mm = pe.transpose(self.bank[:, t * P:(t + 1) * P], self.xn[:, t, :], self.ident[:, :])
        mm.then_inc(self.xT_moved, 1)

    def take_logits(self, pe, b):
        pe.wait_ge(self.xnT_done, 2 * b + 2)
        for t in range(TILES):
            mm = pe.matmul(self.bank[:, t * self.E:(t + 1) * self.E], self.xnT[:, t * P:(t + 1) * P],
                           self.w_router[:, :], start=True, stop=True)
        mm.then_inc(self.logits_done, 1)

    def product(self, pe, b, p, out, high, low):
        pe.matmul(out, high, self.x_high[p][:, :], start=True, stop=False)
        pe.matmul(out, low, self.x_high[p][:, :], start=False, stop=False)
        return pe.matmul(out, high, self.x_low[p][:, :], start=False, stop=True)

    def move_parts(self, pe, b):
        count = pe.to_reg(4 * b + 4)
        pe.wait_ge(self.x_loaded, X_LOAD)
        pe.wait_ge(self.split, count)
        for t in range(TILES):
            mm = pe.transpose(self.bank[:, :].bitcast(BF16)[0:3 * self.E, t * P:(t + 1) * P],
                              self.coef_parts[:, t, :, :].rearrange("p i e -> p (i e)"), self.ident_bf[:, :])
        mm.then_inc(self.coef_moved, 1)


def high_bits(act, w, high, done):
    for n, h in high.items():
        act.activation(h, w[n], ACT.Copy).then_inc(done, 1)


def low_bits(pool, w, high, low, high_done, done, before=0):
    for i, (n, h) in enumerate(high.items()):
        pool.wait_ge(high_done, before + i + 1)
        pool.tensor_tensor(low[n], w[n], h.bitcast(FP32), ALU.subtract).then_inc(done, 1)


def fill_selectors(pool, selectors, experts, width, done):
    pool.memset(selectors[:, :], 0.0).then_inc(done, 1)
    view = selectors[:, :].rearrange("r (e w) -> r e w", w=width)
    for i in range(3):
        pool.wait_ge(done, i + 1)
        pool.affine_select(out=view, in_=view, compare_op=ALU.not_equal, fill=1.0, base=-i * experts,
                           pattern=[[-1, experts], [0, width]], channel_multiplier=1).then_inc(done, 1)


def swiglu_experts_layer(nc, banks, x, x_loaded, ident, ident_bf, minus_half, w, weights_loaded, weights_count,
                         prepare_next, prepare_act, prepare_pool, next_front):
    E, K, D = 8, 2, 64
    PAIRS = E * D // P
    STEPS = PAIRS + 1
    LAG = 2

    with ExitStack() as ctx:
        def sb(name, shape, dt=FP32):
            return ctx.enter_context(nc.sbuf_tensor("sw_" + name, shape, dt))

        def sem(name):
            return ctx.enter_context(nc.semaphore("sw_" + name))

        gate_bank, up_bank, out_bank, coef_bank = banks[1:3], banks[3:5], banks[5:7], banks[7]
        r = Router(nc, ctx, "swr", x, x_loaded, ident, ident_bf, minus_half, E, K, w["router"], None, banks[0])
        yn_done = sem("yn_done")
        norm_out = NormOnAct(sb, sem, "norm_out", minus_half, x_loaded, yn_done)
        selectors = sb("selectors", [P, E * D], BF16)
        tanh_gate = sb("tanh_gate", [P, 2, TOK])
        gated = sb("gated", [P, 2, TOK])
        hidden = sb("hidden", [P, 2, TOK])
        weighed = sb("weighed", [P, 2, TOK])
        yn = sb("yn", [P, TILES, C])
        widths = {"shared_gate": P, "shared_up": P, "gate": E * D, "up": E * D}
        weights = {n: w[n][:, :] for n in widths}
        high = {n: sb("high_" + n, [C, m], FP32R)[:, :] for n, m in widths.items()}
        low = {n: sb("low_" + n, [C, m], FP32R)[:, :] for n, m in widths.items()}

        high_done = sem("high_done")
        low_done = sem("low_done")
        filled = sem("filled")
        selectors_done = sem("selectors_done")
        gate_up = sem("gate_up")
        coef_spread = sem("coef_spread")
        tanh_done = sem("tanh_done")
        gated_done = sem("gated_done")
        hidden_done = sem("hidden_done")
        weighed_done = sem("weighed_done")
        summed = sem("summed")
        x_added = sem("x_added")

        with nc.Block() as block:

            @block.gpsimd
            def _(pool):
                def add(b):
                    pool.wait_ge(yn_done, 4 * b + 4)
                    xs = x[:, bass.ds(4 * b, TILES), :]
                    pool.tensor_tensor(xs, xs, yn[:, :, :], ALU.add).then_inc(x_added, 1)

                def body(b, p, first=False, last=False, next_last=False):
                    if last:
                        next_front.norm.take_power(pool, 0)
                        next_front.second_power(pool, 0, first=True)
                        next_front.norm.take_power(pool, 1)
                    else:
                        r.split_x(pool, b + 1, 1 - p)
                    if not first:
                        norm_out.take_power(pool, b - 1)
                        add(b - 1)
                    if not last and not next_last:
                        r.norm.take_power(pool, b + 2)

                r.norm.take_power(pool, 0)
                fill_selectors(pool, selectors, E, D, selectors_done)
                r.norm.take_power(pool, 1)
                r.split_x(pool, 0, 0)
                low_bits(pool, weights, high, low, high_done, low_done)
                body(0, 0, first=True)
                prepare_pool(pool)
                with pool.Fori(0, (SEQS - 4) // 2) as pair:
                    b = 2 * pair + 1
                    body(b, 1)
                    body(b + 1, 0)
                body(SEQS - 3, 1)
                body(SEQS - 2, 0, next_last=True)
                body(SEQS - 1, 1, last=True)
                norm_out.take_power(pool, SEQS - 1)
                add(SEQS - 1)

            @block.scalar
            def _(act):
                def tanh(b, p, i, first):
                    n, s = b * STEPS + i, (p + i) % 2
                    act.wait_ge(gate_up, n + 1)
                    if not first or i >= 2:
                        act.wait_ge(gated_done, n - 1)
                    act.activation(tanh_gate[:, s, :], gate_bank[s][:, :], ACT.Tanh, scale=0.5)\
                       .then_inc(tanh_done, 1)

                def out_apply(b, p, first=False):
                    if not first:
                        act.wait_ge(x_added, b)
                    norm_out.apply(act, b, lambda t: yn[:, t, :],
                                   lambda t: out_bank[p][:, t * P:(t + 1) * P])

                def body(b, p, first=False, last=False, second=False):
                    for i in range(STEPS):
                        if not last and i == 0:
                            r.normalize(act, b + 1)
                        if not first and i == 3:
                            out_apply(b - 1, 1 - p, second)
                        tanh(b, p, i, first)
                        if not first and i == 0:
                            r.move_coef(act, b, p)
                        if not last and i == 1:
                            r.move_xT(act, b + 1, 1 - p)
                        if not last and i == 3:
                            r.exponents(act, b + 1)
                        if last and i == 2:
                            next_front.scale_xs(act, 0, first=True)
                        if last and i == 3:
                            act.wait_ge(next_front.weights_loaded, next_front.weights_count)
                            next_front.move_xT(act, 0)

                act.wait_ge(weights_loaded, weights_count)
                high_bits(act, weights, high, high_done)
                r.normalize(act, 0, first=True)
                r.move_xT(act, 0, 0)
                r.exponents(act, 0)
                act.wait_ge(filled, 2)
                r.move_coef(act, 0, 0)
                body(0, 0, first=True)
                prepare_act(act)
                body(1, 1, second=True)
                with act.Fori(0, (SEQS - 4) // 2) as pair:
                    b = 2 * pair + 2
                    body(b, 0)
                    body(b + 1, 1)
                body(SEQS - 2, 0)
                body(SEQS - 1, 1, last=True)
                out_apply(SEQS - 1, 1)

            @block.tensor
            def _(pe):
                def gate_and_up(b, p, i, first):
                    n, s = b * STEPS + i, (p + i) % 2
                    if not first or i >= 2:
                        pe.wait_ge(hidden_done, n - 1)
                    if i == 0:
                        pe.wait_ge(r.x_low_done, b + 1)
                    for bank, name in ((gate_bank, "gate"), (up_bank, "up")):
                        if i == 0:
                            parts = high["shared_" + name], low["shared_" + name]
                        else:
                            parts = high[name][:, (i - 1) * P:i * P], low[name][:, (i - 1) * P:i * P]
                        mm = r.product(pe, b, p, bank[s][:, :], *parts)
                    mm.then_inc(gate_up, 1)

                def spread(b, p, i, first):
                    m = b * PAIRS + i - 1
                    if i == 1:
                        pe.wait_ge(r.coefT_done, b + 1)
                    if not first or i >= 2:
                        pe.wait_ge(weighed_done, m)
                    pe.matmul(coef_bank[:, :], selectors[:, (i - 1) * P:i * P], r.coefT[p][:, :], start=True, stop=True)\
                      .then_inc(coef_spread, 1)

                def down(b, p, i, first=False, second=False):
                    if i == 0:
                        pe.wait_ge(hidden_done, b * STEPS + 1)
                        if not first and not second:
                            pe.wait_ge(yn_done, 4 * b - 4)
                    else:
                        pe.wait_ge(weighed_done, b * PAIRS + i)
                    rhs = w["shared_down"][:, :] if i == 0 else w["down"][:, i - 1, :]
                    for t in range(TILES):
                        mm = pe.matmul(out_bank[p][:, t * P:(t + 1) * P], weighed[:, (p + i) % 2, t * P:(t + 1) * P], rhs,
                                       start=(i == 0 and t == 0), stop=(i == STEPS - 1), skip_group_check=True)
                    mm.then_inc(summed, 1)

                def body(b, p, first=False, last=False, second=False):
                    for i in range(STEPS):
                        gate_and_up(b, p, i, first)
                        if i >= LAG:
                            down(b, p, i - LAG, first, second)
                        elif not first:
                            down(b - 1, 1 - p, STEPS - LAG + i)
                        if not first and i == 0:
                            r.move_parts(pe, b)
                        if i >= 1:
                            spread(b, p, i, first)
                        if not last and i == 1:
                            r.move_x(pe, b + 1)
                        if not last and i == 2:
                            r.take_logits(pe, b + 1)
                        if last and i == 3:
                            next_front.move_x(pe, 0)

                pe.wait_ge(weights_loaded, weights_count)
                r.move_x(pe, 0, first=True)
                r.take_logits(pe, 0)
                r.move_parts(pe, 0)
                pe.wait_ge(low_done, len(low))
                pe.wait_ge(selectors_done, 4)
                body(0, 0, first=True)
                body(1, 1, second=True)
                with pe.Fori(0, (SEQS - 4) // 2) as pair:
                    b = 2 * pair + 2
                    body(b, 0)
                    body(b + 1, 1)
                body(SEQS - 2, 0)
                body(SEQS - 1, 1, last=True)
                for i in range(STEPS - LAG, STEPS):
                    down(SEQS - 1, 1, i)

            @block.vector
            def _(dve):
                def hide(b, p, i, first):
                    n, s = b * STEPS + i, (p + i) % 2
                    dve.wait_ge(tanh_done, n + 1)
                    dve.scalar_tensor_tensor(out=gated[:, s, :], in0=tanh_gate[:, s, :], scalar=1.0,
                                             in1=gate_bank[s][:, :], op0=ALU.add, op1=ALU.mult)\
                       .then_inc(gated_done, 1)
                    dve.wait_ge(gated_done, n + 1)
                    if i == 0 and not first:
                        dve.wait_ge(summed, n - 1)
                    out = weighed if i == 0 else hidden
                    dve.scalar_tensor_tensor(out=out[:, s, :], in0=gated[:, s, :], scalar=0.5,
                                             in1=up_bank[s][:, :], op0=ALU.mult, op1=ALU.mult)\
                       .then_inc(hidden_done, 1)
                    if i >= 1:
                        m = b * PAIRS + i - 1
                        dve.wait_ge(hidden_done, n + 1)
                        dve.wait_ge(coef_spread, m + 1)
                        if not first or i >= 2:
                            dve.wait_ge(summed, n - 1)
                        dve.tensor_tensor(weighed[:, s, :], hidden[:, s, :], coef_bank[:, :], ALU.mult)\
                           .then_inc(weighed_done, 1)

                def out_tile(o):
                    return lambda t: out_bank[o][:, t * P:(t + 1) * P]

                def out_moments(b, p):
                    dve.wait_ge(summed, STEPS * b + STEPS)
                    norm_out.take_moments(dve, b, out_tile(p))

                def body(b, p, first=False, last=False, second=False, next_last=False):
                    for i in range(STEPS):
                        hide(b, p, i, first)
                        if last and i == 0:
                            next_front.second_variance(dve, 0)
                        if last and i == 1:
                            next_front.apply_x(dve, 0)
                            next_front.take_moments(dve, 1)
                        if next_last and i == 4:
                            next_front.take_moments(dve, 0)
                        if not first and i == 1:
                            out_moments(b - 1, 1 - p)
                        if not last and i == 2:
                            r.shift(dve, b + 1)
                        if not last and not next_last and i == 3:
                            r.take_moments(dve, b + 2)
                        if not last and i == 3:
                            r.choose(dve, b + 1)

                r.take_moments(dve, 0)
                r.fill(dve, filled)
                r.take_moments(dve, 1)
                r.shift(dve, 0)
                r.choose(dve, 0)
                body(0, 0, first=True)
                prepare_next(dve)
                body(1, 1, second=True)
                with dve.Fori(0, (SEQS - 4) // 2) as pair:
                    b = 2 * pair + 2
                    body(b, 0)
                    body(b + 1, 1)
                body(SEQS - 2, 0, next_last=True)
                body(SEQS - 1, 1, last=True)
                out_moments(SEQS - 1, 1)


class ReluFront:
    E, K = 15, 3
    ONES = 96

    def __init__(self, nc, ctx, bank, x, x_loaded, ident, ident_bf, minus_half, w, weights_loaded, weights_count):
        def sb(name, shape, dt=FP32):
            return ctx.enter_context(nc.sbuf_tensor("re_" + name, shape, dt))

        def sem(name):
            return ctx.enter_context(nc.semaphore("re_" + name))

        self.w, self.weights_loaded, self.weights_count = w, weights_loaded, weights_count
        self.r = Router(nc, ctx, "rer", x, x_loaded, ident, ident_bf, minus_half, self.E, self.K, w["router"],
                        w["b_router"], bank)
        self.selectors = sb("selectors", [P, self.E * P], BF16)
        self.b2_rest = sb("b2_rest", [P, C])
        self.b2_parts = sb("b2_parts", [P, 3, C], BF16)
        self.filled = sem("filled")
        self.b2_split = sem("b2_split")
        self.selectors_done = sem("selectors_done")

    def fill_pool(self, pool):
        fill_selectors(pool, self.selectors, self.E, P, self.selectors_done)

    def fill_dve(self, dve):
        filled, b2_split, b2_parts, b2_rest, w = self.filled, self.b2_split, self.b2_parts, self.b2_rest, self.w
        self.r.fill(dve, filled)
        dve.wait_ge(filled, 2)
        for coefT in self.r.coefT:
            last = dve.memset(coefT[self.ONES:self.ONES + 1, :], 1.0)
        last.then_inc(filled, 1)
        dve.wait_ge(self.weights_loaded, self.weights_count)
        dve.tensor_copy(b2_parts[:, 0, :], w["b2_rows"][:, :]).then_inc(b2_split, 1)
        dve.wait_ge(b2_split, 1)
        dve.tensor_tensor(b2_rest[:, :], w["b2_rows"][:, :], b2_parts[:, 0, :], ALU.subtract)\
           .then_inc(b2_split, 1)
        dve.wait_ge(b2_split, 2)
        dve.tensor_copy(b2_parts[:, 1, :], b2_rest[:, :]).then_inc(b2_split, 1)
        dve.wait_ge(b2_split, 3)
        dve.tensor_tensor(b2_parts[:, 2, :], b2_rest[:, :], b2_parts[:, 1, :], ALU.subtract)\
           .then_inc(b2_split, 2)


def relu_experts_layer(nc, banks, x, ident, minus_half, x_loaded, front, w, high, low, bits_done,
                       weights_loaded, weights_count):
    E = front.E
    STEPS = E + 1
    HIDDEN = 4
    PARTS = 8
    LAG = 4

    with ExitStack() as ctx:
        def sb(name, shape, dt=FP32):
            return ctx.enter_context(nc.sbuf_tensor("re_" + name, shape, dt))

        def sem(name):
            return ctx.enter_context(nc.semaphore("re_" + name))

        hidden_bank, coef_bank, sum_bank, out_bank = banks[1:3], banks[3:5], banks[5:7], banks[7]
        r, selectors, b2_parts = front.r, front.selectors, front.b2_parts
        selectors_done, b2_split = front.selectors_done, front.b2_split
        norm_out = Norm(sb, sem, "norm_out", minus_half, x_loaded)
        hidden = sb("hidden", [P, HIDDEN, TOK])
        weighed = sb("weighed", [P, HIDDEN, TOK])
        weighed_high = sb("weighed_high", [P, PARTS, TOK], FP32R)
        weighed_low = sb("weighed_low", [P, PARTS, TOK], FP32R)
        sumT = sb("sumT", [C, TOK])
        w2 = {"w2": w["w2"][:, :, :]}
        high_2 = {"w2": sb("high_w2", [P, STEPS, C], FP32R)[:, :, :]}
        low_2 = {"w2": sb("low_w2", [P, STEPS, C], FP32R)[:, :, :]}
        high_bits_done, low_bits_done = bits_done
        yn = sb("yn", [P, TILES, C])

        first_product = sem("first_product")
        coef_spread = sem("coef_spread")
        hidden_done = sem("hidden_done")
        weighed_done = sem("weighed_done")
        high_done = sem("high_done")
        low_even_done = sem("low_even_done")
        low_odd_done = sem("low_odd_done")
        summed = sem("summed")
        sum_copied = sem("sum_copied")
        out_moved = sem("out_moved")
        yn_done = sem("yn_done")
        x_added = sem("x_added")

        def take_low(engine, b, i, first, done):
            n, s = b * STEPS + i, i % PARTS
            engine.wait_ge(high_done, n + 1)
            if not first or i >= PARTS:
                engine.wait_ge(summed, n + 1 - PARTS)
            source = hidden if i == 0 else weighed
            engine.tensor_tensor(weighed_low[:, s, :], source[:, i % HIDDEN, :], weighed_high[:, s, :].bitcast(FP32),
                                 ALU.subtract).then_inc(done, 1)

        with nc.Block() as block:

            @block.gpsimd
            def _(pool):
                def add(b):
                    pool.wait_ge(yn_done, 4 * b + 4)
                    xs = x[:, bass.ds(4 * b, TILES), :]
                    pool.tensor_tensor(xs, xs, yn[:, :, :], ALU.add).then_inc(x_added, 1)

                def body(b, p, first=False, last=False, next_last=False):
                    for i in range(1, STEPS, 2):
                        take_low(pool, b, i, first, low_odd_done)
                        if not first and i == 5:
                            norm_out.take_power(pool, b - 1)
                        if not last and i == 7:
                            r.split_x(pool, b + 1, 1 - p)
                        if not first and i == 9:
                            add(b - 1)
                        if not last and not next_last and i == 13:
                            r.norm.take_power(pool, b + 2)

                low_bits(pool, w2, high_2, low_2, high_bits_done, low_bits_done, before=1)
                body(0, 0, first=True)
                with pool.Fori(0, (SEQS - 4) // 2) as pair:
                    b = 2 * pair + 1
                    body(b, 1)
                    body(b + 1, 0)
                body(SEQS - 3, 1)
                body(SEQS - 2, 0, next_last=True)
                body(SEQS - 1, 1, last=True)
                norm_out.take_power(pool, SEQS - 1)
                add(SEQS - 1)

            @block.scalar
            def _(act):
                def relu(b, i, first):
                    n = b * STEPS + i
                    act.wait_ge(first_product, n + 1)
                    if i == HIDDEN:
                        act.wait_ge(low_even_done, b * (STEPS // 2) + 1)
                    elif i > HIDDEN:
                        act.wait_ge(weighed_done, b * E + i - HIDDEN)
                    elif not first:
                        act.wait_ge(weighed_done, b * E + i + 1 - HIDDEN)
                    act.activation(hidden[:, i % HIDDEN, :], hidden_bank[i % 2][:, :], ACT.Relu,
                                   bias=w["b1"][:, i:i + 1]).then_inc(hidden_done, 1)

                def take_high(b, i, first=False):
                    n = b * STEPS + i
                    if i > 0:
                        act.wait_ge(weighed_done, b * E + i)
                    else:
                        act.wait_ge(hidden_done, n + 1)
                    if not first or i >= PARTS:
                        act.wait_ge(summed, n + 1 - PARTS)
                    source = hidden if i == 0 else weighed
                    act.activation(weighed_high[:, i % PARTS, :], source[:, i % HIDDEN, :], ACT.Copy).then_inc(high_done, 1)

                def copy_sum(b, p):
                    act.wait_ge(summed, STEPS * b + STEPS)
                    act.activation(sumT[:, :], sum_bank[p][:, :], ACT.Copy).then_inc(sum_copied, 1)

                def body(b, p, first=False, last=False):
                    for i in range(STEPS):
                        relu(b, i, first)
                        if i >= 1:
                            take_high(b, i - 1, first)
                        elif not first:
                            take_high(b - 1, STEPS - 1)
                        if not first and i == LAG:
                            copy_sum(b - 1, 1 - p)
                        if not last:
                            if i < TILES:
                                r.normalize(act, b + 1, tiles=(i,))
                            if i == 6:
                                r.move_xT(act, b + 1, 1 - p)
                            if i == 9:
                                r.exponents(act, b + 1)
                            if i == 15:
                                r.move_coef(act, b + 1, 1 - p)

                act.wait_ge(weights_loaded, weights_count)
                high_bits(act, w2, high_2, high_bits_done)
                body(0, 0, first=True)
                with act.Fori(0, (SEQS - 2) // 2) as pair:
                    b = 2 * pair + 1
                    body(b, 1)
                    body(b + 1, 0)
                body(SEQS - 1, 1, last=True)
                take_high(SEQS - 1, STEPS - 1)
                copy_sum(SEQS - 1, 1)

            @block.tensor
            def _(pe):
                def first_product_of(b, p, i, first):
                    if not first or i >= 2:
                        pe.wait_ge(hidden_done, b * STEPS + i - 1)
                    if i == 0:
                        pe.wait_ge(r.x_low_done, b + 1)
                    r.product(pe, b, p, hidden_bank[i % 2][:, :], high["w1"][:, i, :], low["w1"][:, i, :])\
                     .then_inc(first_product, 1)

                def spread(b, p, i, first):
                    m = b * E + i - 1
                    if i == 1:
                        pe.wait_ge(r.coefT_done, b + 1)
                    if not first or i > 2:
                        pe.wait_ge(weighed_done, m - 1)
                    pe.matmul(coef_bank[(p + i) % 2][:, :], selectors[:, (i - 1) * P:i * P], r.coefT[p][:, :],
                              start=True, stop=True).then_inc(coef_spread, 1)

                def biases(b, p, first, second):
                    if not first and not second:
                        pe.wait_ge(sum_copied, b - 1)
                    for i in range(3):
                        pe.matmul(sum_bank[p][:, :], b2_parts[:, i, :], r.coefT[p][:, :], start=(i == 0), stop=False,
                                  skip_group_check=True)

                def second_product(b, p, i):
                    s = i % PARTS
                    if i % 2 == 0:
                        pe.wait_ge(low_even_done, b * (STEPS // 2) + i // 2 + 1)
                    else:
                        pe.wait_ge(low_odd_done, b * (STEPS // 2) + i // 2 + 1)
                    for j, (weight, h) in enumerate(((high_2, weighed_high), (low_2, weighed_high), (high_2, weighed_low))):
                        mm = pe.matmul(sum_bank[p][:, :], weight["w2"][:, i, :], h[:, s, :], start=False,
                                       stop=(i == STEPS - 1 and j == 2), skip_group_check=True)
                    mm.then_inc(summed, 1)

                def move_out(b, first=False):
                    pe.wait_ge(sum_copied, b + 1)
                    if not first:
                        pe.wait_ge(yn_done, 4 * b)
                    for t in range(TILES):
                        mm = pe.transpose(out_bank[:, t * P:(t + 1) * P], sumT[:, t * P:(t + 1) * P], ident[:, :])
                    mm.then_inc(out_moved, 1)

                def body(b, p, first=False, last=False, second=False):
                    for i in range(STEPS):
                        first_product_of(b, p, i, first)
                        if i >= 1:
                            spread(b, p, i, first)
                        if first and i == LAG:
                            pe.wait_ge(low_bits_done, 2)
                        if i >= LAG:
                            second_product(b, p, i - LAG)
                        elif not first:
                            second_product(b - 1, 1 - p, STEPS - LAG + i)
                        if i == LAG - 1:
                            biases(b, p, first, second)
                        if not first and i == LAG + 1:
                            move_out(b - 1, second)
                        if not last:
                            if i == 5:
                                r.move_x(pe, b + 1)
                            if i == 7:
                                r.take_logits(pe, b + 1)
                            if i == 15:
                                r.move_parts(pe, b + 1)

                pe.wait_ge(weights_loaded, weights_count)
                pe.wait_ge(selectors_done, 4)
                pe.wait_ge(b2_split, 5)
                pe.wait_ge(low_bits_done, 1)
                body(0, 0, first=True)
                body(1, 1, second=True)
                with pe.Fori(0, (SEQS - 4) // 2) as pair:
                    b = 2 * pair + 2
                    body(b, 0)
                    body(b + 1, 1)
                body(SEQS - 2, 0)
                body(SEQS - 1, 1, last=True)
                for i in range(STEPS - LAG, STEPS):
                    second_product(SEQS - 1, 1, i)
                move_out(SEQS - 1)

            @block.vector
            def _(dve):
                def weigh(b, p, i, first):
                    n, m = b * STEPS + i, b * E + i - 1
                    dve.wait_ge(hidden_done, n + 1)
                    dve.wait_ge(coef_spread, m + 1)
                    if not first or i > HIDDEN:
                        dve.wait_ge((low_even_done, low_odd_done)[i % 2], b * (STEPS // 2) + (i - HIDDEN) // 2 + 1)
                    dve.tensor_tensor(weighed[:, i % HIDDEN, :], hidden[:, i % HIDDEN, :],
                                      coef_bank[(p + i) % 2][:, :], ALU.mult).then_inc(weighed_done, 1)

                def out_tile(t):
                    return out_bank[:, t * P:(t + 1) * P]

                def out_moments(b):
                    dve.wait_ge(out_moved, b + 1)
                    norm_out.take_moments(dve, b, out_tile)

                def out_apply(b, first=False):
                    if not first:
                        dve.wait_ge(x_added, b)
                    norm_out.apply(dve, b, lambda t: yn[:, t, :], out_tile, yn_done)

                def body(b, p, first=False, last=False, second=False, next_last=False):
                    for i in range(STEPS):
                        if i >= 2 and i % 2 == 0:
                            take_low(dve, b, i - 2, first, low_even_done)
                        elif i == 0 and not first:
                            take_low(dve, b - 1, STEPS - 2, False, low_even_done)
                        if i >= 1:
                            weigh(b, p, i, first)
                        if not first and i == 6:
                            out_moments(b - 1)
                        if not first and i == 9:
                            out_apply(b - 1, second)
                        if not last and i == 8:
                            r.shift(dve, b + 1)
                        if not last and i == 10:
                            r.divide(dve, b + 1)
                        if not last and i == 11:
                            r.take_top(dve, b + 1)
                        if not last and i == 12:
                            r.split_coefs(dve, b + 1)
                        if not last and not next_last and i == 13:
                            r.take_moments(dve, b + 2)

                body(0, 0, first=True)
                body(1, 1, second=True)
                with dve.Fori(0, (SEQS - 4) // 2) as pair:
                    b = 2 * pair + 2
                    body(b, 0)
                    body(b + 1, 1)
                body(SEQS - 2, 0, next_last=True)
                body(SEQS - 1, 1, last=True)
                take_low(dve, SEQS - 1, STEPS - 2, False, low_even_done)
                out_moments(SEQS - 1)
                out_apply(SEQS - 1)


MIXED = (("wk", "mix_k"), ("wv", "mix_v"), ("wr", "mix_r"), ("wr_ffn", "ffn_mix_r"))


SHARES = 3 * len(MIXED)


def split_mixes(dve, w, shares, weights_loaded, weights_count, done):
    dve.wait_ge(weights_loaded, weights_count)
    for n, (name, mix) in enumerate(MIXED):
        dve.tensor_scalar(shares["rest"][:, n:n + 1], w[mix][:, :], -1.0, 1.0, ALU.mult, ALU.add).then_inc(done, 1)
        dve.tensor_scalar(shares[name][0][:, :], w[name][:, :], w[mix][:, :], None, ALU.mult).then_inc(done, 1)
    for n, (name, mix) in enumerate(MIXED):
        dve.wait_ge(done, 2 * n + 1)
        dve.tensor_scalar(shares[name][1][:, :], w[name][:, :], shares["rest"][:, n:n + 1], None, ALU.mult)\
           .then_inc(done, 1)


class RwkvFront:

    def __init__(self, nc, ctx, bank, x, x_loaded, ident, minus_half, w, weights_loaded, weights_count):
        def sb(name, shape, dt=FP32):
            return ctx.enter_context(nc.sbuf_tensor("rf_" + name, shape, dt))

        def sem(name):
            return ctx.enter_context(nc.semaphore("rf_" + name))

        self.bank, self.x, self.ident, self.minus_half, self.w = bank, x, ident, minus_half, w
        self.weights_loaded, self.weights_count = weights_loaded, weights_count
        self.norm = Norm(sb, sem, "norm", minus_half, x_loaded)
        self.xs = sb("xs", [P, SEQS * TILES, C])
        self.var_2 = sb("var_2", [P, TILES])
        self.rstd_2 = sb("rstd_2", [P, TILES])
        self.xhat = sb("xhat", [P, TILES, C])
        self.xnT = sb("xnT", [C, 1 + TOK])
        self.xs_done = sem("xs_done")
        self.var_2_done = sem("var_2_done")
        self.rstd_2_done = sem("rstd_2_done")
        self.xhat_done = sem("xhat_done")
        self.xT_moved = sem("xT_moved")
        self.xnT_done = sem("xnT_done")

    def tile(self, x, b):
        return lambda t: x[:, bass.ds(4 * b + t, 1), :].rearrange("p a c -> p (a c)")

    def take_moments(self, dve, b):
        self.norm.take_moments(dve, b, self.tile(self.x, b))

    def second_variance(self, dve, b):
        var_2, rstd, done = self.var_2, self.norm.rstd, self.var_2_done
        dve.wait_ge(self.norm.rstd_done, b + 1)
        dve.tensor_tensor(var_2[:, :], rstd[:, :], rstd[:, :], ALU.mult).then_inc(done, 1)
        dve.wait_ge(done, 3 * b + 1)
        dve.tensor_tensor(var_2[:, :], var_2[:, :], self.norm.moments[:, :, 1], ALU.mult).then_inc(done, 1)
        dve.wait_ge(done, 3 * b + 2)
        dve.tensor_scalar(var_2[:, :], var_2[:, :], EPS, None, ALU.add).then_inc(done, 1)

    def apply_x(self, dve, b):
        self.norm.apply(dve, b, self.tile(self.xs, b), self.tile(self.x, b), self.xs_done)

    def second_power(self, pool, b, first=False):
        pool.wait_ge(self.var_2_done, 3 * b + 3)
        if not first:
            pool.wait_ge(self.xhat_done, 4 * b)
        pool.tensor_tensor(self.rstd_2[:, :], self.var_2[:, :], self.minus_half[:, :], ALU.pow)\
            .then_inc(self.rstd_2_done, 1)

    def scale_xs(self, act, b, first=False):
        act.wait_ge(self.rstd_2_done, b + 1)
        if not first:
            act.wait_ge(self.xT_moved, b)
        act.wait_ge(self.xs_done, 4 * b + 4)
        for t in range(TILES):
            act.activation(self.xhat[:, t, :], self.tile(self.xs, b)(t), ACT.Copy, scale=self.rstd_2[:, t:t + 1])\
               .then_inc(self.xhat_done, 1)

    def move_xT(self, act, b):
        act.wait_ge(self.xT_moved, b + 1)
        act.activation(self.xnT[:, 1:1 + TOK], self.bank[:, :], ACT.Identity, scale=self.w["g1"][:, :],
                       bias=self.w["b1"][:, :]).then_inc(self.xnT_done, 1)

    def move_x(self, pe, b):
        for t in range(TILES):
            pe.wait_ge(self.xhat_done, 4 * b + t + 1)
            mm = pe.transpose(self.bank[:, t * P:(t + 1) * P], self.xhat[:, t, :], self.ident[:, :])
        mm.then_inc(self.xT_moved, 1)


def rwkv_layer(nc, banks, x, x_loaded, ident, minus_half, w, shares, shares_done, weights_loaded, weights_count,
               first, front):
    F = 512
    FCH = F // P
    r = front.r
    START = -1e38
    LAG = 2

    with ExitStack() as ctx:
        def sb(name, shape, dt=FP32):
            return ctx.enter_context(nc.sbuf_tensor("rk_" + name, shape, dt))

        def sem(name):
            return ctx.enter_context(nc.semaphore("rk_" + name))

        xT_bank, k_bank, v_bank, r_bank, x1_bank = banks[0:5]
        f_bank, kv_bank = banks[5:7], banks[7]
        norm_x, xs, xnT = first.norm, first.xs, first.xnT
        norm_1 = Norm(sb, sem, "norm_1", minus_half, x_loaded)
        yn_done = sem("yn_done")
        norm_3 = NormOnAct(sb, sem, "norm_3", minus_half, x_loaded, yn_done)
        tanh_r = sb("tanh_r", [C, TOK])
        decay = sb("decay", [C, 1])
        exp_decay = sb("exp_decay", [C, 1])
        top = sb("top", [C, 1 + TOK])
        numer = sb("numer", [C, 1 + TOK])
        denom = sb("denom", [C, 1 + TOK])
        now_max = sb("now_max", [C, TOK])
        args = sb("args", [C, 4, TOK])
        exps = sb("exps", [C, 4, TOK])
        enter_v = sb("enter_v", [C, TOK])
        now_v = sb("now_v", [C, TOK])
        past_v = sb("past_v", [C, TOK])
        past_1 = sb("past_1", [C, TOK])
        sum_v = sb("sum_v", [C, TOK])
        sum_1 = sb("sum_1", [C, TOK])
        sum_inv = sb("sum_inv", [C, TOK])
        wkv = sb("wkv", [C, TOK])
        gated = sb("gated", [C, TOK])
        x1 = sb("x1", [P, TILES, C])
        xhat2 = sb("xhat2", [P, TILES, C])
        xn2T = sb("xn2T", [C, 1 + TOK])
        step2 = sb("step2", [C, TOK])
        xk2 = sb("xk2", [C, TOK])
        relu = sb("relu", [P, FCH, TOK])
        square = sb("square", [P, FCH, TOK])
        tanh_g = sb("tanh_g", [P, TOK])
        kv_gated = sb("kv_gated", [P, TOK])
        out3 = sb("out3", [P, TILES, C])
        yn = sb("yn", [P, TILES, C])

        filled = sem("filled")
        decay_done = sem("decay_done")
        kvr_done = sem("kvr_done")
        tanh_done = sem("tanh_done")
        top_done = sem("top_done")
        args_done = sem("args_done")
        exps_done = sem("exps_done")
        scans = sem("scans")
        now_v_done = sem("now_v_done")
        past_done = sem("past_done")
        sums_done = sem("sums_done")
        gated_done = sem("gated_done")
        x1_projected = sem("x1_projected")
        x1_done = sem("x1_done")
        xhat2_done = sem("xhat2_done")
        x2T_moved = sem("x2T_moved")
        xn2T_done = sem("xn2T_done")
        mixed2 = sem("mixed2")
        f_done = sem("f_done")
        relu_done = sem("relu_done")
        square_done = sem("square_done")
        gate_projected = sem("gate_projected")
        kv_done = sem("kv_done")
        tanh_g_done = sem("tanh_g_done")
        out3_done = sem("out3_done")
        x_added = sem("x_added")

        def tiles(ap):
            return ap.rearrange("p (t c) -> p t c", t=TILES)

        with nc.Block() as block:

            @block.gpsimd
            def _(pool):
                def past(b):
                    pool.wait_ge(exps_done, 4 * b + 3)
                    pool.wait_ge(scans, 3 * b + 1)
                    pool.tensor_tensor(past_1[:, :], exps[:, 2, :], denom[:, 0:TOK], ALU.mult)\
                        .then_inc(past_done, 1)
                    pool.wait_ge(scans, 3 * b + 3)
                    pool.tensor_tensor(past_v[:, :], exps[:, 2, :], numer[:, 0:TOK], ALU.mult)\
                        .then_inc(past_done, 1)

                def add(b):
                    pool.wait_ge(yn_done, 4 * b + 4)
                    xs_ = x[:, bass.ds(4 * b, TILES), :]
                    pool.tensor_tensor(xs_, xs_, yn[:, :, :], ALU.add).then_inc(x_added, 1)

                def body(b, start=False, after=3):
                    norm_1.take_power(pool, b)
                    if after == 0:
                        r.split_x(pool, 0, 0)
                        r.norm.take_power(pool, 1)
                    if after >= 2:
                        first.second_power(pool, b + 2)
                    if after >= 1:
                        past(b + 1)
                    if not start:
                        add(b - 1)
                    if after >= 3:
                        norm_x.take_power(pool, b + 3)
                    norm_3.take_power(pool, b)

                first.second_power(pool, 1)
                past(0)
                norm_x.take_power(pool, 2)
                body(0, start=True)
                with pool.Fori(1, SEQS - 3) as b:
                    body(b)
                body(SEQS - 3, after=2)
                body(SEQS - 2, after=1)
                r.norm.take_power(pool, 0)
                body(SEQS - 1, after=0)
                add(SEQS - 1)

            @block.scalar
            def _(act):
                def gate_r(b):
                    act.wait_ge(kvr_done, 3 * b + 3)
                    act.activation(tanh_r[:, :], r_bank[:, :], ACT.Tanh, scale=0.5).then_inc(tanh_done, 1)

                def exponent(b, n):
                    act.wait_ge(args_done, 5 * b + 2 + n)
                    act.activation(exps[:, n, :], args[:, n, :], ACT.Exp).then_inc(exps_done, 1)

                def move_x2T(b):
                    act.wait_ge(x2T_moved, b + 1)
                    act.activation(xn2T[:, 1:1 + TOK], x1_bank[:, :], ACT.Identity, scale=w["g2"][:, :],
                                   bias=w["b2"][:, :]).then_inc(xn2T_done, 1)

                def squares(b, after):
                    for f in range(FCH):
                        n = b * FCH + f
                        act.wait_ge(f_done, n + 1)
                        act.activation(relu[:, f, :], f_bank[f % 2][:, :], ACT.Relu).then_inc(relu_done, 1)
                        act.wait_ge(relu_done, n + 1)
                        act.activation(square[:, f, :], relu[:, f, :], ACT.Square).then_inc(square_done, 1)
                        if after == 0 and f == 0:
                            r.exponents(act, 0)

                def gate_g(b):
                    act.wait_ge(gate_projected, b + 1)
                    act.activation(tanh_g[:, :], x1_bank[:, :], ACT.Tanh, scale=0.5).then_inc(tanh_g_done, 1)

                def apply_3(b, first=False):
                    if not first:
                        act.wait_ge(x_added, b)
                    norm_3.apply(act, b, lambda t: yn[:, t, :], lambda t: out3[:, t, :])

                def body(b, start=False, second=False, after=2):
                    if not start:
                        apply_3(b - 1, second)
                    if after >= 1:
                        exponent(b + 1, 0)
                    else:
                        r.normalize(act, 0, first=True)
                    move_x2T(b)
                    if after >= 1:
                        for n in range(1, 4):
                            exponent(b + 1, n)
                    else:
                        r.move_xT(act, 0, 0)
                    gate_g(b)
                    squares(b, after)
                    if after >= 2:
                        first.scale_xs(act, b + 2)
                        first.move_xT(act, b + 2)
                        gate_r(b + 2)

                act.wait_ge(weights_loaded, weights_count)
                act.activation(exp_decay[:, :], w["decay"][:, :], ACT.Exp).then_inc(decay_done, 1)
                first.scale_xs(act, 1)
                gate_r(0)
                for n in range(4):
                    exponent(0, n)
                first.move_xT(act, 1)
                gate_r(1)
                body(0, start=True)
                body(1, second=True)
                with act.Fori(2, SEQS - 2) as b:
                    body(b)
                body(SEQS - 2, after=1)
                body(SEQS - 1, after=0)
                act.wait_ge(front.filled, 3)
                r.move_coef(act, 0, 0)
                apply_3(SEQS - 1)

            @block.tensor
            def _(pe):
                def project(b, name, bank):
                    pe.matmul(bank[:, :], shares[name][0][:, :], xnT[:, 1:1 + TOK], start=True, stop=False)
                    pe.matmul(bank[:, :], shares[name][1][:, :], xnT[:, 0:TOK], start=False, stop=True)\
                      .then_inc(kvr_done, 1)

                def project_k(b):
                    pe.wait_ge(first.xnT_done, b + 1)
                    project(b, "wk", k_bank)

                def project_vr(b):
                    project(b, "wv", v_bank)
                    project(b, "wr", r_bank)

                def project_x1(b):
                    pe.wait_ge(gated_done, b + 1)
                    for t in range(TILES):
                        mm = pe.matmul(x1_bank[:, t * P:(t + 1) * P], gated[:, t * P:(t + 1) * P],
                                       w["wo"][:, :], start=True, stop=True)
                    mm.then_inc(x1_projected, 1)

                def move_x1(b):
                    for t in range(TILES):
                        pe.wait_ge(xhat2_done, 4 * b + t + 1)
                        mm = pe.transpose(x1_bank[:, t * P:(t + 1) * P], xhat2[:, t, :], ident[:, :])
                    mm.then_inc(x2T_moved, 1)

                def project_gate(b):
                    pe.wait_ge(xn2T_done, b + 1)
                    for t in range(TILES):
                        for n in range(2):
                            mm = pe.matmul(x1_bank[:, t * P:(t + 1) * P], xn2T[:, t * P + 1 - n:(t + 1) * P + 1 - n],
                                           shares["wr_ffn"][n][:, :], start=(n == 0), stop=(n == 1))
                    mm.then_inc(gate_projected, 1)

                def ffn(b):
                    pe.wait_ge(mixed2, 2 * b + 2)
                    for f in range(FCH + LAG):
                        if f < FCH:
                            if f >= 2:
                                pe.wait_ge(relu_done, b * FCH + f - 1)
                            pe.matmul(f_bank[f % 2][:, :], w["wk_ffn"][:, f * P:(f + 1) * P], xk2[:, :],
                                      start=True, stop=True).then_inc(f_done, 1)
                        if f >= LAG:
                            pe.wait_ge(square_done, b * FCH + f - LAG + 1)
                            for t in range(TILES):
                                mm = pe.matmul(kv_bank[:, t * P:(t + 1) * P],
                                               square[:, f - LAG, t * P:(t + 1) * P], w["wv_ffn"][:, f - LAG, :],
                                               start=(f == LAG and t == 0), stop=(f == FCH + LAG - 1),
                                               skip_group_check=True)
                    mm.then_inc(kv_done, 1)

                def body(b, after=2):
                    move_x1(b)
                    if after == 0:
                        r.move_x(pe, 0, first=True)
                    project_gate(b)
                    if after == 0:
                        r.take_logits(pe, 0)
                    ffn(b)
                    if after >= 2:
                        first.move_x(pe, b + 2)
                        project_k(b + 2)
                    if after >= 1:
                        project_x1(b + 1)
                    if after >= 2:
                        project_vr(b + 2)

                pe.wait_ge(shares_done, SHARES)
                pe.wait_ge(weights_loaded, weights_count)
                pe.wait_ge(filled, 5)
                project_k(0)
                project_vr(0)
                first.move_x(pe, 1)
                pe.wait_ge(args_done, 5)
                project_k(1)
                project_x1(0)
                project_vr(1)
                with pe.Fori(0, SEQS - 2) as b:
                    body(b)
                body(SEQS - 2, after=1)
                body(SEQS - 1, after=0)
                r.move_parts(pe, 0)

            @block.vector
            def _(dve):
                def first_args(b):
                    k, u = k_bank, w["first"][:, :]
                    dve.wait_ge(kvr_done, 3 * b + 1)
                    dve.tensor_tensor_scan(top[:, 1:1 + TOK], decay[:, :].to_broadcast([C, TOK]), k[:, :],
                                           START, ALU.add, ALU.max).then_inc(top_done, 1)
                    dve.wait_ge(top_done, b + 1)
                    dve.scalar_tensor_tensor(out=now_max[:, :], in0=k[:, :], scalar=u, in1=top[:, 0:TOK],
                                             op0=ALU.add, op1=ALU.max).then_inc(args_done, 1)
                    dve.scalar_tensor_tensor(out=args[:, 0, :], in0=top[:, 0:TOK], scalar=decay[:, :],
                                             in1=top[:, 1:1 + TOK], op0=ALU.add, op1=ALU.subtract)\
                       .then_inc(args_done, 1)

                def last_args(b):
                    k, u = k_bank, w["first"][:, :]
                    dve.tensor_tensor(args[:, 1, :], k[:, :], top[:, 1:1 + TOK], ALU.subtract)\
                       .then_inc(args_done, 1)
                    dve.wait_ge(args_done, 5 * b + 1)
                    dve.tensor_tensor(args[:, 2, :], top[:, 0:TOK], now_max[:, :], ALU.subtract)\
                       .then_inc(args_done, 1)
                    dve.scalar_tensor_tensor(out=args[:, 3, :], in0=k[:, :], scalar=u, in1=now_max[:, :],
                                             op0=ALU.add, op1=ALU.subtract).then_inc(args_done, 1)

                def recurrence(b):
                    dve.wait_ge(exps_done, 4 * b + 2)
                    dve.tensor_tensor_scan(denom[:, 1:1 + TOK], exps[:, 0, :], exps[:, 1, :], 0.0,
                                           ALU.mult, ALU.add).then_inc(scans, 1)
                    dve.wait_ge(kvr_done, 3 * b + 2)
                    dve.tensor_tensor(enter_v[:, :], exps[:, 1, :], v_bank[:, :], ALU.mult).then_inc(scans, 1)
                    dve.wait_ge(scans, 3 * b + 2)
                    dve.tensor_tensor_scan(numer[:, 1:1 + TOK], exps[:, 0, :], enter_v[:, :], 0.0,
                                           ALU.mult, ALU.add).then_inc(scans, 1)
                    dve.wait_ge(exps_done, 4 * b + 4)
                    dve.tensor_tensor(now_v[:, :], exps[:, 3, :], v_bank[:, :], ALU.mult).then_inc(now_v_done, 1)

                def output(b):
                    dve.wait_ge(past_done, 2 * b + 1)
                    dve.tensor_tensor(sum_1[:, :], past_1[:, :], exps[:, 3, :], ALU.add).then_inc(sums_done, 1)
                    dve.wait_ge(sums_done, 4 * b + 1)
                    dve.reciprocal(sum_inv[:, :], sum_1[:, :]).then_inc(sums_done, 1)
                    dve.wait_ge(past_done, 2 * b + 2)
                    dve.wait_ge(now_v_done, b + 1)
                    dve.tensor_tensor(sum_v[:, :], past_v[:, :], now_v[:, :], ALU.add).then_inc(sums_done, 1)
                    dve.wait_ge(sums_done, 4 * b + 3)
                    dve.tensor_tensor(wkv[:, :], sum_v[:, :], sum_inv[:, :], ALU.mult).then_inc(sums_done, 1)
                    dve.wait_ge(sums_done, 4 * b + 4)
                    dve.wait_ge(tanh_done, b + 1)
                    dve.scalar_tensor_tensor(out=gated[:, :], in0=tanh_r[:, :], scalar=1.0, in1=wkv[:, :],
                                             op0=ALU.add, op1=ALU.mult).then_inc(gated_done, 1)

                def add_x1(b):
                    dve.wait_ge(x1_projected, b + 1)
                    dve.scalar_tensor_tensor(out=x1[:, :, :], in0=tiles(x1_bank[:, :]), scalar=0.5,
                                             in1=xs[:, bass.ds(4 * b, TILES), :], op0=ALU.mult, op1=ALU.add)\
                       .then_inc(x1_done, 1)

                def mix2(b):
                    dve.wait_ge(xn2T_done, b + 1)
                    dve.tensor_tensor(step2[:, :], xn2T[:, 1:1 + TOK], xn2T[:, 0:TOK], ALU.subtract)\
                       .then_inc(mixed2, 1)
                    dve.wait_ge(mixed2, 2 * b + 1)
                    dve.scalar_tensor_tensor(out=xk2[:, :], in0=step2[:, :], scalar=w["ffn_mix_k"][:, :],
                                             in1=xn2T[:, 0:TOK], op0=ALU.mult, op1=ALU.add).then_inc(mixed2, 1)

                def add_ffn(b):
                    dve.wait_ge(kv_done, b + 1)
                    dve.wait_ge(tanh_g_done, b + 1)
                    dve.scalar_tensor_tensor(out=kv_gated[:, :], in0=tanh_g[:, :], scalar=1.0, in1=kv_bank[:, :],
                                             op0=ALU.add, op1=ALU.mult).then_inc(out3_done, 1)
                    dve.wait_ge(out3_done, 2 * b + 1)
                    dve.scalar_tensor_tensor(out=out3[:, :, :], in0=tiles(kv_gated[:, :]), scalar=0.5,
                                             in1=x1[:, :, :], op0=ALU.mult, op1=ALU.add).then_inc(out3_done, 1)

                def body(b, after=3):
                    add_x1(b)
                    dve.wait_ge(x1_done, b + 1)
                    norm_1.take_moments(dve, b, lambda t: x1[:, t, :])
                    if after >= 1:
                        first_args(b + 1)
                    norm_1.apply(dve, b, lambda t: xhat2[:, t, :], lambda t: x1[:, t, :], xhat2_done)
                    if after >= 1:
                        last_args(b + 1)
                    mix2(b)
                    if after >= 2:
                        first.second_variance(dve, b + 2)
                    if after >= 1:
                        recurrence(b + 1)
                    if after >= 2:
                        first.apply_x(dve, b + 2)
                    if after >= 3:
                        first.take_moments(dve, b + 3)
                    if after >= 1:
                        output(b + 1)
                    else:
                        front.fill_dve(dve)
                        r.shift(dve, 0)
                        r.take_moments(dve, 1)
                        r.choose(dve, 0)
                    add_ffn(b)
                    dve.wait_ge(out3_done, 2 * b + 2)
                    norm_3.take_moments(dve, b, lambda t: out3[:, t, :])
                    if after == 1:
                        r.take_moments(dve, 0)

                for col, value in ((xnT, 0.0), (xn2T, 0.0), (top, START), (numer, 0.0), (denom, 0.0)):
                    dve.memset(col[:, 0:1], value).then_inc(filled, 1)
                dve.wait_ge(filled, 5)
                dve.wait_ge(decay_done, 1)
                dve.tensor_scalar(decay[:, :], exp_decay[:, :], -1.0, None, ALU.mult).then_inc(decay_done, 1)
                dve.wait_ge(first.rstd_2_done, 1)
                first.second_variance(dve, 1)
                first.apply_x(dve, 1)
                dve.wait_ge(decay_done, 2)
                first_args(0)
                last_args(0)
                first.take_moments(dve, 2)
                recurrence(0)
                output(0)
                body(0)
                with dve.Fori(1, SEQS - 3) as b:
                    body(b)
                for after in (2, 1, 0):
                    body(SEQS - 1 - after, after=after)


INPUTS = ['L0_attn_x', 'L0_attn_W_qkv', 'L0_attn_W_proj', 'L0_attn_b_proj', 'L0_ffn_router', 'L0_ffn_experts_gate',
          'L0_ffn_experts_up', 'L0_ffn_experts_down', 'L0_ffn_shared_gate', 'L0_ffn_shared_up', 'L0_ffn_shared_down',
          'L1_attn_ln1_g', 'L1_attn_ln1_b', 'L1_attn_ln2_g', 'L1_attn_ln2_b', 'L1_attn_att_mix_k', 'L1_attn_att_mix_v',
          'L1_attn_att_mix_r', 'L1_attn_time_decay', 'L1_attn_time_first', 'L1_attn_Wk', 'L1_attn_Wv', 'L1_attn_Wr',
          'L1_attn_Wo', 'L1_attn_ffn_mix_k', 'L1_attn_ffn_mix_r', 'L1_attn_Wk_ffn', 'L1_attn_Wr_ffn', 'L1_attn_Wv_ffn',
          'L1_ffn_router_W', 'L1_ffn_router_b', 'L1_ffn_sW1', 'L1_ffn_sb1', 'L1_ffn_sW2', 'L1_ffn_sb2', 'L1_ffn_eW1',
          'L1_ffn_eb1', 'L1_ffn_eW2', 'L1_ffn_eb2']


def sandwich_kernel(nc, a, out):
    E0, D0, E1 = 8, 64, 15

    with ExitStack() as ctx:
        def sb(name, shape, dt=FP32):
            return ctx.enter_context(nc.sbuf_tensor(name, shape, dt))

        def sem(name):
            return ctx.enter_context(nc.semaphore(name))

        x = sb("x_tokens", [P, SEQS * TILES, C])
        ident = sb("ident", [P, P])
        ident_bf = sb("ident_bf", [P, P], BF16)
        minus_half = sb("minus_half", [P, TILES])
        x_first = sem("x_first")
        x_loaded = sem("x_loaded")
        constants = sem("constants")
        x_stored = sem("x_stored")
        weights_0a, weights_0f, weights_1a, weights_1f = (sem("weights_" + n) for n in ("0a", "0f", "1a", "1f"))
        x_view = a['L0_attn_x'].rearrange("b (t p) c -> p (b t) c", p=P)
        out_view = out.rearrange("b (t p) c -> p (b t) c", p=P)

        def row(v):
            return v.rearrange("(a c) -> a c", a=1)

        def column(v):
            return v.rearrange("(c a) -> c a", a=1)

        def load(queue, items, done):
            for dst, src in items:
                queue.dma_start(dst, src).then_inc(done, 16)
            return 16 * len(items)

        w_qkv, w_proj, b_proj = sb("w_qkv", [C, 3 * C]), sb("w_proj", [C, C]), sb("b_proj", [P, C])
        w0 = {"router": sb("router0", [C, E0]), "gate": sb("gate0", [C, E0 * D0]), "up": sb("up0", [C, E0 * D0]),
              "down": sb("down0", [P, E0 * D0 // P, C]), "shared_gate": sb("shared_gate", [C, P]),
              "shared_up": sb("shared_up", [C, P]), "shared_down": sb("shared_down", [P, C])}
        columns = ("g1", "b1", "g2", "b2", "mix_k", "mix_v", "mix_r", "decay", "first", "ffn_mix_k", "ffn_mix_r")
        w1 = {n: sb("rwkv_" + n, [C, 1]) for n in columns}
        w1.update({n: sb("rwkv_" + n, [C, C]) for n in ("wk", "wv", "wr", "wo", "wr_ffn")})
        w1["wk_ffn"] = sb("rwkv_wk_ffn", [C, 4 * C])
        w1["wv_ffn"] = sb("rwkv_wv_ffn", [P, 4, C])
        w2 = {"router": sb("router1", [C, E1]), "b_router": sb("b_router", [P, E1]), "w1": sb("w1", [C, E1 + 1, P]),
              "b1": sb("b1", [P, E1 + 1]), "w2": sb("w2", [P, E1 + 1, C]), "b2_rows": sb("b2_rows", [P, C])}

        items_0a = [(w_qkv[:, :], a['L0_attn_W_qkv']), (w_proj[:, :], a['L0_attn_W_proj']),
                    (b_proj[:, :], row(a['L0_attn_b_proj']).to_broadcast([P, C]))]
        items_0f = [(w0["router"][:, :], a['L0_ffn_router']),
                    (w0["gate"][:, :].rearrange("h (e d) -> h e d", d=D0), a['L0_ffn_experts_gate'].rearrange("e h d -> h e d")),
                    (w0["up"][:, :].rearrange("h (e d) -> h e d", d=D0), a['L0_ffn_experts_up'].rearrange("e h d -> h e d")),
                    (w0["down"][:, :, :], a['L0_ffn_experts_down'].rearrange("(q e) d h -> (e d) q h", e=2)),
                    (w0["shared_gate"][:, :], a['L0_ffn_shared_gate']), (w0["shared_up"][:, :], a['L0_ffn_shared_up']),
                    (w0["shared_down"][:, :], a['L0_ffn_shared_down'])]
        vectors = dict(g1='ln1_g', b1='ln1_b', g2='ln2_g', b2='ln2_b', decay='time_decay', first='time_first')
        mixes = dict(mix_k='att_mix_k', mix_v='att_mix_v', mix_r='att_mix_r', ffn_mix_k='ffn_mix_k', ffn_mix_r='ffn_mix_r')
        matrices = dict(wk='Wk', wv='Wv', wr='Wr', wo='Wo', wr_ffn='Wr_ffn', wk_ffn='Wk_ffn')
        items_1a = [(w1[n][:, :], column(a['L1_attn_' + v])) for n, v in vectors.items()]
        items_1a += [(w1[n][:, :], a['L1_attn_' + v].rearrange("a b c -> c (a b)")) for n, v in mixes.items()]
        items_1a += [(w1[n][:, :], a['L1_attn_' + v]) for n, v in matrices.items()]
        items_1a += [(w1["wv_ffn"][:, :, :], a['L1_attn_Wv_ffn'].rearrange("(f p) c -> p f c", p=P))]
        items_1f = [(w2["router"][:, :], a['L1_ffn_router_W']),
                    (w2["b_router"][:, :], row(a['L1_ffn_router_b']).to_broadcast([P, E1])),
                    (w2["w1"][:, 1:, :], a['L1_ffn_eW1'].rearrange("e d h -> d e h")),
                    (w2["w1"][:, 0, :], a['L1_ffn_sW1']),
                    (w2["w2"][:, 1:, :], a['L1_ffn_eW2'].rearrange("e h d -> h e d")),
                    (w2["w2"][:, 0, :], a['L1_ffn_sW2']),
                    (w2["b1"][:, 1:], a['L1_ffn_eb1']), (w2["b1"][:, 0:1], column(a['L1_ffn_sb1'])),
                    (w2["b2_rows"][96:97, :], row(a['L1_ffn_sb2']))]
        items_1f += [(w2["b2_rows"][i * E1:(i + 1) * E1, :], a['L1_ffn_eb2']) for i in range(3)]

        def fill_constants(pool):
            pool.memset(minus_half[:, :], -0.5).then_inc(constants, 1)
            pool.memset(ident[:, :], 0.0).then_inc(constants, 1)
            pool.memset(ident_bf[:, :], 0.0).then_inc(constants, 1)
            pool.memset(w2["b2_rows"][:, :], 0.0).then_inc(constants, 1)
            pool.wait_ge(constants, 4)
            for m in (ident, ident_bf):
                pool.affine_select(out=m[:, :], in_=m[:, :], compare_op=ALU.not_equal, fill=1.0,
                                   base=0, pattern=[[-1, P]], channel_multiplier=1).then_inc(constants, 1)

        def load_first(queue):
            queue.dma_start(x[:, 0:TILES, :], x_view[:, 0:TILES, :]).then_inc(x_first, 16)
            load(queue, items_0a, weights_0a)
            queue.dma_start(x[:, TILES:, :], x_view[:, TILES:, :]).then_inc(x_loaded, 16)

        def load_next(queue):
            load(queue, items_0f, weights_0f)

        def load_last(queue):
            load(queue, items_1a, weights_1a)
            load(queue, items_1f, weights_1f)

        banks = [ctx.enter_context(nc.psum_tensor(f"bank{i}", [P, TOK], FP32)) for i in range(8)]
        attention_layer(nc, banks, x, x_first, x_loaded, ident, ident_bf, minus_half, w_qkv, w_proj, b_proj, weights_0a,
                        16 * len(items_0a), constants, 6, fill_constants, load_first, load_next, load_last)
        mix_shares = {n: [sb(f"share{i}_{n}", [C, C]) for i in range(2)] for n, _ in MIXED}
        mix_shares["rest"] = sb("mix_rest", [C, len(MIXED)])
        shares_done = sem("shares_done")

        def prepare_rwkv(dve):
            split_mixes(dve, w1, mix_shares, weights_1a, 16 * len(items_1a), shares_done)

        weights2, high2, low2 = ({"w1": sb_("w1", [C, E1 + 1, P])} for sb_ in (
            lambda n, s: w2[n][:, :, :], lambda n, s: sb("high_" + n, s, FP32R)[:, :, :],
            lambda n, s: sb("low_" + n, s, FP32R)[:, :, :]))
        high2_done, low2_done = sem("high2_done"), sem("low2_done")

        def prepare_act(act):
            act.wait_ge(weights_1f, 16 * len(items_1f))
            high_bits(act, weights2, high2, high2_done)

        front = ReluFront(nc, ctx, banks[0], x, x_loaded, ident, ident_bf, minus_half, w2, weights_1f,
                          16 * len(items_1f))

        rwkv_front = RwkvFront(nc, ctx, banks[0], x, x_loaded, ident, minus_half, w1, weights_1a, 16 * len(items_1a))

        def prepare_pool(pool):
            front.fill_pool(pool)
            low_bits(pool, weights2, high2, low2, high2_done, low2_done)

        swiglu_experts_layer(nc, banks, x, x_loaded, ident, ident_bf, minus_half, w0, weights_0f, 16 * len(items_0f),
                             prepare_rwkv, prepare_act, prepare_pool, rwkv_front)
        rwkv_layer(nc, banks, x, x_loaded, ident, minus_half, w1, mix_shares, shares_done, weights_1a, 16 * len(items_1a),
                   rwkv_front, front)
        relu_experts_layer(nc, banks, x, ident, minus_half, x_loaded, front, w2, high2, low2, (high2_done, low2_done), weights_1f,
                           16 * len(items_1f))
        with nc.Block() as block:
            @block.sync
            def _(sp):
                sp.dma_start(out_view, x[:, :, :]).then_inc(x_stored, 16)
                sp.wait_ge(x_stored, 16)


def lay_out(inputs):
    HEADS, D = 16, 8
    arrays = {n: np.asarray(inputs[n]) for n in INPUTS}
    w = arrays['L0_attn_W_qkv']
    q, k = (w[:, i * C:(i + 1) * C].reshape(C, HEADS, D).transpose(0, 2, 1).reshape(C, C) for i in range(2))
    arrays['L0_attn_W_qkv'] = np.concatenate([q, k, w[:, 2 * C:]], axis=1)
    for n in ('Wk', 'Wv', 'Wr', 'Wo', 'Wk_ffn', 'Wr_ffn', 'Wv_ffn'):
        arrays['L1_attn_' + n] = arrays['L1_attn_' + n].T
    arrays['L1_ffn_eb1'] = arrays['L1_ffn_eb1'].T
    return {n: np.ascontiguousarray(v) for n, v in arrays.items()}


def kernel(**inputs):
    import concourse.bacc as bacc
    from concourse.bass_utils import run_bass_kernel_spmd

    nc = bacc.Bacc("TRN2", target_bir_lowering=False, num_devices=1)
    arrays = lay_out(inputs)
    a = {n: nc.dram_tensor("in_" + n, v.shape, mybir.dt.from_np(v.dtype), kind="ExternalInput").ap()
         for n, v in arrays.items()}
    out = nc.dram_tensor("out", (SEQS, TOK, C), FP32, kind="ExternalOutput").ap()
    sandwich_kernel(nc, a, out)
    result = run_bass_kernel_spmd(nc, [{"in_" + n: v for n, v in arrays.items()}], core_ids=[0])
    return result.results[0]["out"]
```
